# Optimizing a Trainium2 kernel written in Bass

```python
import numpy as np
import jax
import jax.numpy as jnp

def _softmax(x, axis=-1):
    return jax.nn.softmax(x, axis=axis)

def _gelu(x):
    return jax.nn.gelu(x, approximate=True)

def _silu(x):
    return jax.nn.silu(x)

def _sigmoid(x):
    return jax.nn.sigmoid(x)

def _layernorm(x, axis=-1, eps=1e-05):
    m = jnp.mean(x, axis=axis, keepdims=True)
    v = jnp.var(x, axis=axis, keepdims=True)
    return (x - m) / jnp.sqrt(v + eps)

def _scatter_add(tgt, idx, src, axis=0):
    return tgt.at[idx].add(src)

def _segment_sum(src, seg, n):
    return jax.ops.segment_sum(src, seg, n)
kernel_name = 'mk_sandwich_d2_jaxref_r4_b388b6'

def setup_inputs(seed: int=0):
    np.random.seed(seed)
    _w = jnp.asarray

    def _L0_attn_setup():
        import jax, jax.numpy as jnp
        import numpy as np
        EPS = 1e-05
        NUM_HEADS = 16

        def _linear_attention(x, Wq, Wk, Wv, Wo, bo):
            B, L, E = x.shape
            H = NUM_HEADS
            D = E // H
            q = (x @ Wq.T).reshape(B, L, H, D)
            k = (x @ Wk.T).reshape(B, L, H, D)
            v = (x @ Wv.T).reshape(B, L, H, D)
            phi_q = jax.nn.elu(q) + 1.0
            phi_k = jax.nn.elu(k) + 1.0
            pq = jnp.moveaxis(phi_q, 1, 0)
            pk = jnp.moveaxis(phi_k, 1, 0)
            vt = jnp.moveaxis(v, 1, 0)
            S0 = jnp.zeros((B, H, D, D), x.dtype)
            z0 = jnp.zeros((B, H, D), x.dtype)

            def step(carry, inp):
                S, z = carry
                pq_t, pk_t, v_t = inp
                S = S + pk_t[..., :, None] * v_t[..., None, :]
                z = z + pk_t
                num = jnp.einsum('bhd,bhde->bhe', pq_t, S)
                den = jnp.sum(pq_t * z, axis=-1, keepdims=True) + EPS
                return ((S, z), num / den)
            (_, _), out = jax.lax.scan(step, (S0, z0), (pq, pk, vt))
            out = jnp.moveaxis(out, 0, 1).reshape(B, L, E)
            return out @ Wo.T + bo
        key = jax.random.key(seed)
        ks = jax.random.split(key, 6)
        B, L, E = (4, 1024, 256)
        s = 1.0 / np.sqrt(E)
        return {'x': jax.random.normal(ks[0], (B, L, E), jnp.float32), 'Wq': jax.random.normal(ks[1], (E, E), jnp.float32) * s, 'Wk': jax.random.normal(ks[2], (E, E), jnp.float32) * s, 'Wv': jax.random.normal(ks[3], (E, E), jnp.float32) * s, 'Wo': jax.random.normal(ks[4], (E, E), jnp.float32) * s, 'bo': jnp.zeros((E,), jnp.float32)}
    _L0_attn_in = _L0_attn_setup()

    def _L0_ffn_setup():
        import jax, jax.numpy as jnp
        import numpy as np
        LORA_DIM = 16
        LORA_TOKEN_INDEX = 1
        B, S, D, H = (4, 512, 256, 1024)
        key = jax.random.key(seed)
        ks = jax.random.split(key, 6)
        x = jax.random.normal(ks[0], (B, S, D), dtype=jnp.float32)
        W1 = jax.random.normal(ks[1], (H, D), dtype=jnp.float32) * 0.02
        b1 = jnp.zeros((H,), dtype=jnp.float32)
        W2 = jax.random.normal(ks[2], (D, H), dtype=jnp.float32) * 0.02
        b2 = jnp.zeros((D,), dtype=jnp.float32)
        scale = jnp.asarray(0.001, dtype=jnp.float32)
        return {'x': x, 'W1': W1, 'b1': b1, 'W2': W2, 'b2': b2, 'scale': scale}
    _L0_ffn_in = _L0_ffn_setup()

    def _L1_attn_setup():
        import math
        import jax, jax.numpy as jnp
        import numpy as np
        from jax import lax
        D_MODEL = 256
        N_LAYERS = 2
        D_STATE = 16
        D_CONV = 4
        EXPAND = 2
        D_INNER = EXPAND * D_MODEL
        DT_RANK = math.ceil(D_MODEL / 16)
        BATCH = 2
        SEQLEN = 256
        BETA = 0.6
        ALPHA = 1.0
        EPS = 1e-05
        DT_MIN, DT_MAX, DT_FLOOR = (0.001, 0.1, 0.0001)

        def _rmsnorm(x, w):
            return x * jax.lax.rsqrt(jnp.mean(x * x, axis=-1, keepdims=True) + EPS) * w

        def _block(x, in_w, cw, cb, xp_w, dtw, dtb, a_log, dp, ow):
            B, L, _ = x.shape
            xz = jnp.einsum('bld,ed->ble', x, in_w)
            xb, z = jnp.split(xz, 2, axis=-1)
            xc = lax.conv_general_dilated(xb.transpose(0, 2, 1), cw[:, None, :], window_strides=(1,), padding=[(D_CONV - 1, 0)], dimension_numbers=('NCH', 'OIH', 'NCH'), feature_group_count=D_INNER)
            xb = jax.nn.silu((xc + cb[None, :, None]).transpose(0, 2, 1))
            dbc = jnp.einsum('ble,re->blr', xb, xp_w)
            delta = dbc[..., :DT_RANK]
            Bm = dbc[..., DT_RANK:DT_RANK + D_STATE]
            Cm = dbc[..., DT_RANK + D_STATE:]
            delta = jax.nn.softplus(jnp.einsum('blr,er->ble', delta, dtw) + dtb)
            dA = jnp.exp(delta[..., None] * -jnp.exp(a_log))
            mi = ALPHA * delta[..., None] * Bm[:, :, None, :] * xb[..., None]

            def scan_fn(carry, inp):
                h, v = carry
                dA_t, mi_t, C_t = inp
                v = BETA * v + mi_t
                h = dA_t * h + v
                y_t = jnp.einsum('ben,bn->be', h, C_t)
                return ((h, v), y_t)
            h0 = jnp.zeros((B, D_INNER, D_STATE), dtype=x.dtype)
            _, ys = lax.scan(scan_fn, (h0, h0), (dA.transpose(1, 0, 2, 3), mi.transpose(1, 0, 2, 3), Cm.transpose(1, 0, 2)))
            y = ys.transpose(1, 0, 2) + dp * xb
            y = y * jax.nn.silu(z)
            return jnp.einsum('ble,de->bld', y, ow)
        key = jax.random.key(seed)
        ks = jax.random.split(key, 10)
        std = 0.02
        nl = N_LAYERS
        x = jax.random.normal(ks[0], (BATCH, SEQLEN, D_MODEL), dtype=jnp.float32)
        in_proj_w = jax.random.normal(ks[1], (nl, 2 * D_INNER, D_MODEL), dtype=jnp.float32) * std
        conv_w = jax.random.normal(ks[2], (nl, D_INNER, D_CONV), dtype=jnp.float32) * std
        conv_b = jnp.zeros((nl, D_INNER), dtype=jnp.float32)
        x_proj_w = jax.random.normal(ks[3], (nl, DT_RANK + 2 * D_STATE, D_INNER), dtype=jnp.float32) * std
        dt_std = DT_RANK ** (-0.5)
        dt_w = jax.random.uniform(ks[4], (nl, D_INNER, DT_RANK), dtype=jnp.float32, minval=-dt_std, maxval=dt_std)
        dt = jnp.exp(jax.random.uniform(ks[5], (nl, D_INNER), dtype=jnp.float32) * (math.log(DT_MAX) - math.log(DT_MIN)) + math.log(DT_MIN))
        dt = jnp.clip(dt, DT_FLOOR, None)
        dt_b = dt + jnp.log(-jnp.expm1(-dt))
        A_log = jnp.broadcast_to(jnp.log(jnp.arange(1, D_STATE + 1, dtype=jnp.float32)), (nl, D_INNER, D_STATE)).copy()
        Dp = jnp.ones((nl, D_INNER), dtype=jnp.float32)
        out_w = jax.random.normal(ks[6], (nl, D_MODEL, D_INNER), dtype=jnp.float32) * std
        norm_w = jnp.ones((nl, D_MODEL), dtype=jnp.float32)
        return {'x': x, 'norm_w': norm_w, 'in_proj_w': in_proj_w, 'conv_w': conv_w, 'conv_b': conv_b, 'x_proj_w': x_proj_w, 'dt_w': dt_w, 'dt_b': dt_b, 'A_log': A_log, 'Dp': Dp, 'out_w': out_w}
    _L1_attn_in = _L1_attn_setup()

    def _L1_ffn_setup():
        import jax, jax.numpy as jnp
        import numpy as np
        N_EMBD = 256
        N_EXPERTS = 8
        TOP_K = 2
        B, T = (4, 512)
        key = jax.random.key(seed)
        ks = jax.random.split(key, 8)
        C, E, H = (N_EMBD, N_EXPERTS, 4 * N_EMBD)
        s_in = 1.0 / np.sqrt(C)
        s_hid = 1.0 / np.sqrt(H)
        x = jax.random.normal(ks[0], (B, T, C), dtype=jnp.float32)
        W1 = jax.random.uniform(ks[1], (E, C, H), minval=-s_in, maxval=s_in, dtype=jnp.float32)
        b1 = jax.random.uniform(ks[2], (E, H), minval=-s_in, maxval=s_in, dtype=jnp.float32)
        W2 = jax.random.uniform(ks[3], (E, H, C), minval=-s_hid, maxval=s_hid, dtype=jnp.float32)
        b2 = jax.random.uniform(ks[4], (E, C), minval=-s_hid, maxval=s_hid, dtype=jnp.float32)
        Wg = jax.random.uniform(ks[5], (C, E), minval=-s_in, maxval=s_in, dtype=jnp.float32)
        bg = jax.random.uniform(ks[6], (E,), minval=-s_in, maxval=s_in, dtype=jnp.float32)
        return {'x': x, 'W1': W1, 'b1': b1, 'W2': W2, 'b2': b2, 'Wg': Wg, 'bg': bg}
    _L1_ffn_in = _L1_ffn_setup()
    _d = {'L0_attn_x': _L0_attn_in['x'], 'L0_attn_Wq': _L0_attn_in['Wq'], 'L0_attn_Wk': _L0_attn_in['Wk'], 'L0_attn_Wv': _L0_attn_in['Wv'], 'L0_attn_Wo': _L0_attn_in['Wo'], 'L0_attn_bo': _L0_attn_in['bo'], 'L0_ffn_W1': _L0_ffn_in['W1'], 'L0_ffn_b1': _L0_ffn_in['b1'], 'L0_ffn_W2': _L0_ffn_in['W2'], 'L0_ffn_b2': _L0_ffn_in['b2'], 'L0_ffn_scale': _L0_ffn_in['scale'], 'L1_attn_norm_w': _L1_attn_in['norm_w'], 'L1_attn_in_proj_w': _L1_attn_in['in_proj_w'], 'L1_attn_conv_w': _L1_attn_in['conv_w'], 'L1_attn_conv_b': _L1_attn_in['conv_b'], 'L1_attn_x_proj_w': _L1_attn_in['x_proj_w'], 'L1_attn_dt_w': _L1_attn_in['dt_w'], 'L1_attn_dt_b': _L1_attn_in['dt_b'], 'L1_attn_A_log': _L1_attn_in['A_log'], 'L1_attn_Dp': _L1_attn_in['Dp'], 'L1_attn_out_w': _L1_attn_in['out_w'], 'L1_ffn_W1': _L1_ffn_in['W1'], 'L1_ffn_b1': _L1_ffn_in['b1'], 'L1_ffn_W2': _L1_ffn_in['W2'], 'L1_ffn_b2': _L1_ffn_in['b2'], 'L1_ffn_Wg': _L1_ffn_in['Wg'], 'L1_ffn_bg': _L1_ffn_in['bg']}
    _x0 = _d['L0_attn_x']
    _d['L0_attn_x'] = jax.random.normal(jax.random.fold_in(jax.random.key(seed), 1), (1, 4096, 256), dtype=_x0.dtype)
    del _x0
    return _d

def reference(L0_attn_x, L0_attn_Wq, L0_attn_Wk, L0_attn_Wv, L0_attn_Wo, L0_attn_bo, L0_ffn_W1, L0_ffn_b1, L0_ffn_W2, L0_ffn_b2, L0_ffn_scale, L1_attn_norm_w, L1_attn_in_proj_w, L1_attn_conv_w, L1_attn_conv_b, L1_attn_x_proj_w, L1_attn_dt_w, L1_attn_dt_b, L1_attn_A_log, L1_attn_Dp, L1_attn_out_w, L1_ffn_W1, L1_ffn_b1, L1_ffn_W2, L1_ffn_b2, L1_ffn_Wg, L1_ffn_bg):

    def _L0_attn_ref(x, Wq, Wk, Wv, Wo, bo):
        import jax, jax.numpy as jnp
        import numpy as np
        EPS = 1e-05
        NUM_HEADS = 16

        def _linear_attention(x, Wq, Wk, Wv, Wo, bo):
            B, L, E = x.shape
            H = NUM_HEADS
            D = E // H
            q = (x @ Wq.T).reshape(B, L, H, D)
            k = (x @ Wk.T).reshape(B, L, H, D)
            v = (x @ Wv.T).reshape(B, L, H, D)
            phi_q = jax.nn.elu(q) + 1.0
            phi_k = jax.nn.elu(k) + 1.0
            pq = jnp.moveaxis(phi_q, 1, 0)
            pk = jnp.moveaxis(phi_k, 1, 0)
            vt = jnp.moveaxis(v, 1, 0)
            S0 = jnp.zeros((B, H, D, D), x.dtype)
            z0 = jnp.zeros((B, H, D), x.dtype)

            def step(carry, inp):
                S, z = carry
                pq_t, pk_t, v_t = inp
                S = S + pk_t[..., :, None] * v_t[..., None, :]
                z = z + pk_t
                num = jnp.einsum('bhd,bhde->bhe', pq_t, S)
                den = jnp.sum(pq_t * z, axis=-1, keepdims=True) + EPS
                return ((S, z), num / den)
            (_, _), out = jax.lax.scan(step, (S0, z0), (pq, pk, vt))
            out = jnp.moveaxis(out, 0, 1).reshape(B, L, E)
            return out @ Wo.T + bo
        return _linear_attention(x, Wq, Wk, Wv, Wo, bo)

    def _L0_ffn_ref(x, W1, b1, W2, b2, scale):
        import jax, jax.numpy as jnp
        import numpy as np
        LORA_DIM = 16
        LORA_TOKEN_INDEX = 1
        B, S, D, H = (4, 512, 256, 1024)
        Bx, Sx, Dx = x.shape
        Hx = W1.shape[0]
        lt = jax.lax.dynamic_slice_in_dim(x, LORA_TOKEN_INDEX, LORA_DIM, axis=1)
        even = lt[:, ::2, :]
        odd = lt[:, 1::2, :]
        m1 = (even[:, :4, :, None] * odd[:, :4, None, :]).reshape(Bx, Hx, Dx)
        m2 = (even[:, 4:, :, None] * odd[:, 4:, None, :]).reshape(Bx, Dx, Hx)
        h = jnp.einsum('bsd,hd->bsh', x, W1) + scale * jnp.einsum('bsd,bhd->bsh', x, m1) + b1
        h = jax.nn.gelu(h, approximate=False)
        out = jnp.einsum('bsh,oh->bso', h, W2) + scale * jnp.einsum('bsh,boh->bso', h, m2) + b2
        return out

    def _L1_attn_ref(x, norm_w, in_proj_w, conv_w, conv_b, x_proj_w, dt_w, dt_b, A_log, Dp, out_w):
        import math
        import jax, jax.numpy as jnp
        import numpy as np
        from jax import lax
        D_MODEL = 256
        N_LAYERS = 2
        D_STATE = 16
        D_CONV = 4
        EXPAND = 2
        D_INNER = EXPAND * D_MODEL
        DT_RANK = math.ceil(D_MODEL / 16)
        BATCH = 2
        SEQLEN = 256
        BETA = 0.6
        ALPHA = 1.0
        EPS = 1e-05
        DT_MIN, DT_MAX, DT_FLOOR = (0.001, 0.1, 0.0001)

        def _rmsnorm(x, w):
            return x * jax.lax.rsqrt(jnp.mean(x * x, axis=-1, keepdims=True) + EPS) * w

        def _block(x, in_w, cw, cb, xp_w, dtw, dtb, a_log, dp, ow):
            B, L, _ = x.shape
            xz = jnp.einsum('bld,ed->ble', x, in_w)
            xb, z = jnp.split(xz, 2, axis=-1)
            xc = lax.conv_general_dilated(xb.transpose(0, 2, 1), cw[:, None, :], window_strides=(1,), padding=[(D_CONV - 1, 0)], dimension_numbers=('NCH', 'OIH', 'NCH'), feature_group_count=D_INNER)
            xb = jax.nn.silu((xc + cb[None, :, None]).transpose(0, 2, 1))
            dbc = jnp.einsum('ble,re->blr', xb, xp_w)
            delta = dbc[..., :DT_RANK]
            Bm = dbc[..., DT_RANK:DT_RANK + D_STATE]
            Cm = dbc[..., DT_RANK + D_STATE:]
            delta = jax.nn.softplus(jnp.einsum('blr,er->ble', delta, dtw) + dtb)
            dA = jnp.exp(delta[..., None] * -jnp.exp(a_log))
            mi = ALPHA * delta[..., None] * Bm[:, :, None, :] * xb[..., None]

            def scan_fn(carry, inp):
                h, v = carry
                dA_t, mi_t, C_t = inp
                v = BETA * v + mi_t
                h = dA_t * h + v
                y_t = jnp.einsum('ben,bn->be', h, C_t)
                return ((h, v), y_t)
            h0 = jnp.zeros((B, D_INNER, D_STATE), dtype=x.dtype)
            _, ys = lax.scan(scan_fn, (h0, h0), (dA.transpose(1, 0, 2, 3), mi.transpose(1, 0, 2, 3), Cm.transpose(1, 0, 2)))
            y = ys.transpose(1, 0, 2) + dp * xb
            y = y * jax.nn.silu(z)
            return jnp.einsum('ble,de->bld', y, ow)
        for i in range(N_LAYERS):
            x = x + _block(_rmsnorm(x, norm_w[i]), in_proj_w[i], conv_w[i], conv_b[i], x_proj_w[i], dt_w[i], dt_b[i], A_log[i], Dp[i], out_w[i])
        return x

    def _L1_ffn_ref(x, W1, b1, W2, b2, Wg, bg):
        import jax, jax.numpy as jnp
        import numpy as np
        N_EMBD = 256
        N_EXPERTS = 8
        TOP_K = 2
        B, T = (4, 512)
        gate_scores = jax.nn.softmax(jnp.einsum('btc,ce->bte', x, Wg) + bg, axis=-1)
        h = jax.nn.relu(jnp.einsum('btc,ech->bteh', x, W1) + b1)
        expert_out = jnp.einsum('bteh,ehc->btec', h, W2) + b2
        topk_scores, topk_idx = jax.lax.top_k(gate_scores, TOP_K)
        top_probs = jax.nn.softmax(topk_scores, axis=-1)
        sel = jnp.take_along_axis(expert_out, topk_idx[..., None], axis=2)
        out = jnp.sum(sel * top_probs[..., None], axis=2)
        return out
    x = L0_attn_x
    x = x + _layernorm(_L0_attn_ref(_layernorm(x, axis=-1), L0_attn_Wq, L0_attn_Wk, L0_attn_Wv, L0_attn_Wo, L0_attn_bo), axis=-1)
    x = x + _layernorm(_L0_ffn_ref(_layernorm(x, axis=-1), L0_ffn_W1, L0_ffn_b1, L0_ffn_W2, L0_ffn_b2, L0_ffn_scale), axis=-1)
    x = x + _layernorm(_L1_attn_ref(_layernorm(x, axis=-1), L1_attn_norm_w, L1_attn_in_proj_w, L1_attn_conv_w, L1_attn_conv_b, L1_attn_x_proj_w, L1_attn_dt_w, L1_attn_dt_b, L1_attn_A_log, L1_attn_Dp, L1_attn_out_w), axis=-1)
    x = x + _layernorm(_L1_ffn_ref(_layernorm(x, axis=-1), L1_ffn_W1, L1_ffn_b1, L1_ffn_W2, L1_ffn_b2, L1_ffn_Wg, L1_ffn_bg), axis=-1)
    return x

_drawn_inputs = setup_inputs


def setup_inputs(seed=0):
    import zlib

    import numpy as np

    out = dict(_drawn_inputs(seed))
    spreads = {'L0_attn_bo': (0.0, 0.1),
     'L0_ffn_b1': (0.0, 0.1),
     'L0_ffn_b2': (0.0, 0.1),
     'L1_attn_norm_w': (1.0, 0.6),
     'L1_attn_conv_b': (0.0, 0.595),
     'L1_attn_Dp': (1.0, 0.6)}
    factors = {'L1_attn_in_proj_w': 4.385,
     'L1_attn_conv_w': 8.0,
     'L1_attn_x_proj_w': 8.0,
     'L1_attn_dt_w': 8.0,
     'L1_attn_dt_b': 8.0,
     'L1_attn_A_log': 8.0,
     'L1_attn_out_w': 4.676}
    for name, (base, spread) in spreads.items():
        noise = np.random.default_rng([zlib.crc32(name.encode()), seed]).standard_normal(out[name].shape)
        drawn = base * np.exp(spread * noise) if base else spread * noise
        out[name] = jnp.asarray(drawn.astype(out[name].dtype))
    for name, factor in factors.items():
        out[name] = (out[name] * factor).astype(out[name].dtype)
    return out
```

```python
from contextlib import ExitStack

import concourse.bass as bass
from concourse import mybir

F32 = mybir.dt.float32
I32 = mybir.dt.int32
ALU = mybir.AluOpType
ACT = mybir.ActivationFunctionType
AX = mybir.AxisListType

P = 128
N = 4096
D = 256
KD = D // P
CH = 512
TPC = CH // P
NCH = N // CH
NT = N // P
EPS = 1e-5
HEADS = 16
DH = D // HEADS
VE = DH + 1
HID = 1024
KH = HID // P
LAYERS = 2
DI = 512
KI = DI // P
NS = 16
RANK = 16
TAPS = 4
SUB = 64
NSUB = CH // SUB
KV = SUB + NS
SMALL = 2.0 ** -6
NE = 8


class Net:

    def __init__(self, nc, ctx, dram, out):
        self.nc, self.ctx, self.dram, self.out = nc, ctx, dram, out
        self.x = self.sb(ctx, "x_res", [P, NT, D])
        self.ident = self.sb(ctx, "ident", [P, P])
        self.half = self.sb(ctx, "minus_half", [P, TPC])
        self.var = self.sb(ctx, "var_eps", [P, TPC])
        self.carrier = ctx.enter_context(nc.semaphore("carrier"))
        self.own_pool = ctx.enter_context(nc.semaphore("own_pool"))

    def sb(self, ctx, name, shape, dt=F32):
        return ctx.enter_context(self.nc.sbuf_tensor(name, shape, dt))

    def banks(self, ctx, name):
        return [ctx.enter_context(self.nc.psum_tensor(f"{name}{i}", [P, 512], F32)) for i in range(8)]

    def own(self, name):
        self.sems.append(self.phase_ctx.enter_context(self.nc.semaphore(name)))
        return self.sems[-1]

    def sem(self, name):
        self.counts.append(self.own(name))
        return self.counts[-1]

    def start(self):
        with self.nc.Block() as block:
            @block.sync
            def _(sp):
                for count in self.counts:
                    sp.sem_inc(count, 1)

    def run(self, phase):
        with ExitStack() as self.phase_ctx:
            self.sems, self.counts = [], []
            phase(self)
            with self.nc.Block() as block:
                @block.sync
                def _(sp):
                    for used in self.sems:
                        sp.sem_clear(used)


def inverse_root(net, pool, out, variance):
    w = out.shape[-1]
    pool.sem_inc(net.carrier, 1)
    pool.sem_clear(net.own_pool)
    net.nc.gpsimd.tensor_scalar(net.var[:, 0:w], variance, EPS, None, ALU.add).then_inc(net.own_pool, 1)
    pool.wait_ge(net.own_pool, 1)
    return net.nc.gpsimd.tensor_tensor(out, net.var[:, 0:w], net.half[:, 0:w], ALU.pow)


def layer_norm_stats(nc, dve, tiles, st, mv, own, n):
    for j, t in enumerate(tiles):
        last = nc.vector.bn_stats(st[:, j, :], t)
    last.then_inc(own, 1)
    dve.wait_ge(own, n + 1)
    for j in range(len(tiles)):
        last = nc.vector.bn_aggr(mv[:, j, :], st[:, j, :])
    return last


def attention_phase(net):
    nc, dram, x = net.nc, net.dram, net.x
    with ExitStack() as ctx:
        wqkv = net.sb(ctx, "wqkv", [P, KD, 3 * D])
        wo = net.sb(ctx, "wo", [P, KD, D])
        bo = net.sb(ctx, "bo", [P, D])
        causal = net.sb(ctx, "causal", [P, P])
        head_rows = net.sb(ctx, "head_rows", [P, HEADS // KD])
        st = net.sb(ctx, "a_st", [P, TPC, 6])
        mv = net.sb(ctx, "a_mv", [P, TPC, 2])
        rstd = net.sb(ctx, "a_rstd", [P, TPC])
        xn = net.sb(ctx, "a_xn", [P, TPC, D])
        xT = net.sb(ctx, "a_xT", [P, KD, CH])
        negs = net.sb(ctx, "a_negs", [P, 2, CH])
        exps = net.sb(ctx, "a_exps", [P, 2, CH])
        phi = net.sb(ctx, "a_phi", [P, 2 * KD, CH])
        qh = net.sb(ctx, "a_qh", [P, HEADS, CH])
        kt = net.sb(ctx, "a_kt", [P, D])
        vt = net.sb(ctx, "a_vt", [P, HEADS, VE])
        probs = net.sb(ctx, "a_probs", [P, HEADS, P])
        state = net.sb(ctx, "a_state", [P, HEADS, VE])
        den = net.sb(ctx, "a_den", [P, HEADS])
        rden = net.sb(ctx, "a_rden", [P, HEADS])
        att = net.sb(ctx, "a_att", [P, D])
        attT = net.sb(ctx, "a_attT", [P, KD, P])
        z = net.sb(ctx, "a_z", [P, TPC, D])
        zn = net.sb(ctx, "a_zn", [P, TPC, D])
        B = net.banks(ctx, "a_bank")
        HG = HEADS // 4

        loaded = net.own("a_loaded")
        ones_set = net.sem("a_ones_set")
        own_dve, own_act = net.own("a_own_dve"), net.own("a_own_act")
        x_stats, x_rstd, xn_done = net.sem("a_x_stats"), net.sem("a_x_rstd"), net.sem("a_xn_done")
        xT_psum, xT_done = net.sem("a_xT_psum"), net.sem("a_xT_done")
        qk_psum, qk_exp, phi_done = net.sem("a_qk_psum"), net.sem("a_qk_exp"), net.sem("a_phi_done")
        qh_dve, qh_pool = net.sem("a_qh_dve"), net.sem("a_qh_pool")
        kv_psum, v_done, kt_exp, kt_done = (net.sem("a_kv_psum"), net.sem("a_v_done"),
                                            net.sem("a_kt_exp"), net.sem("a_kt_done"))
        s_psum, probs_done = net.sem("a_s_psum"), net.sem("a_probs_done")
        o_psum, u_psum, state_done = net.sem("a_o_psum"), net.sem("a_u_psum"), net.sem("a_state_done")
        att_done, attT_psum, attT_done = net.sem("a_att_done"), net.sem("a_attT_psum"), net.sem("a_attT_done")
        z_psum, z_stats, z_rstd = net.sem("a_z_psum"), net.sem("a_z_stats"), net.sem("a_z_rstd")

        net.start()
        with nc.Block() as block:
            @block.sync
            def _(sp):
                sp.dma_start(wqkv[:], dram["wqkv"]).then_inc(loaded, 16)
                sp.dma_start(wo[:], dram["wo"]).then_inc(loaded, 16)
                sp.dma_start(bo[:], dram["bo"].partition_broadcast(P)).then_inc(loaded, 16)
                sp.dma_start(causal[:], dram["causal"]).then_inc(loaded, 16)
                sp.dma_start(head_rows[:], dram["head_rows"]).then_inc(loaded, 16)
            LOADS = 5 * 16

            @block.gpsimd
            def _(pool):
                pool.wait_ge(loaded, LOADS)
                with pool.Fori(0, NCH) as i:
                    pool.wait_ge(x_stats, 1 + i + 1)
                    inverse_root(net, pool, rstd[:], mv[:, :, 1]).then_inc(x_rstd, 1)
                    pool.wait_ge(phi_done, 1 + i * 4 + 2)
                    pool.sem_inc(net.carrier, 1)
                    for h in range(HEADS // 2, HEADS):
                        last = nc.gpsimd.tensor_scalar(qh[:, h, :], phi[:, 1, :],
                                                       head_rows[:, h % 8:h % 8 + 1], None, ALU.mult)
                    last.then_inc(qh_pool, 1)
                    pool.wait_ge(z_stats, 1 + i + 1)
                    inverse_root(net, pool, rstd[:], mv[:, :, 1]).then_inc(z_rstd, 1)

            @block.vector
            def _(dve):
                nc.vector.memset(state[:], 0.0)
                nc.vector.memset(vt[:], 1.0).then_inc(ones_set, 1)
                dve.wait_ge(loaded, LOADS)
                with dve.Fori(0, NCH) as i:
                    dve.sem_clear(own_dve)
                    tiles = [x[:, i * TPC + j, :] for j in range(TPC)]
                    layer_norm_stats(nc, dve, tiles, st, mv, own_dve, 0).then_inc(x_stats, 1)
                    dve.wait_ge(x_rstd, 1 + i + 1)
                    for j in range(TPC):
                        nc.vector.tensor_scalar(xn[:, j, :], tiles[j], mv[:, j, 0:1], rstd[:, j:j + 1],
                                                ALU.subtract, ALU.mult).then_inc(xn_done, 1)
                    for g in range(4):
                        dve.wait_ge(qk_exp, 1 + i * 4 + g + 1)
                        nc.vector.scalar_tensor_tensor(phi[:, g, :], B[[2, 3, 0, 1][g]][:], 0.0, exps[:, g % 2, :],
                                                       ALU.max, ALU.add).then_inc(phi_done, 1)
                    dve.wait_ge(phi_done, 1 + i * 4 + 1)
                    for h in range(HEADS // 2):
                        last = nc.vector.tensor_scalar(qh[:, h, :], phi[:, 0, :],
                                                       head_rows[:, h:h + 1], None, ALU.mult)
                    last.then_inc(qh_dve, 1)
                    own = 1
                    for j in range(TPC):
                        it = i * TPC + j
                        dve.wait_ge(kt_exp, 1 + it + 1)
                        nc.vector.scalar_tensor_tensor(kt[:], B[4][:, 0:D], 0.0, exps[:, 0, 0:D],
                                                       ALU.max, ALU.add).then_inc(kt_done, 1)
                        for g in range(HG):
                            dve.wait_ge(s_psum, 1 + it * HG + g + 1)
                            nc.vector.tensor_tensor(
                                probs[:, 4 * g:4 * g + 4, :], B[5 + g % 2][:].rearrange("p (h t) -> p h t", h=4),
                                causal[:].unsqueeze(1).broadcast_to([P, 4, P]), ALU.mult).then_inc(probs_done, 1)
                        o = B[7][:, 0:HEADS * VE].rearrange("p (h e) -> p h e", e=VE)
                        dve.wait_ge(o_psum, 1 + it + 1)
                        nc.vector.tensor_scalar(den[:], o[:, :, DH], EPS, None, ALU.add).then_inc(own_dve, 1)
                        dve.wait_ge(own_dve, own + 1)
                        nc.vector.reciprocal(rden[:], den[:]).then_inc(own_dve, 1)
                        dve.wait_ge(own_dve, own + 2)
                        own += 2
                        nc.vector.tensor_tensor(att[:].rearrange("p (h e) -> p h e", e=DH), o[:, :, 0:DH],
                                                rden[:].unsqueeze(2).broadcast_to([P, HEADS, DH]),
                                                ALU.mult).then_inc(att_done, 1)
                        dve.wait_ge(u_psum, 1 + it + 1)
                        nc.vector.tensor_tensor(state[:], state[:], B[0][:, 0:HEADS * VE].rearrange(
                            "p (h e) -> p h e", e=VE), ALU.add).then_inc(state_done, 1)
                        dve.wait_ge(z_psum, 1 + it + 1)
                        last = nc.vector.tensor_tensor(z[:, j, :], B[2][:, 0:D], bo[:], ALU.add)
                    last.then_inc(own_dve, 1)
                    own += 1
                    dve.wait_ge(own_dve, own)
                    layer_norm_stats(nc, dve, [z[:, j, :] for j in range(TPC)], st, mv, own_dve, own
                                     ).then_inc(z_stats, 1)
                    own += 1
                    dve.wait_ge(z_rstd, 1 + i + 1)
                    for j in range(TPC):
                        last = nc.vector.tensor_scalar(zn[:, j, :], z[:, j, :], mv[:, j, 0:1], rstd[:, j:j + 1],
                                                       ALU.subtract, ALU.mult)
                    last.then_inc(own_dve, 1)
                    own += 1
                    dve.wait_ge(own_dve, own)
                    xc = x[:, bass.ts(i, TPC), :]
                    nc.vector.tensor_tensor(xc, xc, zn[:], ALU.add).then_inc(own_dve, 1)
                    dve.wait_ge(own_dve, own + 1)

            @block.scalar
            def _(act):
                with act.Fori(0, NCH) as i:
                    act.sem_clear(own_act)
                    own = 0
                    act.wait_ge(xT_psum, 1 + i * TPC + TPC)
                    for k in range(KD):
                        nc.scalar.copy(xT[:, k, :], B[k][:]).then_inc(xT_done, 1)
                    for g in range(4):
                        act.wait_ge(qk_psum, 1 + i * 4 + g + 1)
                        if g >= 2:
                            act.wait_ge(phi_done, 1 + i * 4 + g - 1)
                        nc.scalar.activation(negs[:, g % 2, :], B[[2, 3, 0, 1][g]][:], ACT.Relu,
                                             scale=-1.0).then_inc(own_act, 1)
                        own += 1
                        act.wait_ge(own_act, own)
                        nc.scalar.activation(exps[:, g % 2, :], negs[:, g % 2, :], ACT.Exp,
                                             scale=-1.0).then_inc(qk_exp, 1)
                    act.wait_ge(phi_done, 1 + i * 4 + 3)
                    for j in range(TPC):
                        it = i * TPC + j
                        act.wait_ge(kv_psum, 1 + it + 1)
                        if j == 0:
                            act.wait_ge(ones_set, 1 + 1)
                        nc.scalar.copy(vt[:, :, 0:DH], B[4][:, D:2 * D].rearrange("p (h e) -> p h e", e=DH)
                                       ).then_inc(v_done, 1)
                        nc.scalar.activation(negs[:, 0, 0:D], B[4][:, 0:D], ACT.Relu, scale=-1.0
                                             ).then_inc(own_act, 1)
                        own += 1
                        act.wait_ge(own_act, own)
                        if j:
                            act.wait_ge(kt_done, 1 + it)
                        nc.scalar.activation(exps[:, 0, 0:D], negs[:, 0, 0:D], ACT.Exp, scale=-1.0
                                             ).then_inc(kt_exp, 1)
                        act.wait_ge(attT_psum, 1 + it + 1)
                        nc.scalar.copy(attT[:], B[1][:, 0:D].rearrange("p (k t) -> p k t", k=KD)
                                       ).then_inc(attT_done, 1)

            @block.tensor
            def _(pe):
                pe.wait_ge(loaded, LOADS)
                with pe.Fori(0, NCH) as i:
                    for j in range(TPC):
                        pe.wait_ge(xn_done, 1 + i * TPC + j + 1)
                        for k in range(KD):
                            last = nc.tensor.transpose(B[k][:, j * P:(j + 1) * P], xn[:, j, k * P:(k + 1) * P],
                                                       net.ident[:])
                        last.then_inc(xT_psum, 1)
                    pe.wait_ge(xT_done, 1 + i * KD + KD)
                    for g in range(4):
                        for k in range(KD):
                            last = nc.tensor.matmul(B[[2, 3, 0, 1][g]][:], wqkv[:, k, g * P:(g + 1) * P], xT[:, k, :],
                                                    start=(k == 0), stop=(k == KD - 1))
                        last.then_inc(qk_psum, 1)
                    for j in range(TPC):
                        it = i * TPC + j
                        t = slice(j * P, (j + 1) * P)
                        pe.wait_ge(state_done, 1 + it)
                        pe.wait_ge(kt_done, 1 + it)
                        for k in range(KD):
                            last = nc.tensor.matmul(B[4][:], xT[:, k, t], wqkv[:, k, D:3 * D],
                                                    start=(k == 0), stop=(k == KD - 1))
                        last.then_inc(kv_psum, 1)
                        if j == 0:
                            pe.wait_ge(qh_dve, 1 + i + 1)
                            pe.wait_ge(qh_pool, 1 + i + 1)
                            pe.wait_ge(phi_done, 1 + i * 4 + 4)
                        for g in range(HG):
                            pe.wait_ge(probs_done, 1 + (it * HG + g - 1 if g >= 2 else it * HG))
                            for h in range(4 * g, 4 * g + 4):
                                last = nc.tensor.matmul(B[5 + g % 2][:, (h % 4) * P:(h % 4 + 1) * P],
                                                        phi[:, KD + h // 8, t], qh[:, h, t], start=True, stop=True)
                            last.then_inc(s_psum, 1)
                        pe.wait_ge(probs_done, 1 + it * HG + HG)
                        pe.wait_ge(v_done, 1 + it + 1)
                        pe.wait_ge(att_done, 1 + it)
                        for h in range(HEADS):
                            o = B[7][:, h * VE:(h + 1) * VE]
                            nc.tensor.matmul(o, probs[:, h, :], vt[:, h, :], start=True, stop=False)
                            last = nc.tensor.matmul(o, qh[:, h, t], state[:, h, :], start=False, stop=True)
                        last.then_inc(o_psum, 1)
                        pe.wait_ge(kt_done, 1 + it + 1)
                        for k in range(KD):
                            w = HEADS // KD * VE
                            last = nc.tensor.matmul(B[0][:, k * w:(k + 1) * w], kt[:, k * P:(k + 1) * P],
                                                    vt[:, k * 8:(k + 1) * 8, :], start=True, stop=True)
                        last.then_inc(u_psum, 1)
                        pe.wait_ge(att_done, 1 + it + 1)
                        for k in range(KD):
                            last = nc.tensor.transpose(B[1][:, k * P:(k + 1) * P], att[:, k * P:(k + 1) * P],
                                                       net.ident[:])
                        last.then_inc(attT_psum, 1)
                        pe.wait_ge(attT_done, 1 + it + 1)
                        for k in range(KD):
                            last = nc.tensor.matmul(B[2][:, 0:D], attT[:, k, :], wo[:, k, :],
                                                    start=(k == 0), stop=(k == KD - 1))
                        last.then_inc(z_psum, 1)


def ffn_phase(net):
    nc, dram, x = net.nc, net.dram, net.x
    RANK1 = 4
    with ExitStack() as ctx:
        w1 = net.sb(ctx, "f_w1", [P, KD, HID])
        w2 = net.sb(ctx, "f_w2", [P, KH, D])
        b1 = net.sb(ctx, "f_b1", [P, KH])
        b2 = net.sb(ctx, "f_b2", [P, D])
        scale = net.sb(ctx, "f_scale", [P, 1])
        tok = net.sb(ctx, "f_tok", [1, 4 * RANK1, D])
        st = net.sb(ctx, "f_st", [P, TPC, 6])
        mv = net.sb(ctx, "f_mv", [P, TPC, 2])
        rstd = net.sb(ctx, "f_rstd", [P, TPC])
        xn = net.sb(ctx, "f_xn", [P, TPC, D])
        xT = net.sb(ctx, "f_xT", [P, KD, CH])
        h = net.sb(ctx, "f_h", [P, KH, CH])
        z = net.sb(ctx, "f_z", [P, TPC, D])
        zn = net.sb(ctx, "f_zn", [P, TPC, D])
        B = net.banks(ctx, "f_bank")
        loaded, tok_done = net.own("f_loaded"), net.own("f_tok_done")
        own_dve = net.own("f_own_dve")
        first_stats, first_rstd, first_done = (net.sem("f_first_stats"), net.sem("f_first_rstd"),
                                               net.sem("f_first_done"))
        m1_psum, m2_psum, w_done = net.sem("f_m1_psum"), net.sem("f_m2_psum"), net.sem("f_w_done")
        x_stats, x_rstd, xn_done = net.sem("f_x_stats"), net.sem("f_x_rstd"), net.sem("f_xn_done")
        xT_psum, xT_done = net.sem("f_xT_psum"), net.sem("f_xT_done")
        h_psum, h_done = net.sem("f_h_psum"), net.sem("f_h_done")
        z_psum, z_done, z_stats, z_rstd = (net.sem("f_z_psum"), net.sem("f_z_done"), net.sem("f_z_stats"),
                                           net.sem("f_z_rstd"))
        LOADS = 5 * 16

        net.start()
        with nc.Block() as block:
            @block.sync
            def _(sp):
                sp.dma_start(w1[:], dram["f_w1"]).then_inc(loaded, 16)
                sp.dma_start(w2[:], dram["f_w2"]).then_inc(loaded, 16)
                sp.dma_start(b1[:], dram["f_b1"]).then_inc(loaded, 16)
                sp.dma_start(b2[:], dram["f_b2"].partition_broadcast(P)).then_inc(loaded, 16)
                sp.dma_start(scale[:], dram["f_scale"].partition_broadcast(P)).then_inc(loaded, 16)
                sp.wait_ge(first_done, 1 + 1)
                for r in range(4 * RANK1):
                    sp.dma_start(tok[:, r, :], xn[1 + r:2 + r, 0, :]).then_inc(tok_done, 16)

            @block.gpsimd
            def _(pool):
                pool.wait_ge(first_stats, 1 + 1)
                inverse_root(net, pool, rstd[:, 0:1], mv[:, 0:1, 1]).then_inc(first_rstd, 1)
                with pool.Fori(0, NCH) as i:
                    pool.wait_ge(x_stats, 1 + i + 1)
                    inverse_root(net, pool, rstd[:], mv[:, :, 1]).then_inc(x_rstd, 1)
                    pool.wait_ge(z_stats, 1 + i + 1)
                    inverse_root(net, pool, rstd[:], mv[:, :, 1]).then_inc(z_rstd, 1)

            @block.vector
            def _(dve):
                layer_norm_stats(nc, dve, [x[:, 0, :]], st, mv, own_dve, 0).then_inc(first_stats, 1)
                dve.wait_ge(first_rstd, 1 + 1)
                nc.vector.tensor_scalar(xn[:, 0, :], x[:, 0, :], mv[:, 0, 0:1], rstd[:, 0:1],
                                        ALU.subtract, ALU.mult).then_inc(first_done, 1)
                dve.wait_ge(loaded, LOADS)
                dve.wait_ge(m1_psum, 1 + 1)
                for k in range(KD):
                    for half in range(2):
                        w = w1[:, k, half * 512:(half + 1) * 512]
                        nc.vector.scalar_tensor_tensor(w, B[2 * k + half][:], scale[:, 0:1], w, ALU.mult, ALU.add)
                dve.wait_ge(m2_psum, 1 + 1)
                for q in range(4):
                    w = w2[:, 2 * q:2 * q + 2, :]
                    last = nc.vector.scalar_tensor_tensor(w, B[4 + q][:].rearrange("p (k o) -> p k o", k=2),
                                                          scale[:, 0:1], w, ALU.mult, ALU.add)
                last.then_inc(w_done, 1)
                dve.wait_ge(tok_done, 16 * 4 * RANK1)
                with dve.Fori(0, NCH) as i:
                    dve.sem_clear(own_dve)
                    tiles = [x[:, i * TPC + j, :] for j in range(TPC)]
                    layer_norm_stats(nc, dve, tiles, st, mv, own_dve, 0).then_inc(x_stats, 1)
                    dve.wait_ge(x_rstd, 1 + i + 1)
                    for j in range(TPC):
                        nc.vector.tensor_scalar(xn[:, j, :], tiles[j], mv[:, j, 0:1], rstd[:, j:j + 1],
                                                ALU.subtract, ALU.mult).then_inc(xn_done, 1)
                    for j in range(TPC):
                        dve.wait_ge(z_psum, 1 + i * TPC + j + 1)
                        nc.vector.tensor_tensor(z[:, j, :], B[6 + j % 2][:, 0:D], b2[:], ALU.add
                                                ).then_inc(z_done, 1)
                    dve.wait_ge(z_done, 1 + i * TPC + TPC)
                    layer_norm_stats(nc, dve, [z[:, j, :] for j in range(TPC)], st, mv, own_dve, 1
                                     ).then_inc(z_stats, 1)
                    dve.wait_ge(z_rstd, 1 + i + 1)
                    for j in range(TPC):
                        last = nc.vector.tensor_scalar(zn[:, j, :], z[:, j, :], mv[:, j, 0:1], rstd[:, j:j + 1],
                                                       ALU.subtract, ALU.mult)
                    last.then_inc(own_dve, 1)
                    dve.wait_ge(own_dve, 3)
                    xc = x[:, bass.ts(i, TPC), :]
                    nc.vector.tensor_tensor(xc, xc, zn[:], ALU.add).then_inc(own_dve, 1)
                    dve.wait_ge(own_dve, 4)

            @block.scalar
            def _(act):
                act.wait_ge(loaded, LOADS)
                with act.Fori(0, NCH) as i:
                    act.wait_ge(xT_psum, 1 + i * TPC + TPC)
                    for k in range(KD):
                        nc.scalar.copy(xT[:, k, :], B[k][:]).then_inc(xT_done, 1)
                    for m in range(KH):
                        act.wait_ge(h_psum, 1 + i * KH + m + 1)
                        if m == 0:
                            act.wait_ge(z_psum, 1 + i * TPC)
                        nc.scalar.activation(h[:, m, :], B[2 + m % 4][:], ACT.Gelu, bias=b1[:, m:m + 1]
                                             ).then_inc(h_done, 1)

            @block.tensor
            def _(pe):
                pe.wait_ge(tok_done, 16 * 4 * RANK1)
                for k in range(KD):
                    for i in range(RANK1):
                        last = nc.tensor.matmul(B[2 * k + i // 2][:, (i % 2) * D:(i % 2 + 1) * D],
                                                tok[0:1, 2 * i + 1, k * P:(k + 1) * P], tok[0:1, 2 * i, :],
                                                start=True, stop=True)
                last.then_inc(m1_psum, 1)
                for m in range(KH):
                    r, half = m // 2, m % 2
                    for i in range(RANK1):
                        col = (m % 2) * D + i * (D // 4)
                        last = nc.tensor.matmul(B[4 + m // 2][:, col:col + D // 4],
                                                tok[0:1, 2 * (RANK1 + i) + 1, half * P:(half + 1) * P],
                                                tok[0:1, 2 * (RANK1 + i), r:D:4], start=True, stop=True)
                last.then_inc(m2_psum, 1)
                pe.wait_ge(w_done, 1 + 1)
                with pe.Fori(0, NCH) as i:
                    for j in range(TPC):
                        pe.wait_ge(xn_done, 1 + i * TPC + j + 1)
                        for k in range(KD):
                            last = nc.tensor.transpose(B[k][:, j * P:(j + 1) * P], xn[:, j, k * P:(k + 1) * P],
                                                       net.ident[:])
                        last.then_inc(xT_psum, 1)
                    pe.wait_ge(xT_done, 1 + i * KD + KD)
                    for m in range(KH):
                        pe.wait_ge(h_done, 1 + (i * KH + m - 3 if m >= 4 else i * KH))
                        for k in range(KD):
                            last = nc.tensor.matmul(B[2 + m % 4][:], w1[:, k, m * P:(m + 1) * P], xT[:, k, :],
                                                    start=(k == 0), stop=(k == KD - 1))
                        last.then_inc(h_psum, 1)
                    pe.wait_ge(h_done, 1 + i * KH + KH)
                    for j in range(TPC):
                        pe.wait_ge(z_done, 1 + (i * TPC + j - 1 if j >= 2 else i * TPC))
                        for m in range(KH):
                            last = nc.tensor.matmul(B[6 + j % 2][:, 0:D], h[:, m, j * P:(j + 1) * P], w2[:, m, :],
                                                    start=(m == 0), stop=(m == KH - 1))
                        last.then_inc(z_psum, 1)


def mamba_phase(net, layer, xm):
    nc, dram, x = net.nc, net.dram, net.x
    first, last_layer = layer == 0, layer == LAYERS - 1
    rounds = 2 if first else 1
    nm = lambda s: f"m{layer}_{s}"
    with ExitStack() as ctx:
        sb = lambda s, shape, dt=F32: net.sb(ctx, nm(s), shape, dt)
        norm, w_in, conv, conv_b = sb("norm", [P, KD]), sb("in", [P, KD, 2 * DI]), sb("conv", [P, KI, TAPS]), sb("cb", [P, KI])
        w_xp, w_dt, dt_b = sb("xp", [P, KI, RANK + 2 * NS]), sb("dt", [RANK, DI]), sb("dtb", [P, KI])
        rate, skip, w_out = sb("rate", [P, KI, NS]), sb("skip", [P, KI]), sb("out", [P, KI, D])
        decay = sb("decay", [SUB, SUB])
        st, mv, rstd = sb("st", [P, TPC, 6]), sb("mv", [P, TPC, 2]), sb("rstd", [P, TPC])
        msq = sb("msq", [P, TPC])
        xb, zs = sb("xb", [P, KI, CH]), sb("zs", [P, KI, CH])
        xpre = sb("xpre", [P, KI, TAPS - 1 + CH])
        delta = xpre[:, :, TAPS - 1:]
        halo = sb("halo", [P, KI, TAPS - 1])
        t0, t1, t2 = sb("t0", [P, KI, CH]), sb("t1", [P, KI, CH]), sb("t2", [P, KI, CH])
        mask = sb("mask", [P, KI, CH], mybir.dt.uint8)
        low = sb("low", [RANK, CH])
        Bs, Cs = sb("Bs", [SUB, NSUB, NS]), sb("Cs", [P, TPC, NS])
        M = sb("M", [KV, NSUB, NS, SUB])
        U = sb("U", [KV, NSUB, DI])
        vcarry = sb("vcarry", [KV, DI])
        dA = sb("dA", [P, KI, CH])
        h = sb("h", [P, 2, KI, CH])
        hlast = sb("hlast", [P, NS, KI])
        xr = t2[:, 0:2, :].rearrange("p a (b d) -> p (a b) d", d=D)
        xT = t2[:, 2:4, :]
        decay_n = decay[:].unsqueeze(1).broadcast_to([SUB, NS, SUB])
        B = net.banks(ctx, nm("bank"))
        names = ("loaded own_dve own_act own_pool setup x_stats x_rstd xr_done xT_psum xT_done in_psum in_read "
                 "pre_done conv_done xb_done dt_psum dt_read low_psum low_done bc_psum bc_done "
                 "relu_done exp_done ln_done series_done u_done uT_psum uT_done Mv_done Mp_done halo_done halo_saved "
                 "carry_psum carry_done v_psum da_done scan_done hlast_done ht_psum prod_done "
                 "y_dve y_pool yT_psum gated_done out_psum xm_done z_stats z_rstd rate_done").split()
        s = {n: (net.own if n == "loaded" or "own" in n else net.sem)(nm(n)) for n in names}
        LOADS = 11 * 16 + 16 * NSUB

        net.start()
        with nc.Block() as block:
            @block.sync
            def _(sp):
                for t, key in ((norm, "norm"), (w_in, "in"), (conv, "conv"), (conv_b, "conv_b"), (w_xp, "xp"),
                               (w_dt, "dt"), (dt_b, "dt_b"), (rate, "alog"), (skip, "skip"), (w_out, "out")):
                    sp.dma_start(t[:], dram[f"m{layer}_{key}"]).then_inc(s["loaded"], 16)
                sp.dma_start(decay[:], dram["decay"][0:SUB, 0]).then_inc(s["loaded"], 16)
                for j in range(NSUB):
                    sp.dma_start(M[SUB:KV, j], dram["decay"][SUB:KV]).then_inc(s["loaded"], 16)

            @block.gpsimd
            def _(pool):
                nc.gpsimd.memset(halo[:], 0.0)
                nc.gpsimd.memset(hlast[:], 0.0)
                nc.gpsimd.memset(vcarry[:], 0.0).then_inc(s["setup"], 1)
                pool.wait_ge(s["setup"], 1 + 1)
                pool.wait_ge(s["loaded"], LOADS)
                with pool.Fori(0, NCH) as c:
                    pool.sem_clear(s["own_pool"])
                    pool.wait_ge(s["x_stats"], 1 + c * rounds + 1)
                    if first:
                        inverse_root(net, pool, rstd[:], mv[:, :, 1]).then_inc(s["x_rstd"], 1)
                        pool.wait_ge(s["x_stats"], 1 + c * 2 + 2)
                    inverse_root(net, pool, rstd[:], msq[:]).then_inc(s["x_rstd"], 1)
                    pool.wait_ge(s["conv_done"], 1 + c * KI)
                    pool.sem_inc(net.carrier, 1)
                    nc.gpsimd.tensor_copy(xpre[:, :, 0:TAPS - 1], halo[:]).then_inc(s["halo_done"], 1)
                    pool.wait_ge(s["conv_done"], 1 + c * KI + KI)
                    pool.sem_inc(net.carrier, 1)
                    nc.gpsimd.tensor_copy(halo[:], xpre[:, :, CH:CH + TAPS - 1]).then_inc(s["halo_saved"], 1)
                    pool.wait_ge(s["halo_saved"], 1 + c + 1)
                    pool.wait_ge(s["exp_done"], 1 + c + 1)
                    pool.sem_inc(net.carrier, 1)
                    nc.gpsimd.tensor_scalar(mask[:], t0[:], SMALL, None, ALU.is_lt)
                    nc.gpsimd.tensor_scalar(t2[:], t0[:], -0.25, 1 / 3, ALU.mult, ALU.add).then_inc(s["own_pool"], 1)
                    pool.wait_ge(s["own_pool"], 1)
                    nc.gpsimd.tensor_tensor(t2[:], t2[:], t0[:], ALU.mult).then_inc(s["own_pool"], 1)
                    pool.wait_ge(s["own_pool"], 2)
                    nc.gpsimd.tensor_scalar(t2[:], t2[:], -0.5, None, ALU.add).then_inc(s["own_pool"], 1)
                    pool.wait_ge(s["own_pool"], 3)
                    nc.gpsimd.tensor_tensor(t2[:], t2[:], t0[:], ALU.mult).then_inc(s["own_pool"], 1)
                    pool.wait_ge(s["own_pool"], 4)
                    nc.gpsimd.tensor_scalar(t2[:], t2[:], 1.0, None, ALU.add).then_inc(s["own_pool"], 1)
                    pool.wait_ge(s["own_pool"], 5)
                    nc.gpsimd.tensor_tensor(t2[:], t2[:], t0[:], ALU.mult).then_inc(s["series_done"], 1)
                    pool.wait_ge(s["bc_done"], 1 + c * 2 + 2)
                    for j in range(NSUB // 2, NSUB):
                        last = nc.gpsimd.tensor_tensor(M[0:SUB, j], decay_n, Bs[:, j, :].unsqueeze(2).broadcast_to(
                            [SUB, NS, SUB]), ALU.mult)
                    last.then_inc(s["Mp_done"], 1)

                    def states(n, par):
                        k = c * NS + n
                        pool.wait_ge(s["scan_done"], 1 + (k + 1) * KI)
                        pool.sem_inc(net.carrier, 1)
                        nc.gpsimd.tensor_copy(hlast[:, n, :], h[:, par, :, CH - 1]).then_inc(s["hlast_done"], 1)
                        pool.wait_ge(s["y_pool"], 1 + k)
                        pool.wait_ge(s["prod_done"], 1 + (k + 1) * 2)
                        for tt in (2, 3):
                            y = t0[:, tt, :]
                            last = nc.gpsimd.tensor_tensor(y, y, t2[:, 2 * par + tt - 2, :], ALU.add)
                        last.then_inc(s["y_pool"], 1)

                    pool.wait_ge(s["ln_done"], 1 + c + 1)
                    pool.wait_ge(s["series_done"], 1 + c + 1)
                    pool.sem_inc(net.carrier, 1)
                    nc.gpsimd.memset(t0[:, 2:4, :], 0.0).then_inc(s["own_pool"], 1)
                    pool.wait_ge(s["own_pool"], 6)
                    with pool.Fori(0, NS // 2) as n2:
                        states(n2 * 2, 0)
                        states(n2 * 2 + 1, 1)
                    if last_layer:
                        pool.wait_ge(s["z_stats"], 1 + c + 1)
                        inverse_root(net, pool, rstd[:], mv[:, :, 1]).then_inc(s["z_rstd"], 1)

            @block.vector
            def _(dve):
                dve.wait_ge(s["loaded"], LOADS)
                dve.wait_ge(s["setup"], 1 + 1)
                with dve.Fori(0, NCH) as c:
                    own = [0]

                    def after(ins):
                        own[0] += 1
                        ins.then_inc(s["own_dve"], 1)
                        dve.wait_ge(s["own_dve"], own[0])

                    dve.sem_clear(s["own_dve"])
                    xtiles = [x[:, c * TPC + j, :] for j in range(TPC)]
                    mtiles = [xm[:, c * TPC + j, :] for j in range(TPC)]
                    if first:
                        layer_norm_stats(nc, dve, xtiles, st, mv, s["own_dve"], 0).then_inc(s["x_stats"], 1)
                        own[0] += 1
                        dve.wait_ge(s["x_rstd"], 1 + c * 2 + 1)
                        for j in range(TPC):
                            i = nc.vector.tensor_scalar(mtiles[j], xtiles[j], mv[:, j, 0:1], rstd[:, j:j + 1],
                                                        ALU.subtract, ALU.mult)
                        after(i)
                    after(layer_norm_stats(nc, dve, mtiles, st, mv, s["own_dve"], own[0]))
                    own[0] += 1
                    dve.wait_ge(s["own_dve"], own[0])
                    after(nc.vector.tensor_tensor(msq[:], mv[:, :, 0], mv[:, :, 0], ALU.mult))
                    nc.vector.tensor_tensor(msq[:], msq[:], mv[:, :, 1], ALU.add).then_inc(s["x_stats"], 1)
                    dve.wait_ge(s["x_rstd"], 1 + c * rounds + rounds)
                    for j in range(TPC):
                        nc.vector.tensor_scalar(xr[:, j, :], mtiles[j], rstd[:, j:j + 1], None, ALU.mult
                                                ).then_inc(s["xr_done"], 1)
                    dve.wait_ge(s["pre_done"], 1 + c * KI + KI)
                    for m in range(KI):
                        dve.wait_ge(s["halo_done"], 1 + c + 1)
                        after(nc.vector.tensor_scalar(t0[:, m, :], xpre[:, m, 0:CH], conv[:, m, 0:1], None, ALU.mult))
                        for k in range(1, TAPS):
                            i = nc.vector.scalar_tensor_tensor(t0[:, m, :], xpre[:, m, k:k + CH], conv[:, m, k:k + 1],
                                                               t0[:, m, :], ALU.mult, ALU.add)
                            if k < TAPS - 1:
                                after(i)
                        i.then_inc(s["conv_done"], 1)
                    dve.wait_ge(s["bc_done"], 1 + c * 2 + 2)
                    for j in range(NSUB // 2):
                        i = nc.vector.tensor_tensor(M[0:SUB, j], decay_n, Bs[:, j, :].unsqueeze(2).broadcast_to(
                            [SUB, NS, SUB]), ALU.mult)
                    i.then_inc(s["Mv_done"], 1)
                    dve.wait_ge(s["halo_saved"], 1 + c + 1)
                    for m in range(KI):
                        dve.wait_ge(s["dt_psum"], 1 + c * KI + m + 1)
                        dve.wait_ge(s["dt_read"], 1 + c * KI + m + 1)
                        i = nc.vector.tensor_scalar(delta[:, m, :], B[m][:], dt_b[:, m:m + 1], 0.0, ALU.add, ALU.max)
                    i.then_inc(s["relu_done"], 1)
                    dve.wait_ge(s["ln_done"], 1 + c + 1)
                    dve.wait_ge(s["series_done"], 1 + c + 1)
                    dve.sem_inc(net.carrier, 1)
                    after(nc.vector.copy_predicated(t1[:], mask[:], t2[:]))
                    after(nc.vector.tensor_tensor(delta, delta, t1[:], ALU.add))
                    nc.vector.tensor_tensor(t1[:], delta, xb[:], ALU.mult).then_inc(s["u_done"], 1)
                    after(nc.vector.memset(t0[:, 0:2, :], 0.0))

                    def scans(n, par):
                        for m in range(KI):
                            k = (c * NS + n) * KI + m
                            dve.wait_ge(s["v_psum"], 1 + k + 1)
                            dve.wait_ge(s["da_done"], 1 + k + 1)
                            nc.vector.tensor_tensor_scan(h[:, par, m, :], dA[:, m, :], B[m][:], hlast[:, n, m:m + 1],
                                                         ALU.mult, ALU.add).then_inc(s["scan_done"], 1)

                    def outputs(n):
                        for tt in (0, 1):
                            k = (c * NS + n) * TPC
                            dve.wait_ge(s["ht_psum"], 1 + k + 3 + tt)
                            dve.wait_ge(s["y_dve"], 1 + (c * NS + n) * 2)
                            y = t0[:, tt, :]
                            nc.vector.scalar_tensor_tensor(y, B[4 + tt][:], Cs[:, tt, bass.ts(n, 1)], y, ALU.mult, ALU.add
                                                           ).then_inc(s["y_dve"], 1)

                    scans(0, 0)
                    with dve.Fori(0, NS // 2 - 1) as n2:
                        n = n2 * 2
                        scans(n + 1, 1)
                        outputs(n)
                        dve.wait_ge(s["hlast_done"], 1 + c * NS + n + 1)
                        scans(n + 2, 0)
                        outputs(n + 1)
                        dve.wait_ge(s["hlast_done"], 1 + c * NS + n + 2)
                    scans(NS - 1, 1)
                    outputs(NS - 2)
                    outputs(NS - 1)
                    dve.wait_ge(s["hlast_done"], 1 + c * NS + NS)
                    for m in range(KI):
                        dve.wait_ge(s["yT_psum"], 1 + c * KI + m + 1)
                        after(nc.vector.scalar_tensor_tensor(t1[:, m, :], xb[:, m, :], skip[:, m:m + 1], B[m][:],
                                                             ALU.mult, ALU.add))
                        nc.vector.tensor_tensor(t1[:, m, :], t1[:, m, :], zs[:, m, :], ALU.mult
                                                ).then_inc(s["gated_done"], 1)
                    for j in range(TPC):
                        dve.wait_ge(s["out_psum"], 1 + c * TPC + j + 1)
                        i = nc.vector.tensor_tensor(mtiles[j], mtiles[j], B[4 + j][:, 0:D], ALU.add)
                    after(i)
                    if last_layer:
                        layer_norm_stats(nc, dve, mtiles, st, mv, s["own_dve"], own[0]).then_inc(s["z_stats"], 1)
                        own[0] += 1
                        dve.wait_ge(s["z_rstd"], 1 + c + 1)
                        for j in range(TPC):
                            i = nc.vector.tensor_scalar(xr[:, j, :], mtiles[j], mv[:, j, 0:1], rstd[:, j:j + 1],
                                                        ALU.subtract, ALU.mult)
                        after(i)
                        xc = x[:, bass.ts(c, TPC), :]
                        after(nc.vector.tensor_tensor(xc, xc, xr, ALU.add))

            @block.scalar
            def _(act):
                act.wait_ge(s["loaded"], LOADS)
                nc.scalar.activation(rate[:], rate[:], ACT.Exp).then_inc(s["rate_done"], 1)
                act.wait_ge(s["rate_done"], 1 + 1)
                nc.scalar.mul(rate[:], rate[:], -1.0).then_inc(s["rate_done"], 1)
                act.wait_ge(s["rate_done"], 1 + 2)
                act.wait_ge(s["setup"], 1 + 1)
                with act.Fori(0, NCH) as c:
                    act.sem_clear(s["own_act"])
                    act.wait_ge(s["xT_psum"], 1 + c * TPC + TPC)
                    for k in range(KD):
                        nc.scalar.activation(xT[:, k, :], B[k][:], ACT.Copy, scale=norm[:, k:k + 1]
                                             ).then_inc(s["xT_done"], 1)
                    act.wait_ge(s["halo_done"], 1 + c + 1)
                    for m in range(2 * KI):
                        act.wait_ge(s["in_psum"], 1 + c * 2 * KI + m + 1)
                        if m < KI:
                            nc.scalar.copy(xpre[:, m, TAPS - 1:], B[2 + m % 4][:]).then_inc(s["pre_done"], 1)
                        else:
                            nc.scalar.activation(zs[:, m - KI, :], B[2 + m % 4][:], ACT.Silu).then_inc(s["in_read"], 1)
                    for m in range(KI):
                        act.wait_ge(s["conv_done"], 1 + c * KI + m + 1)
                        nc.scalar.activation(xb[:, m, :], t0[:, m, :], ACT.Silu, bias=conv_b[:, m:m + 1]
                                             ).then_inc(s["xb_done"], 1)
                    act.wait_ge(s["low_psum"], 1 + c + 1)
                    nc.scalar.copy(low[:], B[6][0:RANK, :]).then_inc(s["low_done"], 1)
                    act.wait_ge(s["bc_psum"], 1 + c + 1)
                    nc.scalar.copy(Bs[:], B[7][0:SUB, 0:NSUB * NS].rearrange("p (a n) -> p a n", n=NS)
                                   ).then_inc(s["bc_done"], 1)
                    nc.scalar.copy(Cs[:], B[7][:, 256:256 + TPC * NS].rearrange("p (a n) -> p a n", n=NS)
                                   ).then_inc(s["bc_done"], 1)
                    for m in range(KI):
                        act.wait_ge(s["dt_psum"], 1 + c * KI + m + 1)
                        nc.scalar.activation(t0[:, m, :], B[m][:], ACT.Abs, bias=dt_b[:, m:m + 1]
                                             ).then_inc(s["dt_read"], 1)
                    act.wait_ge(s["dt_read"], 1 + c * KI + KI)
                    nc.scalar.activation(t0[:], t0[:], ACT.Exp, scale=-1.0).then_inc(s["exp_done"], 1)
                    act.wait_ge(s["exp_done"], 1 + c + 1)
                    nc.scalar.activation(t1[:], t0[:], ACT.Ln, bias=1.0).then_inc(s["ln_done"], 1)
                    for j in range(NSUB):
                        act.wait_ge(s["uT_psum"], 1 + c * NSUB + j + 1)
                        if j == 0:
                            nc.scalar.copy(U[SUB:KV, 0, :], vcarry[SUB:KV, :])
                        nc.scalar.copy(U[0:SUB, j, :], B[j % 4][0:SUB, :]).then_inc(s["uT_done"], 1)
                    for j in range(NSUB):
                        act.wait_ge(s["carry_psum"], 1 + c * NSUB + j + 1)
                        to = U[SUB:KV, j + 1, :] if j < NSUB - 1 else vcarry[SUB:KV, :]
                        nc.scalar.copy(to, B[4][0:NS, :]).then_inc(s["carry_done"], 1)

                    def decays(n):
                        for m in range(KI):
                            if not (isinstance(n, int) and n == 0):
                                act.wait_ge(s["scan_done"], 1 + (c * NS + n - 1) * KI + m + 1)
                            act.sem_inc(net.carrier, 1)
                            nc.scalar.activation(dA[:, m, :], delta[:, m, :], ACT.Exp, scale=rate[:, m, bass.ts(n, 1)]
                                                 ).then_inc(s["da_done"], 1)

                    def products(n, par):
                        for tt in (2, 3):
                            k = (c * NS + n) * TPC
                            act.wait_ge(s["ht_psum"], 1 + k + tt - 1)
                            if tt == 2:
                                act.wait_ge(s["y_pool"], 1 + (c * NS + n - 1 if not (isinstance(n, int) and n == 0) else c * NS))
                            act.sem_inc(net.carrier, 1)
                            nc.scalar.activation(t2[:, 2 * par + tt - 2, :], B[4 + tt][:], ACT.Copy,
                                                 scale=Cs[:, tt, bass.ts(n, 1)]).then_inc(s["prod_done"], 1)

                    act.wait_ge(s["u_done"], 1 + c + 1)
                    decays(0)
                    decays(1)
                    products(0, 0)
                    with act.Fori(0, NS // 2 - 1) as n2:
                        n = n2 * 2
                        decays(n + 2)
                        products(n + 1, 1)
                        decays(n + 3)
                        products(n + 2, 0)
                    products(NS - 1, 1)

            @block.tensor
            def _(pe):
                pe.wait_ge(s["loaded"], LOADS)
                pe.wait_ge(s["setup"], 1 + 1)
                with pe.Fori(0, NCH) as c:
                    for j in range(TPC):
                        pe.wait_ge(s["xr_done"], 1 + c * TPC + j + 1)
                        for k in range(KD):
                            last = nc.tensor.transpose(B[k][:, j * P:(j + 1) * P], xr[:, j, k * P:(k + 1) * P],
                                                       net.ident[:])
                        last.then_inc(s["xT_psum"], 1)
                    pe.wait_ge(s["xT_done"], 1 + c * KD + KD)
                    for m in range(2 * KI):
                        if m >= KI:
                            pe.wait_ge(s["pre_done"], 1 + c * KI + m - KI + 1)
                        for k in range(KD):
                            last = nc.tensor.matmul(B[2 + m % 4][:], w_in[:, k, m * P:(m + 1) * P], xT[:, k, :],
                                                    start=(k == 0), stop=(k == KD - 1))
                        last.then_inc(s["in_psum"], 1)
                    pe.wait_ge(s["xb_done"], 1 + c * KI + KI)
                    for k in range(KI):
                        last = nc.tensor.matmul(B[6][0:RANK, :], w_xp[:, k, 0:RANK], xb[:, k, :],
                                                start=(k == 0), stop=(k == KI - 1))
                    last.then_inc(s["low_psum"], 1)
                    for j in range(NSUB):
                        for k in range(KI):
                            nc.tensor.matmul(B[7][0:SUB, j * NS:(j + 1) * NS], xb[:, k, j * SUB:(j + 1) * SUB],
                                             w_xp[:, k, RANK:RANK + NS], start=(k == 0), stop=(k == KI - 1))
                    for j in range(TPC):
                        for k in range(KI):
                            last = nc.tensor.matmul(B[7][:, 256 + j * NS:256 + (j + 1) * NS], xb[:, k, j * P:(j + 1) * P],
                                                    w_xp[:, k, RANK + NS:], start=(k == 0), stop=(k == KI - 1))
                    last.then_inc(s["bc_psum"], 1)
                    pe.wait_ge(s["low_done"], 1 + c + 1)
                    for m in range(KI):
                        nc.tensor.matmul(B[m][:], w_dt[:, m * P:(m + 1) * P], low[:], start=True, stop=True
                                         ).then_inc(s["dt_psum"], 1)
                    pe.wait_ge(s["u_done"], 1 + c + 1)
                    pe.sem_inc(net.carrier, 1)
                    for j in range(NSUB):
                        if j >= 4:
                            pe.wait_ge(s["uT_done"], 1 + c * NSUB + j - 3)
                            pe.sem_inc(net.carrier, 1)
                        for m in range(KI):
                            last = nc.tensor.transpose(B[j % 4][0:SUB, m * P:(m + 1) * P],
                                                       t1[:, m, j * SUB:(j + 1) * SUB], net.ident[:])
                        last.then_inc(s["uT_psum"], 1)
                    pe.wait_ge(s["Mv_done"], 1 + c + 1)
                    pe.wait_ge(s["Mp_done"], 1 + c + 1)
                    pe.wait_ge(s["uT_done"], 1 + c * NSUB + NSUB)
                    for j in range(NSUB):
                        pe.wait_ge(s["carry_done"], 1 + c * NSUB + j)
                        nc.tensor.matmul(B[4][0:NS, :], M[:, j, :, SUB - 1], U[:, j, :], start=True, stop=True
                                         ).then_inc(s["carry_psum"], 1)
                    pe.wait_ge(s["carry_done"], 1 + c * NSUB + NSUB)

                    def velocities(n):
                        for m in range(KI):
                            if not (isinstance(n, int) and n == 0):
                                pe.wait_ge(s["scan_done"], 1 + (c * NS + n - 1) * KI + m + 1)
                            for j in range(NSUB):
                                last = nc.tensor.matmul(B[m][:, j * SUB:(j + 1) * SUB], U[:, j, m * P:(m + 1) * P],
                                                        M[:, j, n, :], start=True, stop=True)
                            last.then_inc(s["v_psum"], 1)

                    def turn(n, par):
                        pe.wait_ge(s["scan_done"], 1 + (c * NS + n + 1) * KI)
                        for tt in (2, 3, 0, 1):
                            if not (isinstance(n, int) and n == 0):
                                if tt >= 2:
                                    pe.wait_ge(s["prod_done"], 1 + (c * NS + n - 1) * 2 + tt - 1)
                                else:
                                    pe.wait_ge(s["y_dve"], 1 + (c * NS + n - 1) * 2 + tt + 1)
                            for m in range(KI):
                                last = nc.tensor.transpose(B[4 + tt][:, m * P:(m + 1) * P],
                                                           h[:, par, m, tt * P:(tt + 1) * P], net.ident[:])
                            last.then_inc(s["ht_psum"], 1)

                    velocities(0)
                    velocities(1)
                    turn(0, 0)
                    with pe.Fori(0, NS // 2 - 1) as n2:
                        n = n2 * 2
                        velocities(n + 2)
                        turn(n + 1, 1)
                        velocities(n + 3)
                        turn(n + 2, 0)
                    turn(NS - 1, 1)
                    pe.wait_ge(s["y_dve"], 1 + (c * NS + NS) * 2)
                    pe.wait_ge(s["y_pool"], 1 + c * NS + NS)
                    for m in range(KI):
                        for tt in range(TPC):
                            last = nc.tensor.transpose(B[m][:, tt * P:(tt + 1) * P], t0[:, tt, m * P:(m + 1) * P],
                                                       net.ident[:])
                        last.then_inc(s["yT_psum"], 1)
                    pe.wait_ge(s["gated_done"], 1 + c * KI + KI)
                    for j in range(TPC):
                        for k in range(KI):
                            last = nc.tensor.matmul(B[4 + j][:, 0:D], t1[:, k, j * P:(j + 1) * P], w_out[:, k, :],
                                                    start=(k == 0), stop=(k == KI - 1))
                        last.then_inc(s["out_psum"], 1)


def mamba_phases(net):
    with ExitStack() as ctx:
        xm = net.sb(ctx, "xm", [P, NT, D])
        for layer in range(LAYERS):
            net.run(lambda n: mamba_phase(n, layer, xm))


def moe_phase(net):
    nc, dram, x = net.nc, net.dram, net.x
    with ExitStack() as ctx:
        sb = lambda s, shape, dt=F32: net.sb(ctx, "e_" + s, shape, dt)
        w1, w2 = sb("w1", [P, 2, KD, HID]), sb("w2", [P, 2, KH, D])
        b1, b2 = sb("b1", [P, NE, KH]), sb("b2", [NE, D])
        wg, bg, rank = sb("wg", [P, KD, NE]), sb("bg", [P, NE]), sb("rank", [P, NE])
        st, mv, rstd = sb("st", [P, TPC, 6]), sb("mv", [P, TPC, 2]), sb("rstd", [P, TPC])
        xn, xT = sb("xn", [P, TPC, D]), sb("xT", [P, KD, CH])
        xT_all = sb("xT_all", [P, KD, N])
        acc = sb("acc", [P, NT, D])
        h = sb("h", [P, KH, CH])
        gate, one1, one2, tmp = (sb(s, [P, NT, NE]) for s in ("gate", "one1", "one2", "tmp"))
        top1, top2, col = (sb(s, [P, NT]) for s in ("top1", "top2", "col"))
        wgt = sb("wgt", [P, NT, NE])
        wc, wT = sb("wc", [P, TPC, NE]), sb("wT", [NE, CH])
        B = net.banks(ctx, "e_bank")
        names = ("loaded weights0 weights1 own_dve x_stats x_rstd xn_done xT_psum xT_done g_psum g_done logits exp_in exp_out "
                 "pair_in pair_out wgt_done wc_done wT_psum wT_done b_psum b_done h_psum h_done z_psum z_done "
                 "z_stats z_rstd setup").split()
        s = {n: (net.own if n in ("loaded", "weights0", "weights1", "own_dve") else net.sem)("e_" + n) for n in names}
        LOADS = 5 * 16
        over = lambda t: t[:].unsqueeze(2).broadcast_to([P, NT, NE])

        net.start()
        with nc.Block() as block:
            @block.sync
            def _(sp):
                for t, key in ((wg, "e_wg"), (b1, "e_b1"), (b2, "e_b2")):
                    sp.dma_start(t[:], dram[key]).then_inc(s["loaded"], 16)
                sp.dma_start(bg[:], dram["e_bg"].partition_broadcast(P)).then_inc(s["loaded"], 16)
                sp.dma_start(rank[:], dram["rank"].partition_broadcast(P)).then_inc(s["loaded"], 16)
                with sp.Fori(0, NE // 2) as e2:
                    for par in range(2):
                        sp.wait_ge(s["z_psum"], 1 + e2 * 2 * NT)
                        sp.dma_start(w1[:, par], dram["e_w1"][e2 * 2 + par]).then_inc(s[f"weights{par}"], 16)
                        sp.dma_start(w2[:, par], dram["e_w2"][e2 * 2 + par]).then_inc(s[f"weights{par}"], 16)

            @block.gpsimd
            def _(pool):
                nc.gpsimd.memset(wc[:], 0.0).then_inc(s["setup"], 1)
                with pool.Fori(0, 2 * NCH) as i:
                    pool.wait_ge(s["x_stats"], 1 + i + 1)
                    inverse_root(net, pool, rstd[:], mv[:, :, 1]).then_inc(s["x_rstd"], 1)

            @block.vector
            def _(dve):
                dve.wait_ge(s["loaded"], LOADS)
                with dve.Fori(0, NCH) as c:
                    dve.sem_clear(s["own_dve"])
                    tiles = [x[:, c * TPC + j, :] for j in range(TPC)]
                    layer_norm_stats(nc, dve, tiles, st, mv, s["own_dve"], 0).then_inc(s["x_stats"], 1)
                    dve.wait_ge(s["x_rstd"], 1 + c + 1)
                    for j in range(TPC):
                        nc.vector.tensor_scalar(xn[:, j, :], tiles[j], mv[:, j, 0:1], rstd[:, j:j + 1],
                                                ALU.subtract, ALU.mult).then_inc(s["xn_done"], 1)
                    dve.wait_ge(s["g_psum"], 1 + c + 1)
                    nc.vector.tensor_tensor(gate[:, bass.ts(c, TPC), :],
                                            B[2][:, 0:TPC * NE].rearrange("p (j e) -> p j e", e=NE),
                                            bg[:].unsqueeze(1).broadcast_to([P, TPC, NE]), ALU.add
                                            ).then_inc(s["g_done"], 1)
                dve.sem_clear(s["own_dve"])
                own = [0]

                def after(ins):
                    own[0] += 1
                    ins.then_inc(s["own_dve"], 1)
                    dve.wait_ge(s["own_dve"], own[0])

                V = nc.vector
                dve.wait_ge(s["g_done"], 1 + NCH)
                after(V.tensor_reduce(top1[:], gate[:], AX.X, ALU.max))
                V.tensor_tensor(gate[:], gate[:], over(top1), ALU.subtract).then_inc(s["exp_in"], 1)
                dve.wait_ge(s["exp_out"], 1 + 1)
                after(V.tensor_reduce(top1[:], gate[:], AX.X, ALU.add))
                after(V.reciprocal(top2[:], top1[:]))
                after(V.tensor_tensor(gate[:], gate[:], over(top2), ALU.mult))

                def pick(one, top):
                    after(V.tensor_reduce(top[:], gate[:], AX.X, ALU.max))
                    after(V.tensor_tensor(tmp[:], gate[:], over(top), ALU.is_equal))
                    after(V.tensor_tensor(tmp[:], tmp[:], rank[:].unsqueeze(1).broadcast_to([P, NT, NE]), ALU.mult))
                    after(V.tensor_reduce(col[:], tmp[:], AX.X, ALU.max))
                    after(V.tensor_tensor(one[:], tmp[:], over(col), ALU.is_equal))

                pick(one1, top1)
                after(V.scalar_tensor_tensor(gate[:], one1[:], -2.0, gate[:], ALU.mult, ALU.add))
                pick(one2, top2)
                V.tensor_tensor(top2[:], top2[:], top1[:], ALU.subtract).then_inc(s["pair_in"], 1)
                dve.wait_ge(s["pair_out"], 1 + 1)
                after(V.tensor_scalar(top1[:], top2[:], 1.0, None, ALU.add))
                after(V.reciprocal(col[:], top1[:]))
                after(V.tensor_tensor(top2[:], top2[:], col[:], ALU.mult))
                V.tensor_tensor(one1[:], one1[:], over(col), ALU.mult)
                after(V.tensor_tensor(one2[:], one2[:], over(top2), ALU.mult))
                V.tensor_tensor(wgt[:], one1[:], one2[:], ALU.add).then_inc(s["wgt_done"], 1)
                with dve.Fori(0, NCH) as c:
                    dve.wait_ge(s["wgt_done"], 1 + 1)
                    dve.wait_ge(s["wT_psum"], 1 + c)
                    V.tensor_copy(wc[:], wgt[:, bass.ts(c, TPC), :]).then_inc(s["wc_done"], 1)
                    for j in range(TPC):
                        dve.wait_ge(s["b_psum"], 1 + c * TPC + j + 1)
                        V.tensor_copy(acc[:, c * TPC + j, :], B[4 + j][:, 0:D]).then_inc(s["b_done"], 1)
                dve.wait_ge(s["b_done"], 1 + NT)
                with dve.Fori(0, NE) as e:
                    with dve.Fori(0, NCH) as c:
                        for j in range(TPC):
                            dve.wait_ge(s["z_psum"], 1 + e * NT + c * TPC + j + 1)
                            a = acc[:, c * TPC + j, :]
                            V.scalar_tensor_tensor(a, B[4 + j][:, 0:D], wgt[:, c * TPC + j, bass.ts(e, 1)], a,
                                                   ALU.mult, ALU.add).then_inc(s["z_done"], 1)
                dve.wait_ge(s["z_done"], 1 + NE * NT)
                with dve.Fori(0, NCH) as c:
                    dve.sem_clear(s["own_dve"])
                    tiles = [acc[:, c * TPC + j, :] for j in range(TPC)]
                    layer_norm_stats(nc, dve, tiles, st, mv, s["own_dve"], 0).then_inc(s["x_stats"], 1)
                    dve.wait_ge(s["x_rstd"], 1 + c + NCH + 1)
                    for j in range(TPC):
                        last = V.tensor_scalar(xn[:, j, :], tiles[j], mv[:, j, 0:1], rstd[:, j:j + 1],
                                               ALU.subtract, ALU.mult)
                    last.then_inc(s["own_dve"], 1)
                    dve.wait_ge(s["own_dve"], 2)
                    xc = x[:, bass.ts(c, TPC), :]
                    V.tensor_tensor(xc, xc, xn[:], ALU.add).then_inc(s["own_dve"], 1)
                    dve.wait_ge(s["own_dve"], 3)

            @block.scalar
            def _(act):
                act.wait_ge(s["loaded"], LOADS)
                with act.Fori(0, NCH) as c:
                    act.wait_ge(s["xT_psum"], 1 + c * TPC + TPC)
                    for k in range(KD):
                        nc.scalar.copy(xT[:, k, :], B[k][:]).then_inc(s["xT_done"], 1)
                    for k in range(KD):
                        nc.scalar.copy(xT_all[:, k, bass.ts(c, CH)], B[k][:]).then_inc(s["xT_done"], 1)
                act.wait_ge(s["exp_in"], 1 + 1)
                nc.scalar.activation(gate[:], gate[:], ACT.Exp).then_inc(s["exp_out"], 1)
                act.wait_ge(s["pair_in"], 1 + 1)
                nc.scalar.activation(top2[:], top2[:], ACT.Exp).then_inc(s["pair_out"], 1)
                with act.Fori(0, NCH) as c:
                    act.wait_ge(s["wT_psum"], 1 + c + 1)
                    nc.scalar.copy(wT[:], B[3][0:NE, :]).then_inc(s["wT_done"], 1)
                with act.Fori(0, NE) as e:
                    with act.Fori(0, NCH) as c:
                        for m in range(KH):
                            act.wait_ge(s["h_psum"], 1 + (e * NCH + c) * KH + m + 1)
                            act.sem_inc(net.carrier, 1)
                            nc.scalar.activation(h[:, m, :], B[m % 4][:], ACT.Relu, bias=b1[:, e, m:m + 1]
                                                 ).then_inc(s["h_done"], 1)

            @block.tensor
            def _(pe):
                pe.wait_ge(s["loaded"], LOADS)
                with pe.Fori(0, NCH) as c:
                    for j in range(TPC):
                        pe.wait_ge(s["xn_done"], 1 + c * TPC + j + 1)
                        pe.wait_ge(s["xT_done"], 1 + c * 2 * KD)
                        for k in range(KD):
                            last = nc.tensor.transpose(B[k][:, j * P:(j + 1) * P], xn[:, j, k * P:(k + 1) * P],
                                                       net.ident[:])
                        last.then_inc(s["xT_psum"], 1)
                    pe.wait_ge(s["xT_done"], 1 + c * 2 * KD + KD)
                    pe.wait_ge(s["g_done"], 1 + c)
                    for j in range(TPC):
                        for k in range(KD):
                            last = nc.tensor.matmul(B[2][:, j * NE:(j + 1) * NE], xT[:, k, j * P:(j + 1) * P], wg[:, k, :],
                                                    start=(k == 0), stop=(k == KD - 1))
                    last.then_inc(s["g_psum"], 1)
                with pe.Fori(0, NCH) as c:
                    pe.wait_ge(s["wc_done"], 1 + c + 1)
                    for j in range(TPC):
                        last = nc.tensor.transpose(B[3][0:NE, j * P:(j + 1) * P], wc[:, j, :], net.ident[:])
                    last.then_inc(s["wT_psum"], 1)
                    pe.wait_ge(s["wT_done"], 1 + c + 1)
                    for j in range(TPC):
                        pe.wait_ge(s["b_done"], 1 + c * TPC)
                        nc.tensor.matmul(B[4 + j][:, 0:D], wT[:, j * P:(j + 1) * P], b2[:], start=True, stop=True
                                         ).then_inc(s["b_psum"], 1)
                pe.wait_ge(s["b_done"], 1 + NT)
                pe.wait_ge(s["xT_done"], 1 + NCH * 2 * KD)
                with pe.Fori(0, NE // 2) as e2:
                    for par in range(2):
                        e = e2 * 2 + par
                        pe.wait_ge(s[f"weights{par}"], e2 * 32 + 32)
                        pe.sem_inc(net.carrier, 1)
                        with pe.Fori(0, NCH) as c:
                            for m in range(KH):
                                i = (e * NCH + c) * KH
                                pe.wait_ge(s["h_done"], 1 + (i + m - 3 if m >= 4 else i))
                                for k in range(KD):
                                    last = nc.tensor.matmul(B[m % 4][:], w1[:, par, k, m * P:(m + 1) * P],
                                                            xT_all[:, k, bass.ts(c, CH)],
                                                            start=(k == 0), stop=(k == KD - 1))
                                last.then_inc(s["h_psum"], 1)
                            pe.wait_ge(s["h_done"], 1 + (e * NCH + c) * KH + KH)
                            for j in range(TPC):
                                pe.wait_ge(s["z_done"], 1 + (e * NCH + c) * TPC)
                                for m in range(KH):
                                    last = nc.tensor.matmul(B[4 + j][:, 0:D], h[:, m, j * P:(j + 1) * P], w2[:, par, m, :],
                                                            start=(m == 0), stop=(m == KH - 1))
                                last.then_inc(s["z_psum"], 1)


def build(nc, dram, out, phases):
    with ExitStack() as ctx:
        net = Net(nc, ctx, dram, out)
        stored = ctx.enter_context(nc.semaphore("stored"))
        with nc.Block() as block:
            @block.gpsimd
            def _(pool):
                nc.gpsimd.memset(net.half[:], -0.5)
            @block.sync
            def _(sp):
                sp.dma_start(net.x[:], dram["x"].rearrange("(n p) d -> p n d", p=P)).then_inc(stored, 16)
                sp.dma_start(net.ident[:], dram["ident"]).then_inc(stored, 16)
                sp.wait_ge(stored, 32)
        for phase in phases:
            if phase is mamba_phases:
                phase(net)
            else:
                net.run(phase)
        with nc.Block() as block:
            @block.sync
            def _(sp):
                sp.dma_start(out.rearrange("(n p) d -> p n d", p=P), net.x[:]).then_inc(stored, 16)
                sp.wait_ge(stored, 48)


def layout(a):
    import numpy as np

    def rows(w):
        return np.ascontiguousarray(w.reshape(-1, P, w.shape[-1]).transpose(1, 0, 2))

    def col(v):
        return np.ascontiguousarray(v.reshape(-1, P).T)

    a = {k: np.asarray(v) for k, v in a.items()}
    t = np.arange(P)
    sub = np.arange(SUB)
    decay = np.zeros((KV, NS, SUB), np.float32)
    gap = sub[None, :] - sub[:, None]
    decay[:SUB] = np.where(gap >= 0, 0.6 ** np.maximum(gap, 0), 0.0)[:, None, :]
    for n in range(NS):
        decay[SUB + n, n] = 0.6 ** (sub + 1)
    d = {
        "x": a["L0_attn_x"][0],
        "ident": np.eye(P, dtype=np.float32),
        "causal": (t[:, None] <= t[None, :]).astype(np.float32),
        "head_rows": (t[:, None] // DH == np.arange(8)[None, :]).astype(np.float32),
        "wqkv": rows(np.concatenate([a["L0_attn_Wq"].T, a["L0_attn_Wk"].T, a["L0_attn_Wv"].T], axis=1)),
        "wo": rows(a["L0_attn_Wo"].T),
        "bo": a["L0_attn_bo"],
        "f_w1": rows(a["L0_ffn_W1"].T),
        "f_w2": rows(a["L0_ffn_W2"].T),
        "f_b1": col(a["L0_ffn_b1"]),
        "f_b2": a["L0_ffn_b2"],
        "f_scale": a["L0_ffn_scale"].reshape(1),
        "decay": decay,
    }
    for l in range(LAYERS):
        d |= {
            f"m{l}_norm": col(a["L1_attn_norm_w"][l]),
            f"m{l}_in": rows(a["L1_attn_in_proj_w"][l].T),
            f"m{l}_conv": rows(a["L1_attn_conv_w"][l]),
            f"m{l}_conv_b": col(a["L1_attn_conv_b"][l]),
            f"m{l}_xp": rows(a["L1_attn_x_proj_w"][l].T),
            f"m{l}_dt": np.ascontiguousarray(a["L1_attn_dt_w"][l].T),
            f"m{l}_dt_b": col(a["L1_attn_dt_b"][l]),
            f"m{l}_alog": rows(a["L1_attn_A_log"][l]),
            f"m{l}_skip": col(a["L1_attn_Dp"][l]),
            f"m{l}_out": rows(a["L1_attn_out_w"][l].T),
        }
    d |= {
        "e_w1": np.ascontiguousarray(a["L1_ffn_W1"].reshape(NE, KD, P, HID).transpose(0, 2, 1, 3)),
        "e_b1": np.ascontiguousarray(a["L1_ffn_b1"].reshape(NE, KH, P).transpose(2, 0, 1)),
        "e_w2": np.ascontiguousarray(a["L1_ffn_W2"].reshape(NE, KH, P, D).transpose(0, 2, 1, 3)),
        "e_b2": a["L1_ffn_b2"],
        "e_wg": rows(a["L1_ffn_Wg"]),
        "e_bg": a["L1_ffn_bg"],
        "rank": np.arange(NE, 0, -1).astype(np.float32),
    }
    return {k: np.ascontiguousarray(v) for k, v in d.items()}


PHASES = (attention_phase, ffn_phase, mamba_phases, moe_phase)


def kernel(**inputs):
    from concourse import bacc
    from concourse.bass_utils import run_bass_kernel_spmd

    arrays = layout(inputs)
    nc = bacc.Bacc("TRN2", target_bir_lowering=False, num_devices=1)
    dram = {name: nc.dram_tensor(f"in_{name}", a.shape, mybir.dt.from_np(a.dtype), kind="ExternalInput").ap()
            for name, a in arrays.items()}
    out = nc.dram_tensor("out_x", (N, D), F32, kind="ExternalOutput").ap()
    build(nc, dram, out, PHASES)
    r = run_bass_kernel_spmd(nc, [{f"in_{name}": a for name, a in arrays.items()}], core_ids=[0])
    return r.results[0]["out_x"].reshape(1, N, D)
```

```python
from contextlib import ExitStack

import concourse.bass as bass
from concourse import mybir

F32 = mybir.dt.float32
I32 = mybir.dt.int32
ALU = mybir.AluOpType
ACT = mybir.ActivationFunctionType
AX = mybir.AxisListType

P = 128
N = 4096
D = 256
KD = D // P
CH = 512
TPC = CH // P
NCH = N // CH
NT = N // P
EPS = 1e-5
HEADS = 16
DH = D // HEADS
VE = DH + 1
HID = 1024
KH = HID // P
LAYERS = 2
DI = 512
KI = DI // P
NS = 16
RANK = 16
TAPS = 4
SUB = 64
NSUB = CH // SUB
KV = SUB + NS
SMALL = 2.0 ** -6
NE = 8


class Net:

    def __init__(self, nc, ctx, dram, out):
        self.nc, self.ctx, self.dram, self.out = nc, ctx, dram, out
        self.x = self.sb(ctx, "x_res", [P, NT, D])
        self.ident = self.sb(ctx, "ident", [P, P])
        self.half = self.sb(ctx, "minus_half", [P, TPC])
        self.var = self.sb(ctx, "var_eps", [P, TPC])
        self.carrier = ctx.enter_context(nc.semaphore("carrier"))
        self.own_pool = ctx.enter_context(nc.semaphore("own_pool"))

    def sb(self, ctx, name, shape, dt=F32):
        return ctx.enter_context(self.nc.sbuf_tensor(name, shape, dt))

    def banks(self, ctx, name):
        return [ctx.enter_context(self.nc.psum_tensor(f"{name}{i}", [P, 512], F32)) for i in range(8)]

    def own(self, name):
        self.sems.append(self.phase_ctx.enter_context(self.nc.semaphore(name)))
        return self.sems[-1]

    def sem(self, name):
        self.counts.append(self.own(name))
        return self.counts[-1]

    def start(self):
        with self.nc.Block() as block:
            @block.sync
            def _(sp):
                for count in self.counts:
                    sp.sem_inc(count, 1)

    def run(self, phase):
        with ExitStack() as self.phase_ctx:
            self.sems, self.counts = [], []
            phase(self)
            with self.nc.Block() as block:
                @block.sync
                def _(sp):
                    for used in self.sems:
                        sp.sem_clear(used)


def inverse_root(net, pool, out, variance):
    w = out.shape[-1]
    pool.sem_inc(net.carrier, 1)
    pool.sem_clear(net.own_pool)
    net.nc.gpsimd.tensor_scalar(net.var[:, 0:w], variance, EPS, None, ALU.add).then_inc(net.own_pool, 1)
    pool.wait_ge(net.own_pool, 1)
    return net.nc.gpsimd.tensor_tensor(out, net.var[:, 0:w], net.half[:, 0:w], ALU.pow)


def layer_norm_stats(nc, dve, tiles, st, mv, own, n):
    for j, t in enumerate(tiles):
        last = nc.vector.bn_stats(st[:, j, :], t)
    last.then_inc(own, 1)
    dve.wait_ge(own, n + 1)
    for j in range(len(tiles)):
        last = nc.vector.bn_aggr(mv[:, j, :], st[:, j, :])
    return last


def attention_phase(net):
    nc, dram, x = net.nc, net.dram, net.x
    with ExitStack() as ctx:
        wqkv = net.sb(ctx, "wqkv", [P, KD, 3 * D])
        wo = net.sb(ctx, "wo", [P, KD, D])
        bo = net.sb(ctx, "bo", [P, D])
        causal = net.sb(ctx, "causal", [P, P])
        head_rows = net.sb(ctx, "head_rows", [P, HEADS // KD])
        st = net.sb(ctx, "a_st", [P, TPC, 6])
        mv = net.sb(ctx, "a_mv", [P, TPC, 2])
        rstd = net.sb(ctx, "a_rstd", [P, TPC])
        xn = net.sb(ctx, "a_xn", [P, TPC, D])
        xT = net.sb(ctx, "a_xT", [P, KD, CH])
        negs = net.sb(ctx, "a_negs", [P, 2, CH])
        exps = net.sb(ctx, "a_exps", [P, 2, CH])
        phi = net.sb(ctx, "a_phi", [P, 2 * KD, CH])
        qh = net.sb(ctx, "a_qh", [P, HEADS, CH])
        kt = net.sb(ctx, "a_kt", [P, D])
        vt = net.sb(ctx, "a_vt", [P, HEADS, VE])
        probs = net.sb(ctx, "a_probs", [P, HEADS, P])
        state = net.sb(ctx, "a_state", [P, HEADS, VE])
        den = net.sb(ctx, "a_den", [P, HEADS])
        rden = net.sb(ctx, "a_rden", [P, HEADS])
        att = net.sb(ctx, "a_att", [P, D])
        attT = net.sb(ctx, "a_attT", [P, KD, P])
        z = net.sb(ctx, "a_z", [P, TPC, D])
        zn = net.sb(ctx, "a_zn", [P, TPC, D])
        B = net.banks(ctx, "a_bank")
        HG = HEADS // 4

        loaded = net.own("a_loaded")
        ones_set = net.sem("a_ones_set")
        own_dve, own_act = net.own("a_own_dve"), net.own("a_own_act")
        x_stats, x_rstd, xn_done = net.sem("a_x_stats"), net.sem("a_x_rstd"), net.sem("a_xn_done")
        xT_psum, xT_done = net.sem("a_xT_psum"), net.sem("a_xT_done")
        qk_psum, qk_exp, phi_done = net.sem("a_qk_psum"), net.sem("a_qk_exp"), net.sem("a_phi_done")
        qh_dve, qh_pool = net.sem("a_qh_dve"), net.sem("a_qh_pool")
        kv_psum, v_done, kt_exp, kt_done = (net.sem("a_kv_psum"), net.sem("a_v_done"),
                                            net.sem("a_kt_exp"), net.sem("a_kt_done"))
        s_psum, probs_done = net.sem("a_s_psum"), net.sem("a_probs_done")
        o_psum, u_psum, state_done = net.sem("a_o_psum"), net.sem("a_u_psum"), net.sem("a_state_done")
        att_done, attT_psum, attT_done = net.sem("a_att_done"), net.sem("a_attT_psum"), net.sem("a_attT_done")
        z_psum, z_stats, z_rstd = net.sem("a_z_psum"), net.sem("a_z_stats"), net.sem("a_z_rstd")

        net.start()
        with nc.Block() as block:
            @block.sync
            def _(sp):
                sp.dma_start(wqkv[:], dram["wqkv"]).then_inc(loaded, 16)
                sp.dma_start(wo[:], dram["wo"]).then_inc(loaded, 16)
                sp.dma_start(bo[:], dram["bo"].partition_broadcast(P)).then_inc(loaded, 16)
                sp.dma_start(causal[:], dram["causal"]).then_inc(loaded, 16)
                sp.dma_start(head_rows[:], dram["head_rows"]).then_inc(loaded, 16)
            LOADS = 5 * 16

            @block.gpsimd
            def _(pool):
                pool.wait_ge(loaded, LOADS)
                with pool.Fori(0, NCH) as i:
                    pool.wait_ge(x_stats, 1 + i + 1)
                    inverse_root(net, pool, rstd[:], mv[:, :, 1]).then_inc(x_rstd, 1)
                    pool.wait_ge(phi_done, 1 + i * 4 + 2)
                    pool.sem_inc(net.carrier, 1)
                    for h in range(HEADS // 2, HEADS):
                        last = nc.gpsimd.tensor_scalar(qh[:, h, :], phi[:, 1, :],
                                                       head_rows[:, h % 8:h % 8 + 1], None, ALU.mult)
                    last.then_inc(qh_pool, 1)
                    pool.wait_ge(z_stats, 1 + i + 1)
                    inverse_root(net, pool, rstd[:], mv[:, :, 1]).then_inc(z_rstd, 1)

            @block.vector
            def _(dve):
                nc.vector.memset(state[:], 0.0)
                nc.vector.memset(vt[:], 1.0).then_inc(ones_set, 1)
                dve.wait_ge(loaded, LOADS)
                with dve.Fori(0, NCH) as i:
                    dve.sem_clear(own_dve)
                    tiles = [x[:, i * TPC + j, :] for j in range(TPC)]
                    layer_norm_stats(nc, dve, tiles, st, mv, own_dve, 0).then_inc(x_stats, 1)
                    dve.wait_ge(x_rstd, 1 + i + 1)
                    for j in range(TPC):
                        nc.vector.tensor_scalar(xn[:, j, :], tiles[j], mv[:, j, 0:1], rstd[:, j:j + 1],
                                                ALU.subtract, ALU.mult).then_inc(xn_done, 1)
                    for g in range(4):
                        dve.wait_ge(qk_exp, 1 + i * 4 + g + 1)
                        nc.vector.scalar_tensor_tensor(phi[:, g, :], B[[2, 3, 0, 1][g]][:], 0.0, exps[:, g % 2, :],
                                                       ALU.max, ALU.add).then_inc(phi_done, 1)
                    dve.wait_ge(phi_done, 1 + i * 4 + 1)
                    for h in range(HEADS // 2):
                        last = nc.vector.tensor_scalar(qh[:, h, :], phi[:, 0, :],
                                                       head_rows[:, h:h + 1], None, ALU.mult)
                    last.then_inc(qh_dve, 1)
                    own = 1
                    for j in range(TPC):
                        it = i * TPC + j
                        dve.wait_ge(kt_exp, 1 + it + 1)
                        nc.vector.scalar_tensor_tensor(kt[:], B[4][:, 0:D], 0.0, exps[:, 0, 0:D],
                                                       ALU.max, ALU.add).then_inc(kt_done, 1)
                        for g in range(HG):
                            dve.wait_ge(s_psum, 1 + it * HG + g + 1)
                            nc.vector.tensor_tensor(
                                probs[:, 4 * g:4 * g + 4, :], B[5 + g % 2][:].rearrange("p (h t) -> p h t", h=4),
                                causal[:].unsqueeze(1).broadcast_to([P, 4, P]), ALU.mult).then_inc(probs_done, 1)
                        o = B[7][:, 0:HEADS * VE].rearrange("p (h e) -> p h e", e=VE)
                        dve.wait_ge(o_psum, 1 + it + 1)
                        nc.vector.tensor_scalar(den[:], o[:, :, DH], EPS, None, ALU.add).then_inc(own_dve, 1)
                        dve.wait_ge(own_dve, own + 1)
                        nc.vector.reciprocal(rden[:], den[:]).then_inc(own_dve, 1)
                        dve.wait_ge(own_dve, own + 2)
                        own += 2
                        nc.vector.tensor_tensor(att[:].rearrange("p (h e) -> p h e", e=DH), o[:, :, 0:DH],
                                                rden[:].unsqueeze(2).broadcast_to([P, HEADS, DH]),
                                                ALU.mult).then_inc(att_done, 1)
                        dve.wait_ge(u_psum, 1 + it + 1)
                        nc.vector.tensor_tensor(state[:], state[:], B[0][:, 0:HEADS * VE].rearrange(
                            "p (h e) -> p h e", e=VE), ALU.add).then_inc(state_done, 1)
                        dve.wait_ge(z_psum, 1 + it + 1)
                        last = nc.vector.tensor_tensor(z[:, j, :], B[2][:, 0:D], bo[:], ALU.add)
                    last.then_inc(own_dve, 1)
                    own += 1
                    dve.wait_ge(own_dve, own)
                    layer_norm_stats(nc, dve, [z[:, j, :] for j in range(TPC)], st, mv, own_dve, own
                                     ).then_inc(z_stats, 1)
                    own += 1
                    dve.wait_ge(z_rstd, 1 + i + 1)
                    for j in range(TPC):
                        last = nc.vector.tensor_scalar(zn[:, j, :], z[:, j, :], mv[:, j, 0:1], rstd[:, j:j + 1],
                                                       ALU.subtract, ALU.mult)
                    last.then_inc(own_dve, 1)
                    own += 1
                    dve.wait_ge(own_dve, own)
                    xc = x[:, bass.ts(i, TPC), :]
                    nc.vector.tensor_tensor(xc, xc, zn[:], ALU.add).then_inc(own_dve, 1)
                    dve.wait_ge(own_dve, own + 1)

            @block.scalar
            def _(act):
                with act.Fori(0, NCH) as i:
                    act.sem_clear(own_act)
                    own = 0
                    act.wait_ge(xT_psum, 1 + i * TPC + TPC)
                    for k in range(KD):
                        nc.scalar.copy(xT[:, k, :], B[k][:]).then_inc(xT_done, 1)
                    for g in range(4):
                        act.wait_ge(qk_psum, 1 + i * 4 + g + 1)
                        if g >= 2:
                            act.wait_ge(phi_done, 1 + i * 4 + g - 1)
                        nc.scalar.activation(negs[:, g % 2, :], B[[2, 3, 0, 1][g]][:], ACT.Relu,
                                             scale=-1.0).then_inc(own_act, 1)
                        own += 1
                        act.wait_ge(own_act, own)
                        nc.scalar.activation(exps[:, g % 2, :], negs[:, g % 2, :], ACT.Exp,
                                             scale=-1.0).then_inc(qk_exp, 1)
                    act.wait_ge(phi_done, 1 + i * 4 + 3)
                    for j in range(TPC):
                        it = i * TPC + j
                        act.wait_ge(kv_psum, 1 + it + 1)
                        if j == 0:
                            act.wait_ge(ones_set, 1 + 1)
                        nc.scalar.copy(vt[:, :, 0:DH], B[4][:, D:2 * D].rearrange("p (h e) -> p h e", e=DH)
                                       ).then_inc(v_done, 1)
                        nc.scalar.activation(negs[:, 0, 0:D], B[4][:, 0:D], ACT.Relu, scale=-1.0
                                             ).then_inc(own_act, 1)
                        own += 1
                        act.wait_ge(own_act, own)
                        if j:
                            act.wait_ge(kt_done, 1 + it)
                        nc.scalar.activation(exps[:, 0, 0:D], negs[:, 0, 0:D], ACT.Exp, scale=-1.0
                                             ).then_inc(kt_exp, 1)
                        act.wait_ge(attT_psum, 1 + it + 1)
                        nc.scalar.copy(attT[:], B[1][:, 0:D].rearrange("p (k t) -> p k t", k=KD)
                                       ).then_inc(attT_done, 1)

            @block.tensor
            def _(pe):
                pe.wait_ge(loaded, LOADS)
                with pe.Fori(0, NCH) as i:
                    for j in range(TPC):
                        pe.wait_ge(xn_done, 1 + i * TPC + j + 1)
                        for k in range(KD):
                            last = nc.tensor.transpose(B[k][:, j * P:(j + 1) * P], xn[:, j, k * P:(k + 1) * P],
                                                       net.ident[:])
                        last.then_inc(xT_psum, 1)
                    pe.wait_ge(xT_done, 1 + i * KD + KD)
                    for g in range(4):
                        for k in range(KD):
                            last = nc.tensor.matmul(B[[2, 3, 0, 1][g]][:], wqkv[:, k, g * P:(g + 1) * P], xT[:, k, :],
                                                    start=(k == 0), stop=(k == KD - 1))
                        last.then_inc(qk_psum, 1)
                    for j in range(TPC):
                        it = i * TPC + j
                        t = slice(j * P, (j + 1) * P)
                        pe.wait_ge(state_done, 1 + it)
                        pe.wait_ge(kt_done, 1 + it)
                        for k in range(KD):
                            last = nc.tensor.matmul(B[4][:], xT[:, k, t], wqkv[:, k, D:3 * D],
                                                    start=(k == 0), stop=(k == KD - 1))
                        last.then_inc(kv_psum, 1)
                        if j == 0:
                            pe.wait_ge(qh_dve, 1 + i + 1)
                            pe.wait_ge(qh_pool, 1 + i + 1)
                            pe.wait_ge(phi_done, 1 + i * 4 + 4)
                        for g in range(HG):
                            pe.wait_ge(probs_done, 1 + (it * HG + g - 1 if g >= 2 else it * HG))
                            for h in range(4 * g, 4 * g + 4):
                                last = nc.tensor.matmul(B[5 + g % 2][:, (h % 4) * P:(h % 4 + 1) * P],
                                                        phi[:, KD + h // 8, t], qh[:, h, t], start=True, stop=True)
                            last.then_inc(s_psum, 1)
                        pe.wait_ge(probs_done, 1 + it * HG + HG)
                        pe.wait_ge(v_done, 1 + it + 1)
                        pe.wait_ge(att_done, 1 + it)
                        for h in range(HEADS):
                            o = B[7][:, h * VE:(h + 1) * VE]
                            nc.tensor.matmul(o, probs[:, h, :], vt[:, h, :], start=True, stop=False)
                            last = nc.tensor.matmul(o, qh[:, h, t], state[:, h, :], start=False, stop=True)
                        last.then_inc(o_psum, 1)
                        pe.wait_ge(kt_done, 1 + it + 1)
                        for k in range(KD):
                            w = HEADS // KD * VE
                            last = nc.tensor.matmul(B[0][:, k * w:(k + 1) * w], kt[:, k * P:(k + 1) * P],
                                                    vt[:, k * 8:(k + 1) * 8, :], start=True, stop=True)
                        last.then_inc(u_psum, 1)
                        pe.wait_ge(att_done, 1 + it + 1)
                        for k in range(KD):
                            last = nc.tensor.transpose(B[1][:, k * P:(k + 1) * P], att[:, k * P:(k + 1) * P],
                                                       net.ident[:])
                        last.then_inc(attT_psum, 1)
                        pe.wait_ge(attT_done, 1 + it + 1)
                        for k in range(KD):
                            last = nc.tensor.matmul(B[2][:, 0:D], attT[:, k, :], wo[:, k, :],
                                                    start=(k == 0), stop=(k == KD - 1))
                        last.then_inc(z_psum, 1)


def ffn_phase(net):
    nc, dram, x = net.nc, net.dram, net.x
    RANK1 = 4
    with ExitStack() as ctx:
        w1 = net.sb(ctx, "f_w1", [P, KD, HID])
        w2 = net.sb(ctx, "f_w2", [P, KH, D])
        b1 = net.sb(ctx, "f_b1", [P, KH])
        b2 = net.sb(ctx, "f_b2", [P, D])
        scale = net.sb(ctx, "f_scale", [P, 1])
        tok = net.sb(ctx, "f_tok", [1, 4 * RANK1, D])
        st = net.sb(ctx, "f_st", [P, TPC, 6])
        mv = net.sb(ctx, "f_mv", [P, TPC, 2])
        rstd = net.sb(ctx, "f_rstd", [P, TPC])
        xn = net.sb(ctx, "f_xn", [P, TPC, D])
        xT = net.sb(ctx, "f_xT", [P, KD, CH])
        h = net.sb(ctx, "f_h", [P, KH, CH])
        z = net.sb(ctx, "f_z", [P, TPC, D])
        zn = net.sb(ctx, "f_zn", [P, TPC, D])
        B = net.banks(ctx, "f_bank")
        loaded, tok_done = net.own("f_loaded"), net.own("f_tok_done")
        own_dve = net.own("f_own_dve")
        first_stats, first_rstd, first_done = (net.sem("f_first_stats"), net.sem("f_first_rstd"),
                                               net.sem("f_first_done"))
        m1_psum, m2_psum, w_done = net.sem("f_m1_psum"), net.sem("f_m2_psum"), net.sem("f_w_done")
        x_stats, x_rstd, xn_done = net.sem("f_x_stats"), net.sem("f_x_rstd"), net.sem("f_xn_done")
        xT_psum, xT_done = net.sem("f_xT_psum"), net.sem("f_xT_done")
        h_psum, h_done = net.sem("f_h_psum"), net.sem("f_h_done")
        z_psum, z_done, z_stats, z_rstd = (net.sem("f_z_psum"), net.sem("f_z_done"), net.sem("f_z_stats"),
                                           net.sem("f_z_rstd"))
        LOADS = 5 * 16

        net.start()
        with nc.Block() as block:
            @block.sync
            def _(sp):
                sp.dma_start(w1[:], dram["f_w1"]).then_inc(loaded, 16)
                sp.dma_start(w2[:], dram["f_w2"]).then_inc(loaded, 16)
                sp.dma_start(b1[:], dram["f_b1"]).then_inc(loaded, 16)
                sp.dma_start(b2[:], dram["f_b2"].partition_broadcast(P)).then_inc(loaded, 16)
                sp.dma_start(scale[:], dram["f_scale"].partition_broadcast(P)).then_inc(loaded, 16)
                sp.wait_ge(first_done, 1 + 1)
                for r in range(4 * RANK1):
                    sp.dma_start(tok[:, r, :], xn[1 + r:2 + r, 0, :]).then_inc(tok_done, 16)

            @block.gpsimd
            def _(pool):
                pool.wait_ge(first_stats, 1 + 1)
                inverse_root(net, pool, rstd[:, 0:1], mv[:, 0:1, 1]).then_inc(first_rstd, 1)
                with pool.Fori(0, NCH) as i:
                    pool.wait_ge(x_stats, 1 + i + 1)
                    inverse_root(net, pool, rstd[:], mv[:, :, 1]).then_inc(x_rstd, 1)
                    pool.wait_ge(z_stats, 1 + i + 1)
                    inverse_root(net, pool, rstd[:], mv[:, :, 1]).then_inc(z_rstd, 1)

            @block.vector
            def _(dve):
                layer_norm_stats(nc, dve, [x[:, 0, :]], st, mv, own_dve, 0).then_inc(first_stats, 1)
                dve.wait_ge(first_rstd, 1 + 1)
                nc.vector.tensor_scalar(xn[:, 0, :], x[:, 0, :], mv[:, 0, 0:1], rstd[:, 0:1],
                                        ALU.subtract, ALU.mult).then_inc(first_done, 1)
                dve.wait_ge(loaded, LOADS)
                dve.wait_ge(m1_psum, 1 + 1)
                for k in range(KD):
                    for half in range(2):
                        w = w1[:, k, half * 512:(half + 1) * 512]
                        nc.vector.scalar_tensor_tensor(w, B[2 * k + half][:], scale[:, 0:1], w, ALU.mult, ALU.add)
                dve.wait_ge(m2_psum, 1 + 1)
                for q in range(4):
                    w = w2[:, 2 * q:2 * q + 2, :]
                    last = nc.vector.scalar_tensor_tensor(w, B[4 + q][:].rearrange("p (k o) -> p k o", k=2),
                                                          scale[:, 0:1], w, ALU.mult, ALU.add)
                last.then_inc(w_done, 1)
                dve.wait_ge(tok_done, 16 * 4 * RANK1)
                with dve.Fori(0, NCH) as i:
                    dve.sem_clear(own_dve)
                    tiles = [x[:, i * TPC + j, :] for j in range(TPC)]
                    layer_norm_stats(nc, dve, tiles, st, mv, own_dve, 0).then_inc(x_stats, 1)
                    dve.wait_ge(x_rstd, 1 + i + 1)
                    for j in range(TPC):
                        nc.vector.tensor_scalar(xn[:, j, :], tiles[j], mv[:, j, 0:1], rstd[:, j:j + 1],
                                                ALU.subtract, ALU.mult).then_inc(xn_done, 1)
                    for j in range(TPC):
                        dve.wait_ge(z_psum, 1 + i * TPC + j + 1)
                        nc.vector.tensor_tensor(z[:, j, :], B[6 + j % 2][:, 0:D], b2[:], ALU.add
                                                ).then_inc(z_done, 1)
                    dve.wait_ge(z_done, 1 + i * TPC + TPC)
                    layer_norm_stats(nc, dve, [z[:, j, :] for j in range(TPC)], st, mv, own_dve, 1
                                     ).then_inc(z_stats, 1)
                    dve.wait_ge(z_rstd, 1 + i + 1)
                    for j in range(TPC):
                        last = nc.vector.tensor_scalar(zn[:, j, :], z[:, j, :], mv[:, j, 0:1], rstd[:, j:j + 1],
                                                       ALU.subtract, ALU.mult)
                    last.then_inc(own_dve, 1)
                    dve.wait_ge(own_dve, 3)
                    xc = x[:, bass.ts(i, TPC), :]
                    nc.vector.tensor_tensor(xc, xc, zn[:], ALU.add).then_inc(own_dve, 1)
                    dve.wait_ge(own_dve, 4)

            @block.scalar
            def _(act):
                act.wait_ge(loaded, LOADS)
                with act.Fori(0, NCH) as i:
                    act.wait_ge(xT_psum, 1 + i * TPC + TPC)
                    for k in range(KD):
                        nc.scalar.copy(xT[:, k, :], B[k][:]).then_inc(xT_done, 1)
                    for m in range(KH):
                        act.wait_ge(h_psum, 1 + i * KH + m + 1)
                        if m == 0:
                            act.wait_ge(z_psum, 1 + i * TPC)
                        nc.scalar.activation(h[:, m, :], B[2 + m % 4][:], ACT.Gelu, bias=b1[:, m:m + 1]
                                             ).then_inc(h_done, 1)

            @block.tensor
            def _(pe):
                pe.wait_ge(tok_done, 16 * 4 * RANK1)
                for k in range(KD):
                    for i in range(RANK1):
                        last = nc.tensor.matmul(B[2 * k + i // 2][:, (i % 2) * D:(i % 2 + 1) * D],
                                                tok[0:1, 2 * i + 1, k * P:(k + 1) * P], tok[0:1, 2 * i, :],
                                                start=True, stop=True)
                last.then_inc(m1_psum, 1)
                for m in range(KH):
                    r, half = m // 2, m % 2
                    for i in range(RANK1):
                        col = (m % 2) * D + i * (D // 4)
                        last = nc.tensor.matmul(B[4 + m // 2][:, col:col + D // 4],
                                                tok[0:1, 2 * (RANK1 + i) + 1, half * P:(half + 1) * P],
                                                tok[0:1, 2 * (RANK1 + i), r:D:4], start=True, stop=True)
                last.then_inc(m2_psum, 1)
                pe.wait_ge(w_done, 1 + 1)
                with pe.Fori(0, NCH) as i:
                    for j in range(TPC):
                        pe.wait_ge(xn_done, 1 + i * TPC + j + 1)
                        for k in range(KD):
                            last = nc.tensor.transpose(B[k][:, j * P:(j + 1) * P], xn[:, j, k * P:(k + 1) * P],
                                                       net.ident[:])
                        last.then_inc(xT_psum, 1)
                    pe.wait_ge(xT_done, 1 + i * KD + KD)
                    for m in range(KH):
                        pe.wait_ge(h_done, 1 + (i * KH + m - 3 if m >= 4 else i * KH))
                        for k in range(KD):
                            last = nc.tensor.matmul(B[2 + m % 4][:], w1[:, k, m * P:(m + 1) * P], xT[:, k, :],
                                                    start=(k == 0), stop=(k == KD - 1))
                        last.then_inc(h_psum, 1)
                    pe.wait_ge(h_done, 1 + i * KH + KH)
                    for j in range(TPC):
                        pe.wait_ge(z_done, 1 + (i * TPC + j - 1 if j >= 2 else i * TPC))
                        for m in range(KH):
                            last = nc.tensor.matmul(B[6 + j % 2][:, 0:D], h[:, m, j * P:(j + 1) * P], w2[:, m, :],
                                                    start=(m == 0), stop=(m == KH - 1))
                        last.then_inc(z_psum, 1)


BF16 = mybir.dt.bfloat16
CM = 256
TM = CM // P
NCM = N // CM
NSUB = CM // SUB
BETA = 0.6
LAG = 2


def mamba_phase(net, layer, xm):
    nc = net.nc
    dram = net.dram
    nm = lambda t: f"m{layer}_{t}"
    with ExitStack() as ctx:
        sb = lambda t, shape, dt=F32: net.sb(ctx, nm(t), shape, dt)
        norm, w_in, conv, conv_b = sb("norm", [P, KD]), sb("in", [P, KD, 2 * DI]), sb("conv", [P, KI, TAPS]), sb("cb", [P, KI])
        w_xp, dt_b = sb("xp", [P, KI, RANK + 2 * NS]), sb("dtb", [P, KI])
        shared = sb("shared", [KV, DI])
        w_dt, v_end = shared[0:RANK, :], shared[32:32 + NS, :]
        vhi, vlo = (shared[SUB:KV, :].bitcast(BF16)[:, i * DI:(i + 1) * DI] for i in range(2))
        rate, skip, w_out = sb("rate", [P, KI, NS]), sb("skip", [P, KI]), sb("out", [P, KI, D])
        decay = sb("decay", [SUB, SUB])
        st, mv, rstd, msq = sb("st", [P, TM, 6]), sb("mv", [P, TM, 2]), sb("rstd", [P, TM]), sb("msq", [P, TM])
        xb, zs, delta = (sb(t, [P, 2, KI, CM]) for t in ("xb", "zs", "delta"))
        xpre = sb("xpre", [P, KI, TAPS - 1 + CM])
        cv = sb("cv", [P, KI, CM])
        u = sb("u", [P, KI, CM])
        pair = sb("pair", [P, 2, KD, CM])
        mask = sb("mask", [P, KI, CM], mybir.dt.uint8)
        xp = u[0:RANK + 2 * NS, 0, :]
        low = xp[0:RANK]
        v_mid = u[0:NS].rearrange("n (a k) t -> n a (k t)", a=2)
        Bs, Cs = sb("Bs", [SUB, NSUB, NS]), sb("Cs", [P, 2, TM, NS])
        Mf = sb("Mf", [KV, NS, SUB])
        Mhi, Mlo = sb("Mhi", [KV, 2, NSUB, NS, SUB], BF16), sb("Mlo", [KV, 2, NSUB, NS, SUB], BF16)
        Uhi, Ulo = sb("Uhi", [KV, 2, NSUB, DI], BF16), sb("Ulo", [KV, 2, NSUB, DI], BF16)
        dA = sb("dA", [P, 2, KI, CM])
        h = sb("h", [P, 2, KI, CM])
        hlast = sb("hlast", [P, NS, KI])
        y = sb("y", [P, 2, TM, DI])
        prod = sb("prod", [P, 2, DI])
        xr = pair[:, 0].rearrange("p k t -> p (k t)").rearrange("p (j d) -> p j d", d=D)
        xT = pair[:, 1]
        series = pair[:].rearrange("p a k t -> p (a k) t")
        decay_n = decay[:].unsqueeze(1).broadcast_to([SUB, NS, SUB])
        banks = net.banks(ctx, nm("bank"))
        VB, HB, H0, H1 = banks[0:4], banks[4:6], banks[6], banks[7]
        names = ("loaded own_dve own_act own_pool setup rms_in rms_out xr_done xT_psum xT_done in_psum pre_done "
                 "z_done conv_done xb_done bc_psum xp_psum xp_done dt_psum dt_done exp_done ln_done "
                 "mask_done u_done delta_done uT_psum uhi_done ulo_done "
                 "mf_done mhi_done mlo_done halo_done before_done carry_psum carry_done vhi_done vlo_done v_psum da_done scan_done "
                 "hlast_done ht_psum prod_done y_dve y_pool yT_psum gated_done out_psum xm_done rate_done const_done"
                 ).split()
        s = {n: (net.own if n == "loaded" or "own" in n else net.sem)(nm(n)) for n in names}
        LOADS = 12 * 16
        net.start()
        with nc.Block() as block:
            @block.sync
            def _(sp):
                for t, key in ((norm, "norm"), (w_in, "in"), (conv, "conv"), (conv_b, "conv_b"), (w_xp, "xp"),
                               (shared, "dt"), (dt_b, "dt_b"), (rate, "alog"), (skip, "skip"), (w_out, "out")):
                    sp.dma_start(t[:] if key != "dt" else w_dt, dram[f"m{layer}_{key}"]).then_inc(s["loaded"], 16)
                sp.dma_start(decay[:], dram["decay"][0:SUB, 0]).then_inc(s["loaded"], 16)
                sp.dma_start(Mf[SUB:KV], dram["decay"][SUB:KV]).then_inc(s["loaded"], 16)

            @block.gpsimd
            def _(pool):
                nc.gpsimd.memset(xpre[:], 0.0)
                nc.gpsimd.memset(hlast[:], 0.0)
                for t in (y, xb, zs):
                    last = nc.gpsimd.memset(t[:, 1], 0.0)
                last.then_inc(s["setup"], 1)
                pool.wait_ge(s["setup"], 1 + 1)
                pool.wait_ge(s["loaded"], LOADS)

                def head(q, par, slot):
                    if slot == 1:
                        pool.wait_ge(s["rms_in"], 1 + q + 1)
                        inverse_root(net, pool, rstd[:], msq[:]).then_inc(s["rms_out"], 1)
                    if slot == 3:
                        pool.wait_ge(s["conv_done"], 1 + q * KI)
                        pool.sem_inc(net.carrier, 1)
                        nc.gpsimd.tensor_copy(xpre[:, :, 0:TAPS - 1], xpre[:, :, CM:CM + TAPS - 1]
                                              ).then_inc(s["halo_done"], 1)
                    if slot == 12:
                        pool.wait_ge(s["exp_done"], 1 + q + 1)
                        pool.sem_inc(net.carrier, 1)
                        nc.gpsimd.tensor_scalar(mask[:], cv[:], SMALL, None, ALU.is_lt).then_inc(s["mask_done"], 1)
                    if slot in (11, 13, 14, 15):
                        j = (11, 13, 14, 15).index(slot)
                        pool.wait_ge(s["mhi_done"], 1 + q * NSUB + j + 1)
                        nc.gpsimd.tensor_tensor(Mlo[0:SUB, par, j], Mf[0:SUB], Mhi[0:SUB, par, j], ALU.subtract
                                                ).then_inc(s["mlo_done"], 1)
                    if slot in (10, 12, 13, 14):
                        j = (10, 12, 13, 14).index(slot)
                        pool.wait_ge(s["xp_done"], 1 + q * 3 + 2)
                        pool.wait_ge(s["mlo_done"], 1 + q * NSUB + j)
                        nc.gpsimd.tensor_tensor(Mf[0:SUB], decay_n, Bs[:, j, :].unsqueeze(2).broadcast_to(
                            [SUB, NS, SUB]), ALU.mult).then_inc(s["mf_done"], 1)

                def slots(c, par):
                    for n in range(NS + LAG):
                        if n < NS:
                            pool.wait_ge(s["scan_done"], 1 + (c * NS + n + 1) * KI)
                            pool.sem_inc(net.carrier, 1)
                            nc.gpsimd.tensor_copy(hlast[:, n, :], h[:, n % 2, :, CM - 1]).then_inc(s["hlast_done"], 1)
                        if n >= LAG:
                            k = c * NS + n - LAG
                            out = y[:, par, 1, :]
                            pool.wait_ge(s["y_pool"], 1 + k)
                            pool.wait_ge(s["prod_done"], 1 + k + 1)
                            if n == LAG:
                                pool.sem_inc(net.carrier, 1)
                                nc.gpsimd.tensor_copy(out, prod[:, n % 2, :]).then_inc(s["y_pool"], 1)
                            else:
                                nc.gpsimd.tensor_tensor(out, out, prod[:, n % 2, :], ALU.add).then_inc(s["y_pool"], 1)
                        head(c + 1, 1 - par, n)

                for slot in range(NS + LAG):
                    head(0, 0, slot)
                with pool.Fori(0, NCM // 2) as c2:
                    slots(c2 * 2, 0)
                    slots(c2 * 2 + 1, 1)

            @block.vector
            def _(dve):
                dve.wait_ge(s["loaded"], LOADS)
                dve.wait_ge(s["setup"], 1 + 1)
                nc.vector.memset(vhi, 0.0)
                nc.vector.memset(vlo, 0.0)
                nc.vector.memset(v_end, 0.0)
                for par in range(2):
                    for j in range(NSUB):
                        V = nc.vector.tensor_copy(Mhi[SUB:KV, par, j], Mf[SUB:KV])
                V.then_inc(s["const_done"], 1)
                dve.wait_ge(s["const_done"], 1 + 1)
                for par in range(2):
                    for j in range(NSUB):
                        V = nc.vector.tensor_tensor(Mlo[SUB:KV, par, j], Mf[SUB:KV], Mhi[SUB:KV, par, j], ALU.subtract)
                V.then_inc(s["const_done"], 1)
                own = [0]

                def after(ins):
                    own[0] += 1
                    ins.then_inc(s["own_dve"], 1)
                    dve.wait_ge(s["own_dve"], own[0])

                def restart():
                    dve.sem_clear(s["own_dve"])
                    own[0] = 0

                def head(q, par, slot):
                    tiles = [xm[:, (q + 1) * TM + j, :] for j in range(TM)]
                    if slot == 0:
                        after(layer_norm_stats(nc, dve, tiles, st, mv, s["own_dve"], own[0]))
                        own[0] += 1
                        dve.wait_ge(s["own_dve"], own[0])
                        after(nc.vector.tensor_tensor(msq[:], mv[:, :, 0], mv[:, :, 0], ALU.mult))
                        nc.vector.tensor_tensor(msq[:], msq[:], mv[:, :, 1], ALU.add).then_inc(s["rms_in"], 1)
                    if slot == 2:
                        dve.wait_ge(s["rms_out"], 1 + q + 1)
                        for j in range(TM):
                            nc.vector.tensor_scalar(xr[:, j, :], tiles[j], rstd[:, j:j + 1], None, ALU.mult
                                                    ).then_inc(s["xr_done"], 1)
                    if slot == 6:
                        dve.wait_ge(s["pre_done"], 1 + q * 2 + 2)
                        dve.wait_ge(s["halo_done"], 1 + q + 1)
                    for m in {6: (0, 1), 7: (2,), 8: (3,)}.get(slot, ()):
                        after(nc.vector.tensor_scalar(cv[:, m, :], xpre[:, m, 0:CM], conv[:, m, 0:1], None, ALU.mult))
                        for k in range(1, TAPS):
                            i = nc.vector.scalar_tensor_tensor(cv[:, m, :], xpre[:, m, k:k + CM], conv[:, m, k:k + 1],
                                                               cv[:, m, :], ALU.mult, ALU.add)
                            if k < TAPS - 1:
                                after(i)
                        i.then_inc(s["conv_done"], 1)
                    if slot == 9:
                        dve.wait_ge(s["vlo_done"], 1 + q * NSUB)
                        nc.vector.tensor_copy(Uhi[SUB:KV, par, 0, :], vhi)
                        nc.vector.tensor_copy(Ulo[SUB:KV, par, 0, :], vlo).then_inc(s["before_done"], 1)
                    if slot in (11, 13, 14, 15):
                        j = (11, 13, 14, 15).index(slot)
                        dve.wait_ge(s["mf_done"], 1 + q * NSUB + j + 1)
                        nc.vector.tensor_copy(Mhi[0:SUB, par, j], Mf[0:SUB]).then_inc(s["mhi_done"], 1)
                    if slot == 12:
                        dve.wait_ge(s["exp_done"], 1 + q + 1)
                        after(nc.vector.tensor_scalar(series, cv[:], -0.25, 1 / 3, ALU.mult, ALU.add))
                        after(nc.vector.tensor_tensor(series, series, cv[:], ALU.mult))
                        after(nc.vector.scalar_tensor_tensor(series, series, -0.5, cv[:], ALU.add, ALU.mult))
                        after(nc.vector.scalar_tensor_tensor(series, series, 1.0, cv[:], ALU.add, ALU.mult))
                    if slot == 13:
                        dve.wait_ge(s["ln_done"], 1 + q + 1)
                        dve.wait_ge(s["mask_done"], 1 + q + 1)
                        dve.sem_inc(net.carrier, 1)
                        after(nc.vector.copy_predicated(u[:], mask[:], series))
                        nc.vector.tensor_tensor(delta[:, par], delta[:, par], u[:], ALU.add).then_inc(s["delta_done"], 1)
                        dve.wait_ge(s["delta_done"], 1 + q + 1)
                        nc.vector.tensor_tensor(u[:], delta[:, par], xb[:, par], ALU.mult).then_inc(s["u_done"], 1)
                    if slot in (14, 15):
                        for j in ((0, 1) if slot == 14 else (2, 3)):
                            dve.wait_ge(s["uhi_done"], 1 + q * NSUB + j + 1)
                            nc.vector.tensor_tensor(Ulo[0:SUB, par, j, :], (H0, H1)[j % 2][0:SUB, :],
                                                    Uhi[0:SUB, par, j, :], ALU.subtract).then_inc(s["ulo_done"], 1)
                    if slot == 16:
                        for i in (0, 1, -1, 2, -2, 3, -3, -4):
                            last = i in (NSUB - 1, -NSUB)
                            if i >= 0:
                                before = v_end if i == 0 else v_mid[:, (i - 1) % 2, :]
                                new = v_end if last else v_mid[:, i % 2, :]
                                dve.wait_ge(s["carry_psum"], 1 + q * NSUB + i + 1)
                                dve.wait_ge(s["carry_done"], 1 + q * NSUB + i)
                                if i >= 2:
                                    dve.wait_ge(s["vlo_done"], 1 + q * NSUB + i - 1)
                                nc.vector.scalar_tensor_tensor(new, before, BETA ** SUB, (H0, H1)[i % 2][0:NS, :],
                                                               ALU.mult, ALU.add).then_inc(s["carry_done"], 1)
                            else:
                                j = -1 - i
                                hi = vhi if last else Uhi[SUB:KV, par, j + 1, :]
                                lo = vlo if last else Ulo[SUB:KV, par, j + 1, :]
                                dve.wait_ge(s["vhi_done"], 1 + q * NSUB + j + 1)
                                nc.vector.tensor_tensor(lo, v_end if last else v_mid[:, j % 2, :], hi,
                                                        ALU.subtract).then_inc(s["vlo_done"], 1)

                def tail(t, par, slot):
                    if slot == 1:
                        for m in range(KI):
                            dve.wait_ge(s["yT_psum"], 1 + t * 2 + m // 2 + 1)
                            g = u[:, m, :]
                            after(nc.vector.scalar_tensor_tensor(g, xb[:, par, m, :], skip[:, m:m + 1],
                                                                 (H0, H1)[m // 2][:, m % 2 * CM:(m % 2 + 1) * CM],
                                                                 ALU.mult, ALU.add))
                            nc.vector.tensor_tensor(g, g, zs[:, par, m, :], ALU.mult).then_inc(s["gated_done"], 1)
                    if slot == 3:
                        dve.wait_ge(s["out_psum"], 1 + t + 1)
                        to = xm[:, bass.ts(t, TM), :]
                        nc.vector.tensor_tensor(to, to, H0[:].rearrange("p (j d) -> p j d", d=D), ALU.add
                                                ).then_inc(s["xm_done"], 1)

                def slots(c, par):
                    restart()
                    for n in range(NS + LAG):
                        if n < NS:
                            if n == 0:
                                dve.wait_ge(s["hlast_done"], 1 + c * NS)
                            if n >= 2:
                                dve.wait_ge(s["hlast_done"], 1 + c * NS + n - 1)
                                dve.wait_ge(s["ht_psum"], 1 + (c * NS + n - 1) * 2)
                            for m in range(KI):
                                dve.wait_ge(s["v_psum"], 1 + (c * NS + n) * 2 + m // 2 + 1)
                                dve.wait_ge(s["da_done"], 1 + (c * NS + n) * KI + m + 1)
                                nc.vector.tensor_tensor_scan(
                                    h[:, n % 2, m, :], dA[:, n % 2, m, :],
                                    VB[(n % 2) * 2 + m // 2][:, (m % 2) * CM:(m % 2 + 1) * CM],
                                    hlast[:, n, m:m + 1], ALU.mult, ALU.add).then_inc(s["scan_done"], 1)
                        if n >= LAG:
                            k = c * NS + n - LAG
                            out = y[:, par, 0, :]
                            dve.wait_ge(s["ht_psum"], 1 + k * 2 + 2)
                            C = Cs[:, par, 0, n - LAG:n - LAG + 1]
                            if n == LAG:
                                nc.vector.tensor_scalar(out, HB[0][:], C, None, ALU.mult).then_inc(s["y_dve"], 1)
                            else:
                                dve.wait_ge(s["y_dve"], 1 + k)
                                nc.vector.scalar_tensor_tensor(out, HB[0][:], C, out, ALU.mult, ALU.add
                                                               ).then_inc(s["y_dve"], 1)
                        tail(c, 1 - par, n)
                        head(c + 1, 1 - par, n)

                restart()
                for slot in range(NS + LAG):
                    head(0, 0, slot)
                with dve.Fori(0, NCM // 2) as c2:
                    slots(c2 * 2, 0)
                    slots(c2 * 2 + 1, 1)
                restart()
                for slot in range(4):
                    tail(NCM, 1, slot)

            @block.scalar
            def _(act):
                act.wait_ge(s["loaded"], LOADS)
                nc.scalar.activation(rate[:], rate[:], ACT.Exp).then_inc(s["rate_done"], 1)
                act.wait_ge(s["rate_done"], 1 + 1)
                nc.scalar.mul(rate[:], rate[:], -1.0).then_inc(s["rate_done"], 1)
                act.wait_ge(s["rate_done"], 1 + 2)
                act.wait_ge(s["setup"], 1 + 1)
                halves = lambda bank: bank[:].rearrange("p (k t) -> p k t", k=2)

                def head(q, par, slot):
                    if slot == 4:
                        act.wait_ge(s["xT_psum"], 1 + q + 1)
                        for k in range(KD):
                            nc.scalar.activation(xT[:, k, :], halves(H0)[:, k, :], ACT.Copy, scale=norm[:, k:k + 1]
                                                 ).then_inc(s["xT_done"], 1)
                    if slot == 5:
                        act.wait_ge(s["halo_done"], 1 + q + 1)
                        for g in range(2):
                            act.wait_ge(s["in_psum"], 1 + q * 4 + g + 1)
                            nc.scalar.copy(xpre[:, 2 * g:2 * g + 2, TAPS - 1:], halves((H1, H0)[g])
                                           ).then_inc(s["pre_done"], 1)
                    if slot == 7:
                        for g in range(2):
                            act.wait_ge(s["in_psum"], 1 + q * 4 + g + 3)
                            if g == 0:
                                act.wait_ge(s["conv_done"], 1 + q * KI + 1)
                            nc.scalar.activation(zs[:, par, 2 * g:2 * g + 2, :], halves((H1, H0)[g]), ACT.Silu
                                                 ).then_inc(s["z_done"], 1)
                    if slot == 8:
                        for m in range(KI):
                            act.wait_ge(s["conv_done"], 1 + q * KI + m + 1)
                            nc.scalar.activation(xb[:, par, m, :], cv[:, m, :], ACT.Silu, bias=conv_b[:, m:m + 1]
                                                 ).then_inc(s["xb_done"], 1)
                    if slot == 9:
                        act.wait_ge(s["xp_psum"], 1 + q + 1)
                        nc.scalar.copy(xp, H1[0:RANK + 2 * NS, 0:CM]).then_inc(s["xp_done"], 1)
                    if slot == 10:
                        act.wait_ge(s["bc_psum"], 1 + q + 1)
                        nc.scalar.copy(Bs[:], H1[0:SUB, CM:CM + NSUB * NS].rearrange("p (a n) -> p a n", n=NS)
                                       ).then_inc(s["xp_done"], 1)
                        nc.scalar.copy(Cs[:, par], H1[:, CM + 64:CM + 64 + TM * NS].rearrange("p (a n) -> p a n", n=NS)
                                       ).then_inc(s["xp_done"], 1)
                    if slot in (10, 11):
                        for m in ((0, 1) if slot == 10 else (2, 3)):
                            act.wait_ge(s["dt_psum"], 1 + q * 2 + m // 2 + 1)
                            v = halves((H0, H1)[m // 2])[:, m % 2, :]
                            nc.scalar.activation(delta[:, par, m, :], v, ACT.Relu, bias=dt_b[:, m:m + 1])
                            nc.scalar.activation(cv[:, m, :], v, ACT.Abs, bias=dt_b[:, m:m + 1]
                                                 ).then_inc(s["dt_done"], 1)
                    if slot == 11:
                        act.wait_ge(s["dt_done"], 1 + q * KI + KI)
                        nc.scalar.activation(cv[:], cv[:], ACT.Exp, scale=-1.0).then_inc(s["exp_done"], 1)
                    if slot == 12:
                        act.wait_ge(s["exp_done"], 1 + q + 1)
                        nc.scalar.activation(u[:], cv[:], ACT.Ln, bias=1.0).then_inc(s["ln_done"], 1)
                    if slot in (14, 15):
                        for j in ((0, 1) if slot == 14 else (2, 3)):
                            act.wait_ge(s["uT_psum"], 1 + q * NSUB + j + 1)
                            nc.scalar.copy(Uhi[0:SUB, par, j, :], (H0, H1)[j % 2][0:SUB, :]).then_inc(s["uhi_done"], 1)
                    if slot == 16:
                        for j in range(NSUB):
                            last = j == NSUB - 1
                            act.wait_ge(s["carry_done"], 1 + q * NSUB + j + 1)
                            nc.scalar.copy(vhi if last else Uhi[SUB:KV, par, j + 1, :],
                                           v_end if last else v_mid[:, j % 2, :]).then_inc(s["vhi_done"], 1)

                def decays(c, par, n, first=False):
                    if n == 0:
                        act.wait_ge(s["delta_done"], 1 + c + 1)
                    for m in range(KI):
                        if n != 1 and not first:
                            act.wait_ge(s["scan_done"], 1 + (c * NS + n - 2) * KI + m + 1)
                        act.sem_inc(net.carrier, 1)
                        nc.scalar.activation(dA[:, n % 2, m, :], delta[:, par, m, :], ACT.Exp,
                                             scale=rate[:, m, n:n + 1]).then_inc(s["da_done"], 1)

                def slots(c, par):
                    for n in range(NS + LAG):
                        if n < NS - 1:
                            decays(c, par, n + 1)
                        if n == NS:
                            decays(c + 1, 1 - par, 0)
                        if n >= LAG:
                            k = c * NS + n - LAG
                            act.wait_ge(s["ht_psum"], 1 + k * 2 + 1)
                            act.wait_ge(s["y_pool"], 1 + (k - 1 if n > LAG else k))
                            nc.scalar.activation(prod[:, n % 2, :], HB[1][:], ACT.Copy,
                                                 scale=Cs[:, par, 1, n - LAG:n - LAG + 1]).then_inc(s["prod_done"], 1)
                        head(c + 1, 1 - par, n)

                for slot in range(NS + LAG):
                    head(0, 0, slot)
                decays(0, 0, 0, True)
                with act.Fori(0, NCM // 2) as c2:
                    slots(c2 * 2, 0)
                    slots(c2 * 2 + 1, 1)

            @block.tensor
            def _(pe):
                pe.wait_ge(s["loaded"], LOADS)
                pe.wait_ge(s["setup"], 1 + 1)
                pe.wait_ge(s["const_done"], 1 + 2)
                PARTS = ((Mlo, Uhi), (Mhi, Ulo), (Mhi, Uhi))

                def head(q, par, slot):
                    if slot == 4:
                        pe.wait_ge(s["xr_done"], 1 + q * TM + TM)
                        pe.wait_ge(s["xm_done"], 1 + q)
                        for j in range(TM):
                            for k in range(KD):
                                last = nc.tensor.transpose(H0[:, k * CM + j * P:k * CM + (j + 1) * P],
                                                           xr[:, j, k * P:(k + 1) * P], net.ident[:])
                        last.then_inc(s["xT_psum"], 1)
                    if slot in (5, 6):
                        if slot == 5:
                            pe.wait_ge(s["xT_done"], 1 + q * KD + KD)
                        for g in ((0, 1) if slot == 5 else (2, 3)):
                            bank = (H1, H0)[g % 2]
                            if g == 0:
                                pe.wait_ge(s["gated_done"], 1 + q * KI)
                            if g >= 2:
                                pe.wait_ge(s["pre_done"], 1 + q * 2 + g - 1)
                            for half in range(2):
                                m = 2 * g + half
                                for k in range(KD):
                                    last = nc.tensor.matmul(bank[:, half * CM:(half + 1) * CM],
                                                            w_in[:, k, m * P:(m + 1) * P], xT[:, k, :],
                                                            start=(k == 0), stop=(k == KD - 1))
                            last.then_inc(s["in_psum"], 1)
                    if slot == 9:
                        pe.wait_ge(s["xb_done"], 1 + q * KI + KI)
                        for k in range(KI):
                            last = nc.tensor.matmul(H1[0:RANK + 2 * NS, 0:CM], w_xp[:, k, :], xb[:, par, k, :],
                                                    start=(k == 0), stop=(k == KI - 1))
                        last.then_inc(s["xp_psum"], 1)
                    if slot == 10:
                        pe.wait_ge(s["xp_done"], 1 + q * 3 + 1)
                        pe.sem_inc(net.carrier, 1)
                        for j in range(NSUB):
                            nc.tensor.matmul(H1[0:SUB, CM + j * NS:CM + (j + 1) * NS], xp[:, j * SUB:(j + 1) * SUB],
                                             net.ident[0:RANK + 2 * NS, RANK:RANK + NS], start=True, stop=True)
                        for j in range(TM):
                            last = nc.tensor.matmul(H1[:, CM + 64 + j * NS:CM + 64 + (j + 1) * NS],
                                                    xp[:, j * P:(j + 1) * P],
                                                    net.ident[0:RANK + 2 * NS, RANK + NS:RANK + 2 * NS],
                                                    start=True, stop=True)
                        last.then_inc(s["bc_psum"], 1)
                        for g in range(2):
                            pe.wait_ge(s["xp_done"], 1 + q * 3 + (1, 3)[g])
                            for half in range(2):
                                m = 2 * g + half
                                last = nc.tensor.matmul((H0, H1)[g][:, half * CM:(half + 1) * CM],
                                                        w_dt[:, m * P:(m + 1) * P], low, start=True, stop=True)
                            last.then_inc(s["dt_psum"], 1)
                    if slot in (14, 15):
                        if slot == 14:
                            pe.wait_ge(s["u_done"], 1 + q + 1)
                            pe.wait_ge(s["dt_done"], 1 + q * KI + KI)
                        for j in ((0, 1) if slot == 14 else (2, 3)):
                            if j >= 2:
                                pe.wait_ge(s["ulo_done"], 1 + q * NSUB + j - 1)
                            pe.sem_inc(net.carrier, 1)
                            for m in range(KI):
                                last = nc.tensor.transpose((H0, H1)[j % 2][0:SUB, m * P:(m + 1) * P],
                                                           u[:, m, j * SUB:(j + 1) * SUB], net.ident[:])
                            last.then_inc(s["uT_psum"], 1)
                    if slot == 16:
                        for j in range(NSUB):
                            pe.wait_ge(s["mlo_done"], 1 + q * NSUB + j + 1)
                            pe.wait_ge(s["ulo_done"], 1 + q * NSUB + NSUB)
                            if j >= 2:
                                pe.wait_ge(s["carry_done"], 1 + q * NSUB + j - 1)
                            pe.sem_inc(net.carrier, 1)
                            for i, (m_part, u_part) in enumerate(PARTS):
                                last = nc.tensor.matmul((H0, H1)[j % 2][0:NS, :], m_part[0:SUB, par, j, :, SUB - 1],
                                                        u_part[0:SUB, par, j, :], start=(i == 0), stop=(i == 2))
                            last.then_inc(s["carry_psum"], 1)

                def tail(t, par, slot):
                    if slot == 0:
                        pe.wait_ge(s["vlo_done"], 1 + (t + 1) * NSUB)
                        pe.wait_ge(s["y_dve"], 1 + t * NS)
                        pe.wait_ge(s["y_pool"], 1 + t * NS)
                        for m in range(KI):
                            for j in range(TM):
                                last = nc.tensor.transpose(
                                    (H0, H1)[m // 2][:, (m % 2) * CM + j * P:(m % 2) * CM + (j + 1) * P],
                                    y[:, par, j, m * P:(m + 1) * P], net.ident[:])
                            if m % 2:
                                last.then_inc(s["yT_psum"], 1)
                    if slot == 2:
                        pe.wait_ge(s["gated_done"], 1 + t * KI + KI)
                        for j in range(TM):
                            for k in range(KI):
                                last = nc.tensor.matmul(H0[:, j * D:(j + 1) * D], u[:, k, j * P:(j + 1) * P],
                                                        w_out[:, k, :], start=(k == 0), stop=(k == KI - 1))
                        last.then_inc(s["out_psum"], 1)

                def turn(c, n):
                    k = c * NS + n
                    pe.wait_ge(s["scan_done"], 1 + (k + 1) * KI)
                    for tt in (1, 0):
                        if tt:
                            pe.wait_ge(s["prod_done"], 1 + k)
                        else:
                            pe.wait_ge(s["y_dve"], 1 + k)
                        for m in range(KI):
                            last = nc.tensor.transpose(HB[tt][:, m * P:(m + 1) * P],
                                                       h[:, n % 2, m, tt * P:(tt + 1) * P], net.ident[:])
                        last.then_inc(s["ht_psum"], 1)

                def velocity(c, par, n):
                    if n >= 2:
                        pe.wait_ge(s["scan_done"], 1 + (c * NS + n - 1) * KI)
                    for j in range(NSUB) if n == 0 else (None,):
                        if j == 0:
                            pe.wait_ge(s["before_done"], 1 + c + 1)
                        elif j:
                            pe.wait_ge(s["vlo_done"], 1 + c * NSUB + j)
                        for m in range(KI):
                            bank = VB[(n % 2) * 2 + m // 2]
                            for jj in range(NSUB) if j is None else (j,):
                                at = (m % 2) * CM + jj * SUB
                                for i, (m_part, u_part) in enumerate(PARTS):
                                    last = nc.tensor.matmul(bank[:, at:at + SUB], u_part[:, par, jj, m * P:(m + 1) * P],
                                                            m_part[:, par, jj, n, :], start=(i == 0), stop=(i == 2))
                            if m % 2 and (j is None or j == NSUB - 1):
                                last.then_inc(s["v_psum"], 1)

                def slots(c, par):
                    velocity(c, par, 0)
                    for n in range(NS + LAG):
                        if n < NS - 1:
                            velocity(c, par, n + 1)
                        if n >= 1 and n <= NS:
                            turn(c, n - 1)
                        tail(c, 1 - par, n)
                        head(c + 1, 1 - par, n)

                for slot in range(NS + LAG):
                    head(0, 0, slot)
                with pe.Fori(0, NCM // 2) as c2:
                    slots(c2 * 2, 0)
                    slots(c2 * 2 + 1, 1)
                for slot in range(3):
                    tail(NCM, 1, slot)


def mamba_phases(net):
    nc, x = net.nc, net.x
    with ExitStack() as ctx:
        xm = net.sb(ctx, "xm", [P, NT + 2 * TM, D])
        net.run(lambda n: stream_in(n, xm))
        for layer in range(LAYERS):
            net.run(lambda n: mamba_phase(n, layer, xm))
        net.run(lambda n: stream_out(n, xm))


def normalise_all(net, ctx, tag, source, target, add):
    nc = net.nc
    st, mv = net.sb(ctx, tag + "st", [P, NT, 6]), net.sb(ctx, tag + "mv", [P, NT, 2])
    var, rstd, half = net.sb(ctx, tag + "var", [P, NT]), net.sb(ctx, tag + "rstd", [P, NT]), net.sb(ctx, tag + "half", [P, NT])
    tmp = net.sb(ctx, tag + "tmp", [P, 2, TPC, D])
    stats, root, own, done = net.sem(tag + "stats"), net.sem(tag + "root"), net.own(tag + "own"), net.sem(tag + "done")
    net.start()
    with nc.Block() as block:
        @block.gpsimd
        def _(pool):
            nc.gpsimd.memset(half[:], -0.5).then_inc(root, 1)
            pool.wait_ge(root, 1 + 1)
            pool.wait_ge(stats, 1 + 1)
            nc.gpsimd.tensor_scalar(var[:], mv[:, :, 1], EPS, None, ALU.add).then_inc(root, 1)
            pool.wait_ge(root, 1 + 2)
            nc.gpsimd.tensor_tensor(rstd[:], var[:], half[:], ALU.pow).then_inc(root, 1)
            if add:
                for i in range(NCH):
                    pool.wait_ge(done, 1 + i + 1)
                    to = target[:, i * TPC:(i + 1) * TPC, :]
                    nc.gpsimd.tensor_tensor(to, to, tmp[:, i % 2], ALU.add).then_inc(root, 1)

        @block.vector
        def _(dve):
            layer_norm_stats(nc, dve, [source[:, j, :] for j in range(NT)], st, mv, own, 0).then_inc(stats, 1)
            dve.wait_ge(root, 1 + 3)
            for i in range(NT):
                if add and i % TPC == 0 and i >= 2 * TPC:
                    dve.wait_ge(root, 1 + 3 + i // TPC - 1)
                to = tmp[:, i // TPC % 2, i % TPC, :] if add else target[:, i, :]
                last = nc.vector.tensor_scalar(to, source[:, i, :], mv[:, i, 0:1], rstd[:, i:i + 1],
                                               ALU.subtract, ALU.mult)
                if i % TPC == TPC - 1:
                    last.then_inc(done, 1)


def stream_in(net, xm):
    with ExitStack() as ctx:
        with net.nc.Block() as block:
            @block.gpsimd
            def _(pool):
                net.nc.gpsimd.memset(xm[:, 0:TM, :], 0.0)
                net.nc.gpsimd.memset(xm[:, TM + NT:, :], 0.0)
        normalise_all(net, ctx, "si_", net.x, xm[:, TM:TM + NT, :], False)


def stream_out(net, xm):
    with ExitStack() as ctx:
        normalise_all(net, ctx, "so_", xm[:, TM:TM + NT, :], net.x, True)


def moe_phase(net):
    nc, dram, x = net.nc, net.dram, net.x
    with ExitStack() as ctx:
        sb = lambda s, shape, dt=F32: net.sb(ctx, "e_" + s, shape, dt)
        w1, w2 = sb("w1", [P, 2, KD, HID]), sb("w2", [P, 2, KH, D])
        b1, b2 = sb("b1", [P, NE, KH]), sb("b2", [NE, D])
        wg, bg, rank = sb("wg", [P, KD, NE]), sb("bg", [P, NE]), sb("rank", [P, NE])
        st, mv, rstd = sb("st", [P, TPC, 6]), sb("mv", [P, TPC, 2]), sb("rstd", [P, TPC])
        xn, xT = sb("xn", [P, TPC, D]), sb("xT", [P, KD, CH])
        xT_all = sb("xT_all", [P, KD, N])
        acc = sb("acc", [P, NT, D])
        h = sb("h", [P, KH, CH])
        gate, one1, one2, tmp = (sb(s, [P, NT, NE]) for s in ("gate", "one1", "one2", "tmp"))
        top1, top2, col = (sb(s, [P, NT]) for s in ("top1", "top2", "col"))
        wgt = sb("wgt", [P, NT, NE])
        wc, wT = sb("wc", [P, TPC, NE]), sb("wT", [NE, CH])
        B = net.banks(ctx, "e_bank")
        names = ("loaded weights0 weights1 own_dve x_stats x_rstd xn_done xT_psum xT_done g_psum g_done logits exp_in exp_out "
                 "pair_in pair_out wgt_done wc_done wT_psum wT_done b_psum b_done h_psum h_done z_psum z_done "
                 "z_stats z_rstd setup").split()
        s = {n: (net.own if n in ("loaded", "weights0", "weights1", "own_dve") else net.sem)("e_" + n) for n in names}
        LOADS = 5 * 16
        over = lambda t: t[:].unsqueeze(2).broadcast_to([P, NT, NE])

        net.start()
        with nc.Block() as block:
            @block.sync
            def _(sp):
                for t, key in ((wg, "e_wg"), (b1, "e_b1"), (b2, "e_b2")):
                    sp.dma_start(t[:], dram[key]).then_inc(s["loaded"], 16)
                sp.dma_start(bg[:], dram["e_bg"].partition_broadcast(P)).then_inc(s["loaded"], 16)
                sp.dma_start(rank[:], dram["rank"].partition_broadcast(P)).then_inc(s["loaded"], 16)
                with sp.Fori(0, NE // 2) as e2:
                    for par in range(2):
                        sp.wait_ge(s["z_psum"], 1 + e2 * 2 * NT)
                        sp.dma_start(w1[:, par], dram["e_w1"][e2 * 2 + par]).then_inc(s[f"weights{par}"], 16)
                        sp.dma_start(w2[:, par], dram["e_w2"][e2 * 2 + par]).then_inc(s[f"weights{par}"], 16)

            @block.gpsimd
            def _(pool):
                nc.gpsimd.memset(wc[:], 0.0).then_inc(s["setup"], 1)
                with pool.Fori(0, 2 * NCH) as i:
                    pool.wait_ge(s["x_stats"], 1 + i + 1)
                    inverse_root(net, pool, rstd[:], mv[:, :, 1]).then_inc(s["x_rstd"], 1)

            @block.vector
            def _(dve):
                dve.wait_ge(s["loaded"], LOADS)
                with dve.Fori(0, NCH) as c:
                    dve.sem_clear(s["own_dve"])
                    tiles = [x[:, c * TPC + j, :] for j in range(TPC)]
                    layer_norm_stats(nc, dve, tiles, st, mv, s["own_dve"], 0).then_inc(s["x_stats"], 1)
                    dve.wait_ge(s["x_rstd"], 1 + c + 1)
                    for j in range(TPC):
                        nc.vector.tensor_scalar(xn[:, j, :], tiles[j], mv[:, j, 0:1], rstd[:, j:j + 1],
                                                ALU.subtract, ALU.mult).then_inc(s["xn_done"], 1)
                    dve.wait_ge(s["g_psum"], 1 + c + 1)
                    nc.vector.tensor_tensor(gate[:, bass.ts(c, TPC), :],
                                            B[2][:, 0:TPC * NE].rearrange("p (j e) -> p j e", e=NE),
                                            bg[:].unsqueeze(1).broadcast_to([P, TPC, NE]), ALU.add
                                            ).then_inc(s["g_done"], 1)
                dve.sem_clear(s["own_dve"])
                own = [0]

                def after(ins):
                    own[0] += 1
                    ins.then_inc(s["own_dve"], 1)
                    dve.wait_ge(s["own_dve"], own[0])

                V = nc.vector
                dve.wait_ge(s["g_done"], 1 + NCH)
                after(V.tensor_reduce(top1[:], gate[:], AX.X, ALU.max))
                V.tensor_tensor(gate[:], gate[:], over(top1), ALU.subtract).then_inc(s["exp_in"], 1)
                dve.wait_ge(s["exp_out"], 1 + 1)
                after(V.tensor_reduce(top1[:], gate[:], AX.X, ALU.add))
                after(V.reciprocal(top2[:], top1[:]))
                after(V.tensor_tensor(gate[:], gate[:], over(top2), ALU.mult))

                def pick(one, top):
                    after(V.tensor_reduce(top[:], gate[:], AX.X, ALU.max))
                    after(V.tensor_tensor(tmp[:], gate[:], over(top), ALU.is_equal))
                    after(V.tensor_tensor(tmp[:], tmp[:], rank[:].unsqueeze(1).broadcast_to([P, NT, NE]), ALU.mult))
                    after(V.tensor_reduce(col[:], tmp[:], AX.X, ALU.max))
                    after(V.tensor_tensor(one[:], tmp[:], over(col), ALU.is_equal))

                pick(one1, top1)
                after(V.scalar_tensor_tensor(gate[:], one1[:], -2.0, gate[:], ALU.mult, ALU.add))
                pick(one2, top2)
                V.tensor_tensor(top2[:], top2[:], top1[:], ALU.subtract).then_inc(s["pair_in"], 1)
                dve.wait_ge(s["pair_out"], 1 + 1)
                after(V.tensor_scalar(top1[:], top2[:], 1.0, None, ALU.add))
                after(V.reciprocal(col[:], top1[:]))
                after(V.tensor_tensor(top2[:], top2[:], col[:], ALU.mult))
                V.tensor_tensor(one1[:], one1[:], over(col), ALU.mult)
                after(V.tensor_tensor(one2[:], one2[:], over(top2), ALU.mult))
                V.tensor_tensor(wgt[:], one1[:], one2[:], ALU.add).then_inc(s["wgt_done"], 1)
                with dve.Fori(0, NCH) as c:
                    dve.wait_ge(s["wgt_done"], 1 + 1)
                    dve.wait_ge(s["wT_psum"], 1 + c)
                    V.tensor_copy(wc[:], wgt[:, bass.ts(c, TPC), :]).then_inc(s["wc_done"], 1)
                    for j in range(TPC):
                        dve.wait_ge(s["b_psum"], 1 + c * TPC + j + 1)
                        V.tensor_copy(acc[:, c * TPC + j, :], B[4 + j][:, 0:D]).then_inc(s["b_done"], 1)
                dve.wait_ge(s["b_done"], 1 + NT)
                with dve.Fori(0, NE) as e:
                    with dve.Fori(0, NCH) as c:
                        for j in range(TPC):
                            dve.wait_ge(s["z_psum"], 1 + e * NT + c * TPC + j + 1)
                            a = acc[:, c * TPC + j, :]
                            V.scalar_tensor_tensor(a, B[4 + j][:, 0:D], wgt[:, c * TPC + j, bass.ts(e, 1)], a,
                                                   ALU.mult, ALU.add).then_inc(s["z_done"], 1)
                dve.wait_ge(s["z_done"], 1 + NE * NT)
                with dve.Fori(0, NCH) as c:
                    dve.sem_clear(s["own_dve"])
                    tiles = [acc[:, c * TPC + j, :] for j in range(TPC)]
                    layer_norm_stats(nc, dve, tiles, st, mv, s["own_dve"], 0).then_inc(s["x_stats"], 1)
                    dve.wait_ge(s["x_rstd"], 1 + c + NCH + 1)
                    for j in range(TPC):
                        last = V.tensor_scalar(xn[:, j, :], tiles[j], mv[:, j, 0:1], rstd[:, j:j + 1],
                                               ALU.subtract, ALU.mult)
                    last.then_inc(s["own_dve"], 1)
                    dve.wait_ge(s["own_dve"], 2)
                    xc = x[:, bass.ts(c, TPC), :]
                    V.tensor_tensor(xc, xc, xn[:], ALU.add).then_inc(s["own_dve"], 1)
                    dve.wait_ge(s["own_dve"], 3)

            @block.scalar
            def _(act):
                act.wait_ge(s["loaded"], LOADS)
                with act.Fori(0, NCH) as c:
                    act.wait_ge(s["xT_psum"], 1 + c * TPC + TPC)
                    for k in range(KD):
                        nc.scalar.copy(xT[:, k, :], B[k][:]).then_inc(s["xT_done"], 1)
                    for k in range(KD):
                        nc.scalar.copy(xT_all[:, k, bass.ts(c, CH)], B[k][:]).then_inc(s["xT_done"], 1)
                act.wait_ge(s["exp_in"], 1 + 1)
                nc.scalar.activation(gate[:], gate[:], ACT.Exp).then_inc(s["exp_out"], 1)
                act.wait_ge(s["pair_in"], 1 + 1)
                nc.scalar.activation(top2[:], top2[:], ACT.Exp).then_inc(s["pair_out"], 1)
                with act.Fori(0, NCH) as c:
                    act.wait_ge(s["wT_psum"], 1 + c + 1)
                    nc.scalar.copy(wT[:], B[3][0:NE, :]).then_inc(s["wT_done"], 1)
                with act.Fori(0, NE) as e:
                    with act.Fori(0, NCH) as c:
                        for m in range(KH):
                            act.wait_ge(s["h_psum"], 1 + (e * NCH + c) * KH + m + 1)
                            act.sem_inc(net.carrier, 1)
                            nc.scalar.activation(h[:, m, :], B[m % 4][:], ACT.Relu, bias=b1[:, e, m:m + 1]
                                                 ).then_inc(s["h_done"], 1)

            @block.tensor
            def _(pe):
                pe.wait_ge(s["loaded"], LOADS)
                with pe.Fori(0, NCH) as c:
                    for j in range(TPC):
                        pe.wait_ge(s["xn_done"], 1 + c * TPC + j + 1)
                        pe.wait_ge(s["xT_done"], 1 + c * 2 * KD)
                        for k in range(KD):
                            last = nc.tensor.transpose(B[k][:, j * P:(j + 1) * P], xn[:, j, k * P:(k + 1) * P],
                                                       net.ident[:])
                        last.then_inc(s["xT_psum"], 1)
                    pe.wait_ge(s["xT_done"], 1 + c * 2 * KD + KD)
                    pe.wait_ge(s["g_done"], 1 + c)
                    for j in range(TPC):
                        for k in range(KD):
                            last = nc.tensor.matmul(B[2][:, j * NE:(j + 1) * NE], xT[:, k, j * P:(j + 1) * P], wg[:, k, :],
                                                    start=(k == 0), stop=(k == KD - 1))
                    last.then_inc(s["g_psum"], 1)
                with pe.Fori(0, NCH) as c:
                    pe.wait_ge(s["wc_done"], 1 + c + 1)
                    for j in range(TPC):
                        last = nc.tensor.transpose(B[3][0:NE, j * P:(j + 1) * P], wc[:, j, :], net.ident[:])
                    last.then_inc(s["wT_psum"], 1)
                    pe.wait_ge(s["wT_done"], 1 + c + 1)
                    for j in range(TPC):
                        pe.wait_ge(s["b_done"], 1 + c * TPC)
                        nc.tensor.matmul(B[4 + j][:, 0:D], wT[:, j * P:(j + 1) * P], b2[:], start=True, stop=True
                                         ).then_inc(s["b_psum"], 1)
                pe.wait_ge(s["b_done"], 1 + NT)
                pe.wait_ge(s["xT_done"], 1 + NCH * 2 * KD)
                with pe.Fori(0, NE // 2) as e2:
                    for par in range(2):
                        e = e2 * 2 + par
                        pe.wait_ge(s[f"weights{par}"], e2 * 32 + 32)
                        pe.sem_inc(net.carrier, 1)
                        with pe.Fori(0, NCH) as c:
                            for m in range(KH):
                                i = (e * NCH + c) * KH
                                pe.wait_ge(s["h_done"], 1 + (i + m - 3 if m >= 4 else i))
                                for k in range(KD):
                                    last = nc.tensor.matmul(B[m % 4][:], w1[:, par, k, m * P:(m + 1) * P],
                                                            xT_all[:, k, bass.ts(c, CH)],
                                                            start=(k == 0), stop=(k == KD - 1))
                                last.then_inc(s["h_psum"], 1)
                            pe.wait_ge(s["h_done"], 1 + (e * NCH + c) * KH + KH)
                            for j in range(TPC):
                                pe.wait_ge(s["z_done"], 1 + (e * NCH + c) * TPC)
                                for m in range(KH):
                                    last = nc.tensor.matmul(B[4 + j][:, 0:D], h[:, m, j * P:(j + 1) * P], w2[:, par, m, :],
                                                            start=(m == 0), stop=(m == KH - 1))
                                last.then_inc(s["z_psum"], 1)


def build(nc, dram, out, phases):
    with ExitStack() as ctx:
        net = Net(nc, ctx, dram, out)
        stored = ctx.enter_context(nc.semaphore("stored"))
        with nc.Block() as block:
            @block.gpsimd
            def _(pool):
                nc.gpsimd.memset(net.half[:], -0.5)
            @block.sync
            def _(sp):
                sp.dma_start(net.x[:], dram["x"].rearrange("(n p) d -> p n d", p=P)).then_inc(stored, 16)
                sp.dma_start(net.ident[:], dram["ident"]).then_inc(stored, 16)
                sp.wait_ge(stored, 32)
        for phase in phases:
            if phase is mamba_phases:
                phase(net)
            else:
                net.run(phase)
        with nc.Block() as block:
            @block.sync
            def _(sp):
                sp.dma_start(out.rearrange("(n p) d -> p n d", p=P), net.x[:]).then_inc(stored, 16)
                sp.wait_ge(stored, 48)


def layout(a):
    import numpy as np

    def rows(w):
        return np.ascontiguousarray(w.reshape(-1, P, w.shape[-1]).transpose(1, 0, 2))

    def col(v):
        return np.ascontiguousarray(v.reshape(-1, P).T)

    a = {k: np.asarray(v) for k, v in a.items()}
    t = np.arange(P)
    sub = np.arange(SUB)
    decay = np.zeros((KV, NS, SUB), np.float32)
    gap = sub[None, :] - sub[:, None]
    decay[:SUB] = np.where(gap >= 0, 0.6 ** np.maximum(gap, 0), 0.0)[:, None, :]
    for n in range(NS):
        decay[SUB + n, n] = 0.6 ** (sub + 1)
    d = {
        "x": a["L0_attn_x"][0],
        "ident": np.eye(P, dtype=np.float32),
        "causal": (t[:, None] <= t[None, :]).astype(np.float32),
        "head_rows": (t[:, None] // DH == np.arange(8)[None, :]).astype(np.float32),
        "wqkv": rows(np.concatenate([a["L0_attn_Wq"].T, a["L0_attn_Wk"].T, a["L0_attn_Wv"].T], axis=1)),
        "wo": rows(a["L0_attn_Wo"].T),
        "bo": a["L0_attn_bo"],
        "f_w1": rows(a["L0_ffn_W1"].T),
        "f_w2": rows(a["L0_ffn_W2"].T),
        "f_b1": col(a["L0_ffn_b1"]),
        "f_b2": a["L0_ffn_b2"],
        "f_scale": a["L0_ffn_scale"].reshape(1),
        "decay": decay,
    }
    for l in range(LAYERS):
        d |= {
            f"m{l}_norm": col(a["L1_attn_norm_w"][l]),
            f"m{l}_in": rows(a["L1_attn_in_proj_w"][l].T),
            f"m{l}_conv": rows(a["L1_attn_conv_w"][l]),
            f"m{l}_conv_b": col(a["L1_attn_conv_b"][l]),
            f"m{l}_xp": rows(a["L1_attn_x_proj_w"][l].T),
            f"m{l}_dt": np.ascontiguousarray(a["L1_attn_dt_w"][l].T),
            f"m{l}_dt_b": col(a["L1_attn_dt_b"][l]),
            f"m{l}_alog": rows(a["L1_attn_A_log"][l]),
            f"m{l}_skip": col(a["L1_attn_Dp"][l]),
            f"m{l}_out": rows(a["L1_attn_out_w"][l].T),
        }
    d |= {
        "e_w1": np.ascontiguousarray(a["L1_ffn_W1"].reshape(NE, KD, P, HID).transpose(0, 2, 1, 3)),
        "e_b1": np.ascontiguousarray(a["L1_ffn_b1"].reshape(NE, KH, P).transpose(2, 0, 1)),
        "e_w2": np.ascontiguousarray(a["L1_ffn_W2"].reshape(NE, KH, P, D).transpose(0, 2, 1, 3)),
        "e_b2": a["L1_ffn_b2"],
        "e_wg": rows(a["L1_ffn_Wg"]),
        "e_bg": a["L1_ffn_bg"],
        "rank": np.arange(NE, 0, -1).astype(np.float32),
    }
    return {k: np.ascontiguousarray(v) for k, v in d.items()}


PHASES = (attention_phase, ffn_phase, mamba_phases, moe_phase)


def kernel(**inputs):
    from concourse import bacc
    from concourse.bass_utils import run_bass_kernel_spmd

    arrays = layout(inputs)
    nc = bacc.Bacc("TRN2", target_bir_lowering=False, num_devices=1)
    dram = {name: nc.dram_tensor(f"in_{name}", a.shape, mybir.dt.from_np(a.dtype), kind="ExternalInput").ap()
            for name, a in arrays.items()}
    out = nc.dram_tensor("out_x", (N, D), F32, kind="ExternalOutput").ap()
    build(nc, dram, out, PHASES)
    r = run_bass_kernel_spmd(nc, [{f"in_{name}": a for name, a in arrays.items()}], core_ids=[0])
    return r.results[0]["out_x"].reshape(1, N, D)
```

```python
from contextlib import ExitStack

import concourse.bass as bass
from concourse import mybir

F32 = mybir.dt.float32
I32 = mybir.dt.int32
ALU = mybir.AluOpType
ACT = mybir.ActivationFunctionType
AX = mybir.AxisListType

P = 128
N = 4096
D = 256
KD = D // P
CH = 512
TPC = CH // P
NCH = N // CH
NT = N // P
EPS = 1e-5
HEADS = 16
DH = D // HEADS
VE = DH + 1
HID = 1024
KH = HID // P
LAYERS = 2
DI = 512
KI = DI // P
NS = 16
RANK = 16
TAPS = 4
SUB = 64
NSUB = CH // SUB
KV = SUB + NS
SMALL = 2.0 ** -6
NE = 8
SPARE = 2


class Net:

    def __init__(self, nc, ctx, dram, out):
        self.nc, self.ctx, self.dram, self.out = nc, ctx, dram, out
        self.x_all = self.sb(ctx, "x_res", [P, NT + 2 * SPARE, D])
        self.x = self.x_all[:, SPARE:SPARE + NT, :]
        self.ident = self.sb(ctx, "ident", [P, P])
        self.half = self.sb(ctx, "minus_half", [P, TPC])
        self.var = self.sb(ctx, "var_eps", [P, TPC])
        self.carrier = ctx.enter_context(nc.semaphore("carrier"))
        self.own_pool = ctx.enter_context(nc.semaphore("own_pool"))

    def sb(self, ctx, name, shape, dt=F32):
        return ctx.enter_context(self.nc.sbuf_tensor(name, shape, dt))

    def banks(self, ctx, name):
        return [ctx.enter_context(self.nc.psum_tensor(f"{name}{i}", [P, 512], F32)) for i in range(8)]

    def own(self, name):
        self.sems.append(self.phase_ctx.enter_context(self.nc.semaphore(name)))
        return self.sems[-1]

    def sem(self, name):
        self.counts.append(self.own(name))
        return self.counts[-1]

    def start(self):
        with self.nc.Block() as block:
            @block.sync
            def _(sp):
                for count in self.counts:
                    sp.sem_inc(count, 1)

    def run(self, phase):
        with ExitStack() as self.phase_ctx:
            self.sems, self.counts = [], []
            phase(self)
            with self.nc.Block() as block:
                @block.sync
                def _(sp):
                    for used in self.sems:
                        sp.sem_clear(used)


def inverse_root(net, pool, out, variance):
    w = out.shape[-1]
    pool.sem_inc(net.carrier, 1)
    pool.sem_clear(net.own_pool)
    net.nc.gpsimd.tensor_scalar(net.var[:, 0:w], variance, EPS, None, ALU.add).then_inc(net.own_pool, 1)
    pool.wait_ge(net.own_pool, 1)
    return net.nc.gpsimd.tensor_tensor(out, net.var[:, 0:w], net.half[:, 0:w], ALU.pow)


def layer_norm_stats(nc, dve, tiles, st, mv, own, n):
    for j, t in enumerate(tiles):
        last = nc.vector.bn_stats(st[:, j, :], t)
    last.then_inc(own, 1)
    dve.wait_ge(own, n + 1)
    for j in range(len(tiles)):
        last = nc.vector.bn_aggr(mv[:, j, :], st[:, j, :])
    return last


def attention_phase(net):
    nc, dram, x = net.nc, net.dram, net.x
    with ExitStack() as ctx:
        wqkv = net.sb(ctx, "wqkv", [P, KD, 3 * D])
        wo = net.sb(ctx, "wo", [P, KD, D])
        bo = net.sb(ctx, "bo", [P, D])
        causal = net.sb(ctx, "causal", [P, P])
        head_rows = net.sb(ctx, "head_rows", [P, HEADS // KD])
        st = net.sb(ctx, "a_st", [P, TPC, 6])
        mv = net.sb(ctx, "a_mv", [P, TPC, 2])
        rstd = net.sb(ctx, "a_rstd", [P, TPC])
        xn = net.sb(ctx, "a_xn", [P, TPC, D])
        xT = net.sb(ctx, "a_xT", [P, KD, CH])
        negs = net.sb(ctx, "a_negs", [P, 2, CH])
        exps = net.sb(ctx, "a_exps", [P, 2, CH])
        phi = net.sb(ctx, "a_phi", [P, 2 * KD, CH])
        qh = net.sb(ctx, "a_qh", [P, HEADS, CH])
        kt = net.sb(ctx, "a_kt", [P, 2, D])
        vt = net.sb(ctx, "a_vt", [P, 2, HEADS, VE])
        probs = net.sb(ctx, "a_probs", [P, 2, HEADS, P])
        state = net.sb(ctx, "a_state", [P, HEADS, VE])
        update = net.sb(ctx, "a_update", [P, HEADS, VE])
        den = net.sb(ctx, "a_den", [P, HEADS])
        rden = net.sb(ctx, "a_rden", [P, HEADS])
        att = net.sb(ctx, "a_att", [P, D])
        attT = net.sb(ctx, "a_attT", [P, KD, P])
        z = net.sb(ctx, "a_z", [P, TPC, D])
        zn = net.sb(ctx, "a_zn", [P, TPC, D])
        B = net.banks(ctx, "a_bank")
        HG = HEADS // 4
        DVE_HEADS, ACT_HEADS = 9, 13

        loaded = net.own("a_loaded")
        ones_set = net.sem("a_ones_set")
        own_dve, own_act = net.own("a_own_dve"), net.own("a_own_act")
        x_stats, x_rstd, xn_done = net.sem("a_x_stats"), net.sem("a_x_rstd"), net.sem("a_xn_done")
        xT_psum, xT_done = net.sem("a_xT_psum"), net.sem("a_xT_done")
        qk_psum, qk_exp, phi_done = net.sem("a_qk_psum"), net.sem("a_qk_exp"), net.sem("a_phi_done")
        qh_dve, qh_act, qh_pool = net.sem("a_qh_dve"), net.sem("a_qh_act"), net.sem("a_qh_pool")
        update_done = net.sem("a_update_done")
        kv_psum, v_done, kt_exp, kt_done = (net.sem("a_kv_psum"), net.sem("a_v_done"),
                                            net.sem("a_kt_exp"), net.sem("a_kt_done"))
        s_psum, probs_done = net.sem("a_s_psum"), net.sem("a_probs_done")
        o_psum, u_psum, state_done = net.sem("a_o_psum"), net.sem("a_u_psum"), net.sem("a_state_done")
        att_done, attT_psum, attT_done = net.sem("a_att_done"), net.sem("a_attT_psum"), net.sem("a_attT_done")
        z_psum, z_stats, z_rstd = net.sem("a_z_psum"), net.sem("a_z_stats"), net.sem("a_z_rstd")

        net.start()
        with nc.Block() as block:
            @block.sync
            def _(sp):
                sp.dma_start(wqkv[:], dram["wqkv"]).then_inc(loaded, 16)
                sp.dma_start(wo[:], dram["wo"]).then_inc(loaded, 16)
                sp.dma_start(bo[:], dram["bo"].partition_broadcast(P)).then_inc(loaded, 16)
                sp.dma_start(causal[:], dram["causal"]).then_inc(loaded, 16)
                sp.dma_start(head_rows[:], dram["head_rows"]).then_inc(loaded, 16)
            LOADS = 5 * 16

            @block.gpsimd
            def _(pool):
                pool.wait_ge(loaded, LOADS)

                def head(i):
                    pool.wait_ge(x_stats, 1 + i + 1)
                    inverse_root(net, pool, rstd[:], mv[:, :, 1]).then_inc(x_rstd, 1)

                def chunk(i, last_chunk):
                    pool.wait_ge(phi_done, 1 + i * 4 + 2)
                    pool.sem_inc(net.carrier, 1)
                    for h in range(ACT_HEADS, HEADS):
                        last = nc.gpsimd.tensor_scalar(qh[:, h, :], phi[:, 1, :],
                                                       head_rows[:, h % 8:h % 8 + 1], None, ALU.mult)
                    last.then_inc(qh_pool, 1)
                    if not last_chunk:
                        head(i + 1)
                    pool.wait_ge(z_stats, 1 + i + 1)
                    inverse_root(net, pool, rstd[:], mv[:, :, 1]).then_inc(z_rstd, 1)

                head(0)
                with pool.Fori(0, NCH - 1) as i:
                    chunk(i, False)
                chunk(NCH - 1, True)

            @block.vector
            def _(dve):
                nc.vector.memset(state[:], 0.0)
                nc.vector.memset(vt[:], 1.0).then_inc(ones_set, 1)
                dve.wait_ge(loaded, LOADS)

                def head(i, own):
                    tiles = [x[:, i * TPC + j, :] for j in range(TPC)]
                    layer_norm_stats(nc, dve, tiles, st, mv, own_dve, own).then_inc(x_stats, 1)
                    dve.wait_ge(x_rstd, 1 + i + 1)
                    dve.wait_ge(xT_psum, 1 + i * TPC)
                    for j in range(TPC):
                        nc.vector.tensor_scalar(xn[:, j, :], tiles[j], mv[:, j, 0:1], rstd[:, j:j + 1],
                                                ALU.subtract, ALU.mult).then_inc(xn_done, 1)

                def chunk(i, last_chunk):
                    dve.sem_clear(own_dve)
                    for g in range(4):
                        dve.wait_ge(qk_exp, 1 + i * 4 + g + 1)
                        nc.vector.scalar_tensor_tensor(phi[:, g, :], B[[2, 3, 0, 1][g]][:], 0.0, exps[:, g % 2, :],
                                                       ALU.max, ALU.add).then_inc(phi_done, 1)
                    dve.wait_ge(phi_done, 1 + i * 4 + 2)
                    for h in range(DVE_HEADS):
                        last = nc.vector.tensor_scalar(qh[:, h, :], phi[:, h // 8, :],
                                                       head_rows[:, h % 8:h % 8 + 1], None, ALU.mult)
                    last.then_inc(qh_dve, 1)
                    own = 0

                    def scores(j):
                        it = i * TPC + j
                        dve.wait_ge(kt_exp, 1 + it + 1)
                        nc.vector.scalar_tensor_tensor(kt[:, j % 2, :], B[4][:, 0:D], 0.0, exps[:, 0, 0:D],
                                                       ALU.max, ALU.add).then_inc(kt_done, 1)
                        for g in range(HG):
                            dve.wait_ge(s_psum, 1 + it * HG + g + 1)
                            nc.vector.tensor_tensor(
                                probs[:, j % 2, 4 * g:4 * g + 4, :], B[5 + g % 2][:].rearrange("p (h t) -> p h t", h=4),
                                causal[:].unsqueeze(1).broadcast_to([P, 4, P]), ALU.mult).then_inc(probs_done, 1)

                    scores(0)
                    for j in range(TPC):
                        it = i * TPC + j
                        o = B[7][:, 0:HEADS * VE].rearrange("p (h e) -> p h e", e=VE)
                        dve.wait_ge(o_psum, 1 + it + 1)
                        nc.vector.tensor_scalar(den[:], o[:, :, DH], EPS, None, ALU.add).then_inc(own_dve, 1)
                        dve.wait_ge(own_dve, own + 1)
                        nc.vector.reciprocal(rden[:], den[:]).then_inc(own_dve, 1)
                        dve.wait_ge(own_dve, own + 2)
                        own += 2
                        nc.vector.tensor_tensor(att[:].rearrange("p (h e) -> p h e", e=DH), o[:, :, 0:DH],
                                                rden[:].unsqueeze(2).broadcast_to([P, HEADS, DH]),
                                                ALU.mult).then_inc(att_done, 1)
                        dve.wait_ge(u_psum, 1 + it + 1)
                        own_rows = head_rows[:].unsqueeze(2).broadcast_to([P, HEADS // KD, VE])
                        for k in range(KD):
                            heads = slice(k * (HEADS // KD), (k + 1) * (HEADS // KD))
                            last = nc.vector.tensor_tensor(update[:, heads, :], B[0][:, 0:HEADS * VE].rearrange(
                                "p (h e) -> p h e", e=VE)[:, heads, :], own_rows, ALU.mult)
                        last.then_inc(update_done, 1)
                        dve.wait_ge(update_done, 1 + it + 1)
                        nc.vector.tensor_tensor(state[:], state[:], update[:], ALU.add).then_inc(state_done, 1)
                        if j < TPC - 1:
                            scores(j + 1)
                        if j == TPC - 2 and not last_chunk:
                            head(i + 1, own)
                            own += 1
                        dve.wait_ge(z_psum, 1 + it + 1)
                        last = nc.vector.tensor_tensor(z[:, j, :], B[2][:, 0:D], bo[:], ALU.add)
                    last.then_inc(own_dve, 1)
                    own += 1
                    dve.wait_ge(own_dve, own)
                    layer_norm_stats(nc, dve, [z[:, j, :] for j in range(TPC)], st, mv, own_dve, own
                                     ).then_inc(z_stats, 1)
                    own += 1
                    dve.wait_ge(z_rstd, 1 + i + 1)
                    for j in range(TPC):
                        last = nc.vector.tensor_scalar(zn[:, j, :], z[:, j, :], mv[:, j, 0:1], rstd[:, j:j + 1],
                                                       ALU.subtract, ALU.mult)
                    last.then_inc(own_dve, 1)
                    own += 1
                    dve.wait_ge(own_dve, own)
                    xc = x[:, bass.ts(i, TPC), :]
                    nc.vector.tensor_tensor(xc, xc, zn[:], ALU.add).then_inc(own_dve, 1)
                    dve.wait_ge(own_dve, own + 1)

                head(0, 0)
                with dve.Fori(0, NCH - 1) as i:
                    chunk(i, False)
                chunk(NCH - 1, True)

            @block.scalar
            def _(act):
                def head(i):
                    act.wait_ge(xT_psum, 1 + i * TPC + TPC)
                    for k in range(KD):
                        nc.scalar.copy(xT[:, k, :], B[3 + k][:]).then_inc(xT_done, 1)

                def chunk(i, last_chunk):
                    act.sem_clear(own_act)
                    own = 0
                    act.wait_ge(kt_done, 1 + i * TPC)
                    for g in range(4):
                        act.wait_ge(qk_psum, 1 + i * 4 + g + 1)
                        if g >= 2:
                            act.wait_ge(phi_done, 1 + i * 4 + g - 1)
                        nc.scalar.activation(negs[:, g % 2, :], B[[2, 3, 0, 1][g]][:], ACT.Relu,
                                             scale=-1.0).then_inc(own_act, 1)
                        own += 1
                        act.wait_ge(own_act, own)
                        nc.scalar.activation(exps[:, g % 2, :], negs[:, g % 2, :], ACT.Exp,
                                             scale=-1.0).then_inc(qk_exp, 1)
                    act.wait_ge(phi_done, 1 + i * 4 + 3)
                    act.sem_inc(net.carrier, 1)
                    for h in range(DVE_HEADS, ACT_HEADS):
                        last = nc.scalar.activation(qh[:, h, :], phi[:, 1, :], ACT.Copy,
                                                    scale=head_rows[:, h % 8:h % 8 + 1])
                    last.then_inc(qh_act, 1)

                    def keys_values(j, own):
                        it = i * TPC + j
                        act.wait_ge(kv_psum, 1 + it + 1)
                        if j >= 2:
                            act.wait_ge(u_psum, 1 + it - 1)
                        nc.scalar.copy(vt[:, j % 2, :, 0:DH], B[4][:, D:2 * D].rearrange("p (h e) -> p h e", e=DH)
                                       ).then_inc(v_done, 1)
                        nc.scalar.activation(negs[:, 0, 0:D], B[4][:, 0:D], ACT.Relu, scale=-1.0
                                             ).then_inc(own_act, 1)
                        act.wait_ge(own_act, own)
                        if j:
                            act.wait_ge(kt_done, 1 + it)
                        nc.scalar.activation(exps[:, 0, 0:D], negs[:, 0, 0:D], ACT.Exp, scale=-1.0
                                             ).then_inc(kt_exp, 1)

                    keys_values(0, own + 1)
                    for j in range(TPC):
                        it = i * TPC + j
                        if j < TPC - 1:
                            keys_values(j + 1, own + j + 2)
                        elif not last_chunk:
                            head(i + 1)
                        act.wait_ge(attT_psum, 1 + it + 1)
                        nc.scalar.copy(attT[:], B[1][:, 0:D].rearrange("p (k t) -> p k t", k=KD)
                                       ).then_inc(attT_done, 1)

                head(0)
                with act.Fori(0, NCH - 1) as i:
                    chunk(i, False)
                chunk(NCH - 1, True)

            @block.tensor
            def _(pe):
                pe.wait_ge(loaded, LOADS)

                def head(i):
                    for j in range(TPC):
                        pe.wait_ge(xn_done, 1 + i * TPC + j + 1)
                        for k in range(KD):
                            last = nc.tensor.transpose(B[3 + k][:, j * P:(j + 1) * P], xn[:, j, k * P:(k + 1) * P],
                                                       net.ident[:])
                        last.then_inc(xT_psum, 1)

                def chunk(i, last_chunk):
                    pe.wait_ge(xT_done, 1 + i * KD + KD)
                    pe.wait_ge(z_stats, 1 + i)
                    pe.wait_ge(state_done, 1 + i * TPC)
                    for g in range(4):
                        for k in range(KD):
                            last = nc.tensor.matmul(B[[2, 3, 0, 1][g]][:], wqkv[:, k, g * P:(g + 1) * P], xT[:, k, :],
                                                    start=(k == 0), stop=(k == KD - 1))
                        last.then_inc(qk_psum, 1)

                    def scores(j):
                        it = i * TPC + j
                        t = slice(j * P, (j + 1) * P)
                        pe.wait_ge(v_done, 1 + it)
                        pe.wait_ge(kt_done, 1 + it)
                        for k in range(KD):
                            last = nc.tensor.matmul(B[4][:], xT[:, k, t], wqkv[:, k, D:3 * D],
                                                    start=(k == 0), stop=(k == KD - 1))
                        last.then_inc(kv_psum, 1)
                        if j == 0:
                            pe.wait_ge(qh_dve, 1 + i + 1)
                            pe.wait_ge(qh_act, 1 + i + 1)
                            pe.wait_ge(qh_pool, 1 + i + 1)
                            pe.wait_ge(phi_done, 1 + i * 4 + 4)
                        for g in range(HG):
                            pe.wait_ge(probs_done, 1 + (it * HG + g - 1 if g >= 2 else it * HG))
                            nc.tensor.matmul(B[5 + g % 2][:].rearrange("p (h t) -> p h t", h=4),
                                             phi[:, KD + g // 2, t], qh[:, 4 * g:4 * g + 4, t], start=True, stop=True
                                             ).then_inc(s_psum, 1)

                    scores(0)
                    for j in range(TPC):
                        it = i * TPC + j
                        t = slice(j * P, (j + 1) * P)
                        w = HEADS // KD * VE
                        pe.wait_ge(state_done, 1 + it)
                        pe.wait_ge(att_done, 1 + it)
                        for k in range(KD):
                            nc.tensor.matmul(B[7][:, k * w:(k + 1) * w], phi[:, k, t], state[:, k * 8:(k + 1) * 8, :],
                                             start=True, stop=False)
                            if k == 0:
                                pe.wait_ge(probs_done, 1 + it * HG + HG)
                                pe.wait_ge(v_done, 1 + it + 1)
                            for h in range(k * 8, (k + 1) * 8):
                                last = nc.tensor.matmul(B[7][:, h * VE:(h + 1) * VE], probs[:, j % 2, h, :],
                                                        vt[:, j % 2, h, :], start=False, stop=(h % 8 == 7))
                        last.then_inc(o_psum, 1)
                        pe.wait_ge(kt_done, 1 + it + 1)
                        for k in range(KD):
                            last = nc.tensor.matmul(B[0][:, k * w:(k + 1) * w], kt[:, j % 2, k * P:(k + 1) * P],
                                                    vt[:, j % 2, k * 8:(k + 1) * 8, :], start=True, stop=True)
                        last.then_inc(u_psum, 1)
                        if j < TPC - 1:
                            scores(j + 1)
                        elif not last_chunk:
                            head(i + 1)
                        pe.wait_ge(att_done, 1 + it + 1)
                        for k in range(KD):
                            last = nc.tensor.transpose(B[1][:, k * P:(k + 1) * P], att[:, k * P:(k + 1) * P],
                                                       net.ident[:])
                        last.then_inc(attT_psum, 1)
                        pe.wait_ge(attT_done, 1 + it + 1)
                        for k in range(KD):
                            last = nc.tensor.matmul(B[2][:, 0:D], attT[:, k, :], wo[:, k, :],
                                                    start=(k == 0), stop=(k == KD - 1))
                        last.then_inc(z_psum, 1)

                head(0)
                with pe.Fori(0, NCH - 1) as i:
                    chunk(i, False)
                chunk(NCH - 1, True)





def ffn_phase(net):
    nc, dram, x = net.nc, net.dram, net.x
    RANK1 = 4
    with ExitStack() as ctx:
        w1 = net.sb(ctx, "f_w1", [P, KD, HID])
        w2 = net.sb(ctx, "f_w2", [P, KH, D])
        b1 = net.sb(ctx, "f_b1", [P, KH])
        b2 = net.sb(ctx, "f_b2", [P, D])
        scale = net.sb(ctx, "f_scale", [P, 1])
        tok = net.sb(ctx, "f_tok", [1, 4 * RANK1, D])
        st = net.sb(ctx, "f_st", [P, TPC, 6])
        mv = net.sb(ctx, "f_mv", [P, TPC, 2])
        rstd = net.sb(ctx, "f_rstd", [P, TPC])
        xn = net.sb(ctx, "f_xn", [P, TPC, D])
        xT = net.sb(ctx, "f_xT", [P, KD, CH])
        h = net.sb(ctx, "f_h", [P, KH, CH])
        z = net.sb(ctx, "f_z", [P, TPC, D])
        zn = net.sb(ctx, "f_zn", [P, TPC, D])
        B = net.banks(ctx, "f_bank")
        loaded, tok_done = net.own("f_loaded"), net.own("f_tok_done")
        own_dve = net.own("f_own_dve")
        first_stats, first_rstd, first_done = (net.sem("f_first_stats"), net.sem("f_first_rstd"),
                                               net.sem("f_first_done"))
        m1_psum, m2_psum, w_done = net.sem("f_m1_psum"), net.sem("f_m2_psum"), net.sem("f_w_done")
        x_stats, x_rstd, xn_done = net.sem("f_x_stats"), net.sem("f_x_rstd"), net.sem("f_xn_done")
        xT_psum, xT_done = net.sem("f_xT_psum"), net.sem("f_xT_done")
        h_psum, h_done = net.sem("f_h_psum"), net.sem("f_h_done")
        z_psum, z_done, z_stats, z_rstd = (net.sem("f_z_psum"), net.sem("f_z_done"), net.sem("f_z_stats"),
                                           net.sem("f_z_rstd"))
        LOADS = 5 * 16

        net.start()
        with nc.Block() as block:
            @block.sync
            def _(sp):
                sp.dma_start(w1[:], dram["f_w1"]).then_inc(loaded, 16)
                sp.dma_start(w2[:], dram["f_w2"]).then_inc(loaded, 16)
                sp.dma_start(b1[:], dram["f_b1"]).then_inc(loaded, 16)
                sp.dma_start(b2[:], dram["f_b2"].partition_broadcast(P)).then_inc(loaded, 16)
                sp.dma_start(scale[:], dram["f_scale"].partition_broadcast(P)).then_inc(loaded, 16)
                sp.wait_ge(first_done, 1 + 1)
                for r in range(4 * RANK1):
                    sp.dma_start(tok[:, r, :], xn[1 + r:2 + r, 0, :]).then_inc(tok_done, 16)

            @block.gpsimd
            def _(pool):
                pool.wait_ge(first_stats, 1 + 1)
                inverse_root(net, pool, rstd[:, 0:1], mv[:, 0:1, 1]).then_inc(first_rstd, 1)

                def head(i):
                    pool.wait_ge(x_stats, 1 + i + 1)
                    inverse_root(net, pool, rstd[:], mv[:, :, 1]).then_inc(x_rstd, 1)

                def tail(i):
                    pool.wait_ge(z_stats, 1 + i + 1)
                    inverse_root(net, pool, rstd[:], mv[:, :, 1]).then_inc(z_rstd, 1)

                head(0)
                with pool.Fori(0, NCH - 1) as i:
                    head(i + 1)
                    tail(i)
                tail(NCH - 1)

            @block.vector
            def _(dve):
                layer_norm_stats(nc, dve, [x[:, 0, :]], st, mv, own_dve, 0).then_inc(first_stats, 1)
                dve.wait_ge(first_rstd, 1 + 1)
                nc.vector.tensor_scalar(xn[:, 0, :], x[:, 0, :], mv[:, 0, 0:1], rstd[:, 0:1],
                                        ALU.subtract, ALU.mult).then_inc(first_done, 1)
                dve.wait_ge(loaded, LOADS)
                dve.wait_ge(m1_psum, 1 + 1)
                for k in range(KD):
                    for half in range(2):
                        w = w1[:, k, half * 512:(half + 1) * 512]
                        nc.vector.scalar_tensor_tensor(w, B[2 * k + half][:], scale[:, 0:1], w, ALU.mult, ALU.add)
                dve.wait_ge(m2_psum, 1 + 1)
                for q in range(4):
                    w = w2[:, 2 * q:2 * q + 2, :]
                    last = nc.vector.scalar_tensor_tensor(w, B[4 + q][:].rearrange("p (k o) -> p k o", k=2),
                                                          scale[:, 0:1], w, ALU.mult, ALU.add)
                last.then_inc(w_done, 1)
                dve.wait_ge(tok_done, 16 * 4 * RANK1)

                def head(i):
                    dve.sem_clear(own_dve)
                    tiles = [x[:, i * TPC + j, :] for j in range(TPC)]
                    layer_norm_stats(nc, dve, tiles, st, mv, own_dve, 0).then_inc(x_stats, 1)
                    dve.wait_ge(x_rstd, 1 + i + 1)
                    dve.wait_ge(xT_psum, 1 + i * TPC)
                    for j in range(TPC):
                        nc.vector.tensor_scalar(xn[:, j, :], tiles[j], mv[:, j, 0:1], rstd[:, j:j + 1],
                                                ALU.subtract, ALU.mult).then_inc(xn_done, 1)

                def tail(i):
                    dve.sem_clear(own_dve)
                    for j in range(TPC):
                        dve.wait_ge(z_psum, 1 + i * TPC + j + 1)
                        nc.vector.tensor_tensor(z[:, j, :], B[6 + j % 2][:, 0:D], b2[:], ALU.add
                                                ).then_inc(z_done, 1)
                    dve.wait_ge(z_done, 1 + i * TPC + TPC)
                    layer_norm_stats(nc, dve, [z[:, j, :] for j in range(TPC)], st, mv, own_dve, 0
                                     ).then_inc(z_stats, 1)
                    dve.wait_ge(z_rstd, 1 + i + 1)
                    for j in range(TPC):
                        last = nc.vector.tensor_scalar(zn[:, j, :], z[:, j, :], mv[:, j, 0:1], rstd[:, j:j + 1],
                                                       ALU.subtract, ALU.mult)
                    last.then_inc(own_dve, 1)
                    dve.wait_ge(own_dve, 2)
                    xc = x[:, bass.ts(i, TPC), :]
                    nc.vector.tensor_tensor(xc, xc, zn[:], ALU.add).then_inc(own_dve, 1)
                    dve.wait_ge(own_dve, 3)

                head(0)
                with dve.Fori(0, NCH - 1) as i:
                    head(i + 1)
                    tail(i)
                tail(NCH - 1)

            @block.scalar
            def _(act):
                act.wait_ge(loaded, LOADS)

                def head(i):
                    act.wait_ge(xT_psum, 1 + i * TPC + TPC)
                    for k in range(KD):
                        nc.scalar.copy(xT[:, k, :], B[k][:]).then_inc(xT_done, 1)

                def hidden(i):
                    for m in range(KH):
                        act.wait_ge(h_psum, 1 + i * KH + m + 1)
                        if m == 0:
                            act.wait_ge(z_psum, 1 + i * TPC)
                        nc.scalar.activation(h[:, m, :], B[2 + m % 4][:], ACT.Gelu, bias=b1[:, m:m + 1]
                                             ).then_inc(h_done, 1)

                head(0)
                with act.Fori(0, NCH - 1) as i:
                    hidden(i)
                    head(i + 1)
                hidden(NCH - 1)

            @block.tensor
            def _(pe):
                pe.wait_ge(tok_done, 16 * 4 * RANK1)
                for k in range(KD):
                    for i in range(RANK1):
                        last = nc.tensor.matmul(B[2 * k + i // 2][:, (i % 2) * D:(i % 2 + 1) * D],
                                                tok[0:1, 2 * i + 1, k * P:(k + 1) * P], tok[0:1, 2 * i, :],
                                                start=True, stop=True)
                last.then_inc(m1_psum, 1)
                for m in range(KH):
                    r, half = m // 2, m % 2
                    for i in range(RANK1):
                        col = (m % 2) * D + i * (D // 4)
                        last = nc.tensor.matmul(B[4 + m // 2][:, col:col + D // 4],
                                                tok[0:1, 2 * (RANK1 + i) + 1, half * P:(half + 1) * P],
                                                tok[0:1, 2 * (RANK1 + i), r:D:4], start=True, stop=True)
                last.then_inc(m2_psum, 1)
                pe.wait_ge(w_done, 1 + 1)

                def head(i):
                    for j in range(TPC):
                        pe.wait_ge(xn_done, 1 + i * TPC + j + 1)
                        for k in range(KD):
                            last = nc.tensor.transpose(B[k][:, j * P:(j + 1) * P], xn[:, j, k * P:(k + 1) * P],
                                                       net.ident[:])
                        last.then_inc(xT_psum, 1)

                def hidden(i):
                    pe.wait_ge(xT_done, 1 + i * KD + KD)
                    for m in range(KH):
                        pe.wait_ge(h_done, 1 + (i * KH + m - 3 if m >= 4 else i * KH))
                        for k in range(KD):
                            last = nc.tensor.matmul(B[2 + m % 4][:], w1[:, k, m * P:(m + 1) * P], xT[:, k, :],
                                                    start=(k == 0), stop=(k == KD - 1))
                        last.then_inc(h_psum, 1)

                def result(i):
                    pe.wait_ge(h_done, 1 + i * KH + KH)
                    for j in range(TPC):
                        pe.wait_ge(z_done, 1 + (i * TPC + j - 1 if j >= 2 else i * TPC))
                        for m in range(KH):
                            last = nc.tensor.matmul(B[6 + j % 2][:, 0:D], h[:, m, j * P:(j + 1) * P], w2[:, m, :],
                                                    start=(m == 0), stop=(m == KH - 1))
                        last.then_inc(z_psum, 1)

                head(0)
                with pe.Fori(0, NCH - 1) as i:
                    hidden(i)
                    head(i + 1)
                    result(i)
                hidden(NCH - 1)
                result(NCH - 1)


BF16 = mybir.dt.bfloat16
CM = 256
TM = CM // P
assert TM == SPARE
NCM = N // CM
NSUB = CM // SUB
BETA = 0.6
LAG = 2


def mamba_phase(net, layer, xm):
    nc = net.nc
    dram = net.dram
    nm = lambda t: f"m{layer}_{t}"
    with ExitStack() as ctx:
        sb = lambda t, shape, dt=F32: net.sb(ctx, nm(t), shape, dt)
        norm, w_in, conv, conv_b = sb("norm", [P, KD]), sb("in", [P, KD, 2 * DI]), sb("conv", [P, KI, TAPS]), sb("cb", [P, KI])
        w_xp, dt_b = sb("xp", [P, KI, RANK + 2 * NS]), sb("dtb", [P, KI])
        shared = sb("shared", [KV, DI])
        w_dt, v_end = shared[0:RANK, :], shared[32:32 + NS, :]
        vhi, vlo = (shared[SUB:KV, :].bitcast(BF16)[:, i * DI:(i + 1) * DI] for i in range(2))
        rate, skip, w_out = sb("rate", [P, KI, NS]), sb("skip", [P, KI]), sb("out", [P, KI, D])
        decay = sb("decay", [SUB, SUB])
        st, mv, rstd, msq = sb("st", [P, TM, 6]), sb("mv", [P, TM, 2]), sb("rstd", [P, TM]), sb("msq", [P, TM])
        xb, zs, delta = (sb(t, [P, 2, KI, CM]) for t in ("xb", "zs", "delta"))
        xpre = sb("xpre", [P, KI, TAPS - 1 + CM])
        cv = sb("cv", [P, KI, CM])
        u = sb("u", [P, KI, CM])
        pair = sb("pair", [P, 2, KD, CM])
        mask = sb("mask", [P, KI, CM], mybir.dt.uint8)
        xp = u[0:RANK + 2 * NS, 0, :]
        low = xp[0:RANK]
        v_mid = u[0:NS].rearrange("n (a k) t -> n a (k t)", a=2)
        Bs, Cs = sb("Bs", [SUB, NSUB, NS]), sb("Cs", [P, 2, TM, NS])
        Mf = sb("Mf", [KV, NS, SUB])
        Mhi, Mlo = sb("Mhi", [KV, 2, NSUB, NS, SUB], BF16), sb("Mlo", [KV, 2, NSUB, NS, SUB], BF16)
        Uhi, Ulo = sb("Uhi", [KV, 2, NSUB, DI], BF16), sb("Ulo", [KV, 2, NSUB, DI], BF16)
        dA = sb("dA", [P, 3, KI, CM])
        h = sb("h", [P, 3, KI, CM])
        hlast = sb("hlast", [P, NS, KI])
        y = sb("y", [P, 2, TM, DI])
        prod = sb("prod", [P, 2, DI])
        xr = pair[:, 0].rearrange("p k t -> p (k t)").rearrange("p (j d) -> p j d", d=D)
        xT = pair[:, 1]
        series = pair[:].rearrange("p a k t -> p (a k) t")
        decay_n = decay[:].unsqueeze(1).broadcast_to([SUB, NS, SUB])
        banks = net.banks(ctx, nm("bank"))
        VB, HB, H0, H1 = banks[0:4], banks[4:6], banks[6], banks[7]
        names = ("loaded own_dve own_act own_pool setup rms_in rms_out xr_done xT_psum xT_done in_psum pre_done "
                 "z_done conv_done xb_done bc_psum xp_psum xp_done dt_psum dt_done exp_done ln_done "
                 "mask_done u_done delta_done uT_psum uhi_done ulo_done "
                 "mf_done mhi_done mlo_done halo_done before_done carry_psum carry_done vhi_done vlo_done v_psum da_done scan_done "
                 "hlast_done ht_psum prod_done y_dve y_pool yT_psum gated_done out_psum xm_done rate_done const_done"
                 ).split()
        s = {n: (net.own if n == "loaded" or "own" in n else net.sem)(nm(n)) for n in names}
        LOADS = 12 * 16
        net.start()
        with nc.Block() as block:
            @block.sync
            def _(sp):
                for t, key in ((norm, "norm"), (w_in, "in"), (conv, "conv"), (conv_b, "conv_b"), (w_xp, "xp"),
                               (shared, "dt"), (dt_b, "dt_b"), (rate, "alog"), (skip, "skip"), (w_out, "out")):
                    sp.dma_start(t[:] if key != "dt" else w_dt, dram[f"m{layer}_{key}"]).then_inc(s["loaded"], 16)
                sp.dma_start(decay[:], dram["decay"][0:SUB, 0]).then_inc(s["loaded"], 16)
                sp.dma_start(Mf[SUB:KV], dram["decay"][SUB:KV]).then_inc(s["loaded"], 16)

            @block.gpsimd
            def _(pool):
                nc.gpsimd.memset(xpre[:], 0.0)
                nc.gpsimd.memset(hlast[:], 0.0)
                for t in (y, xb, zs):
                    last = nc.gpsimd.memset(t[:, 1], 0.0)
                last.then_inc(s["setup"], 1)
                pool.wait_ge(s["setup"], 1 + 1)
                pool.wait_ge(s["loaded"], LOADS)

                def head(q, par, slot):
                    if slot == 1:
                        pool.wait_ge(s["rms_in"], 1 + q + 1)
                        inverse_root(net, pool, rstd[:], msq[:]).then_inc(s["rms_out"], 1)
                    if slot == 3:
                        pool.wait_ge(s["conv_done"], 1 + q * KI)
                        pool.sem_inc(net.carrier, 1)
                        nc.gpsimd.tensor_copy(xpre[:, :, 0:TAPS - 1], xpre[:, :, CM:CM + TAPS - 1]
                                              ).then_inc(s["halo_done"], 1)
                    if slot == 11:
                        pool.wait_ge(s["exp_done"], 1 + q + 1)
                        pool.sem_inc(net.carrier, 1)
                        nc.gpsimd.tensor_scalar(mask[:], cv[:], SMALL, None, ALU.is_lt).then_inc(s["mask_done"], 1)
                    if slot in (12, 13, 14, 15):
                        j = (12, 13, 14, 15).index(slot)
                        pool.wait_ge(s["mhi_done"], 1 + q * NSUB + j + 1)
                        nc.gpsimd.tensor_tensor(Mlo[0:SUB, par, j], Mf[0:SUB], Mhi[0:SUB, par, j], ALU.subtract
                                                ).then_inc(s["mlo_done"], 1)
                    if slot in (10, 12, 13, 14):
                        j = (10, 12, 13, 14).index(slot)
                        pool.wait_ge(s["xp_done"], 1 + q * 3 + 2)
                        pool.wait_ge(s["mlo_done"], 1 + q * NSUB + j)
                        nc.gpsimd.tensor_tensor(Mf[0:SUB], decay_n, Bs[:, j, :].unsqueeze(2).broadcast_to(
                            [SUB, NS, SUB]), ALU.mult).then_inc(s["mf_done"], 1)

                def slots(c, par):
                    for n in range(NS + LAG):
                        if n < NS:
                            pool.wait_ge(s["scan_done"], 1 + (c * NS + n + 1) * KI)
                            pool.sem_inc(net.carrier, 1)
                            nc.gpsimd.tensor_copy(hlast[:, n, :], h[:, n % 3, :, CM - 1]).then_inc(s["hlast_done"], 1)
                        if n >= LAG:
                            k = c * NS + n - LAG
                            out = y[:, par, 1, :]
                            pool.wait_ge(s["y_pool"], 1 + k)
                            pool.wait_ge(s["prod_done"], 1 + k + 1)
                            if n == LAG:
                                pool.sem_inc(net.carrier, 1)
                                nc.gpsimd.tensor_copy(out, prod[:, n % 2, :]).then_inc(s["y_pool"], 1)
                            else:
                                nc.gpsimd.tensor_tensor(out, out, prod[:, n % 2, :], ALU.add).then_inc(s["y_pool"], 1)
                        head(c + 1, 1 - par, n)

                for slot in range(NS + LAG):
                    head(0, 0, slot)
                with pool.Fori(0, NCM // 2) as c2:
                    slots(c2 * 2, 0)
                    slots(c2 * 2 + 1, 1)

            @block.vector
            def _(dve):
                dve.wait_ge(s["loaded"], LOADS)
                dve.wait_ge(s["setup"], 1 + 1)
                nc.vector.memset(vhi, 0.0)
                nc.vector.memset(vlo, 0.0)
                nc.vector.memset(v_end, 0.0)
                for par in range(2):
                    for j in range(NSUB):
                        V = nc.vector.tensor_copy(Mhi[SUB:KV, par, j], Mf[SUB:KV])
                V.then_inc(s["const_done"], 1)
                dve.wait_ge(s["const_done"], 1 + 1)
                for par in range(2):
                    for j in range(NSUB):
                        V = nc.vector.tensor_tensor(Mlo[SUB:KV, par, j], Mf[SUB:KV], Mhi[SUB:KV, par, j], ALU.subtract)
                V.then_inc(s["const_done"], 1)
                own = [0]

                def after(ins):
                    own[0] += 1
                    ins.then_inc(s["own_dve"], 1)
                    dve.wait_ge(s["own_dve"], own[0])

                def restart():
                    dve.sem_clear(s["own_dve"])
                    own[0] = 0

                def head(q, par, slot):
                    tiles = [xm[:, (q + 1) * TM + j, :] for j in range(TM)]
                    if slot == 0:
                        after(layer_norm_stats(nc, dve, tiles, st, mv, s["own_dve"], own[0]))
                        own[0] += 1
                        dve.wait_ge(s["own_dve"], own[0])
                        after(nc.vector.tensor_tensor(msq[:], mv[:, :, 0], mv[:, :, 0], ALU.mult))
                        nc.vector.tensor_tensor(msq[:], msq[:], mv[:, :, 1], ALU.add).then_inc(s["rms_in"], 1)
                    if slot == 2:
                        dve.wait_ge(s["rms_out"], 1 + q + 1)
                        for j in range(TM):
                            nc.vector.tensor_scalar(xr[:, j, :], tiles[j], rstd[:, j:j + 1], None, ALU.mult
                                                    ).then_inc(s["xr_done"], 1)
                    for m in {6: (0,), 7: (1, 2), 8: (3,)}.get(slot, ()):
                        dve.wait_ge(s["pre_done"], 1 + q * 2 + m // 2 + 1)
                        dve.wait_ge(s["halo_done"], 1 + q + 1)
                        after(nc.vector.tensor_scalar(cv[:, m, :], xpre[:, m, 0:CM], conv[:, m, 0:1], None, ALU.mult))
                        for k in range(1, TAPS):
                            i = nc.vector.scalar_tensor_tensor(cv[:, m, :], xpre[:, m, k:k + CM], conv[:, m, k:k + 1],
                                                               cv[:, m, :], ALU.mult, ALU.add)
                            if k < TAPS - 1:
                                after(i)
                        i.then_inc(s["conv_done"], 1)
                    if slot == 9:
                        dve.wait_ge(s["vlo_done"], 1 + q * NSUB)
                        nc.vector.tensor_copy(Uhi[SUB:KV, par, 0, :], vhi)
                        nc.vector.tensor_copy(Ulo[SUB:KV, par, 0, :], vlo).then_inc(s["before_done"], 1)
                    if slot in (12, 13, 14, 15):
                        j = (12, 13, 14, 15).index(slot)
                        dve.wait_ge(s["mf_done"], 1 + q * NSUB + j + 1)
                        nc.vector.tensor_copy(Mhi[0:SUB, par, j], Mf[0:SUB]).then_inc(s["mhi_done"], 1)
                    if slot == 12:
                        dve.wait_ge(s["exp_done"], 1 + q + 1)
                        after(nc.vector.tensor_scalar(series, cv[:], -0.25, 1 / 3, ALU.mult, ALU.add))
                        after(nc.vector.tensor_tensor(series, series, cv[:], ALU.mult))
                        after(nc.vector.scalar_tensor_tensor(series, series, -0.5, cv[:], ALU.add, ALU.mult))
                        after(nc.vector.scalar_tensor_tensor(series, series, 1.0, cv[:], ALU.add, ALU.mult))
                    if slot == 13:
                        dve.wait_ge(s["ln_done"], 1 + q + 1)
                        dve.wait_ge(s["mask_done"], 1 + q + 1)
                        dve.sem_inc(net.carrier, 1)
                        after(nc.vector.copy_predicated(u[:], mask[:], series))
                        nc.vector.tensor_tensor(delta[:, par], delta[:, par], u[:], ALU.add).then_inc(s["delta_done"], 1)
                        dve.wait_ge(s["delta_done"], 1 + q + 1)
                        nc.vector.tensor_tensor(u[:], delta[:, par], xb[:, par], ALU.mult).then_inc(s["u_done"], 1)
                    if slot in (15, 16):
                        for j in ((0, 1) if slot == 15 else (2, 3)):
                            dve.wait_ge(s["uhi_done"], 1 + q * NSUB + j + 1)
                            nc.vector.tensor_tensor(Ulo[0:SUB, par, j, :], (H0, H1)[j % 2][0:SUB, :],
                                                    Uhi[0:SUB, par, j, :], ALU.subtract).then_inc(s["ulo_done"], 1)
                    if slot == 16:
                        for i in (0, 1, -1, 2, -2, 3, -3, -4):
                            last = i in (NSUB - 1, -NSUB)
                            if i >= 0:
                                before = v_end if i == 0 else v_mid[:, (i - 1) % 2, :]
                                new = v_end if last else v_mid[:, i % 2, :]
                                dve.wait_ge(s["carry_psum"], 1 + q * NSUB + i + 1)
                                dve.wait_ge(s["carry_done"], 1 + q * NSUB + i)
                                if i >= 2:
                                    dve.wait_ge(s["vlo_done"], 1 + q * NSUB + i - 1)
                                nc.vector.scalar_tensor_tensor(new, before, BETA ** SUB, (H0, H1)[i % 2][0:NS, :],
                                                               ALU.mult, ALU.add).then_inc(s["carry_done"], 1)
                            else:
                                j = -1 - i
                                hi = vhi if last else Uhi[SUB:KV, par, j + 1, :]
                                lo = vlo if last else Ulo[SUB:KV, par, j + 1, :]
                                dve.wait_ge(s["vhi_done"], 1 + q * NSUB + j + 1)
                                nc.vector.tensor_tensor(lo, v_end if last else v_mid[:, j % 2, :], hi,
                                                        ALU.subtract).then_inc(s["vlo_done"], 1)

                def tail(t, par, slot):
                    if slot == 1:
                        for m in range(KI):
                            dve.wait_ge(s["yT_psum"], 1 + t * 2 + m // 2 + 1)
                            g = u[:, m, :]
                            after(nc.vector.scalar_tensor_tensor(g, xb[:, par, m, :], skip[:, m:m + 1],
                                                                 (H0, H1)[m // 2][:, m % 2 * CM:(m % 2 + 1) * CM],
                                                                 ALU.mult, ALU.add))
                            nc.vector.tensor_tensor(g, g, zs[:, par, m, :], ALU.mult).then_inc(s["gated_done"], 1)
                    if slot == 4:
                        dve.wait_ge(s["out_psum"], 1 + t + 1)
                        to = xm[:, bass.ts(t, TM), :]
                        nc.vector.tensor_tensor(to, to, H1[:].rearrange("p (j d) -> p j d", d=D), ALU.add
                                                ).then_inc(s["xm_done"], 1)

                def slots(c, par):
                    restart()
                    for n in range(NS + LAG):
                        if n < NS:
                            if n == 0:
                                dve.wait_ge(s["hlast_done"], 1 + c * NS)
                                dve.wait_ge(s["ht_psum"], 1 + c * NS * 2)
                            if n >= 3:
                                dve.wait_ge(s["hlast_done"], 1 + c * NS + n - 2)
                                dve.wait_ge(s["ht_psum"], 1 + (c * NS + n - 2) * 2)
                            for m in range(KI):
                                dve.wait_ge(s["v_psum"], 1 + (c * NS + n) * 2 + m // 2 + 1)
                                dve.wait_ge(s["da_done"], 1 + (c * NS + n) * KI + m + 1)
                                nc.vector.tensor_tensor_scan(
                                    h[:, n % 3, m, :], dA[:, n % 3, m, :],
                                    VB[(n % 2) * 2 + m // 2][:, (m % 2) * CM:(m % 2 + 1) * CM],
                                    hlast[:, n, m:m + 1], ALU.mult, ALU.add).then_inc(s["scan_done"], 1)
                        if n >= LAG:
                            k = c * NS + n - LAG
                            out = y[:, par, 0, :]
                            dve.wait_ge(s["ht_psum"], 1 + k * 2 + 2)
                            C = Cs[:, par, 0, n - LAG:n - LAG + 1]
                            if n == LAG:
                                nc.vector.tensor_scalar(out, HB[0][:], C, None, ALU.mult).then_inc(s["y_dve"], 1)
                            else:
                                dve.wait_ge(s["y_dve"], 1 + k)
                                nc.vector.scalar_tensor_tensor(out, HB[0][:], C, out, ALU.mult, ALU.add
                                                               ).then_inc(s["y_dve"], 1)
                        tail(c, 1 - par, n)
                        head(c + 1, 1 - par, n)

                restart()
                for slot in range(NS + LAG):
                    head(0, 0, slot)
                with dve.Fori(0, NCM // 2) as c2:
                    slots(c2 * 2, 0)
                    slots(c2 * 2 + 1, 1)
                restart()
                for slot in range(5):
                    tail(NCM, 1, slot)

            @block.scalar
            def _(act):
                act.wait_ge(s["loaded"], LOADS)
                nc.scalar.activation(rate[:], rate[:], ACT.Exp).then_inc(s["rate_done"], 1)
                act.wait_ge(s["rate_done"], 1 + 1)
                nc.scalar.mul(rate[:], rate[:], -1.0).then_inc(s["rate_done"], 1)
                act.wait_ge(s["rate_done"], 1 + 2)
                act.wait_ge(s["setup"], 1 + 1)
                halves = lambda bank: bank[:].rearrange("p (k t) -> p k t", k=2)

                def head(q, par, slot):
                    if slot == 4:
                        act.wait_ge(s["xT_psum"], 1 + q + 1)
                        for k in range(KD):
                            nc.scalar.activation(xT[:, k, :], halves(H0)[:, k, :], ACT.Copy, scale=norm[:, k:k + 1]
                                                 ).then_inc(s["xT_done"], 1)
                    if slot == 5:
                        act.wait_ge(s["halo_done"], 1 + q + 1)
                        for g in range(2):
                            act.wait_ge(s["in_psum"], 1 + q * 4 + g + 1)
                            nc.scalar.copy(xpre[:, 2 * g:2 * g + 2, TAPS - 1:], halves((H1, H0)[g])
                                           ).then_inc(s["pre_done"], 1)
                    if slot == 7:
                        for g in range(2):
                            act.wait_ge(s["in_psum"], 1 + q * 4 + g + 3)
                            if g == 0:
                                act.wait_ge(s["conv_done"], 1 + q * KI + 1)
                            nc.scalar.activation(zs[:, par, 2 * g:2 * g + 2, :], halves((H1, H0)[g]), ACT.Silu
                                                 ).then_inc(s["z_done"], 1)
                    if slot == 8:
                        for m in range(KI):
                            act.wait_ge(s["conv_done"], 1 + q * KI + m + 1)
                            nc.scalar.activation(xb[:, par, m, :], cv[:, m, :], ACT.Silu, bias=conv_b[:, m:m + 1]
                                                 ).then_inc(s["xb_done"], 1)
                    if slot == 9:
                        act.wait_ge(s["xp_psum"], 1 + q + 1)
                        nc.scalar.copy(xp, H1[0:RANK + 2 * NS, 0:CM]).then_inc(s["xp_done"], 1)
                    if slot == 10:
                        act.wait_ge(s["bc_psum"], 1 + q + 1)
                        nc.scalar.copy(Bs[:], H1[0:SUB, CM:CM + NSUB * NS].rearrange("p (a n) -> p a n", n=NS)
                                       ).then_inc(s["xp_done"], 1)
                        nc.scalar.copy(Cs[:, par], H1[:, CM + 64:CM + 64 + TM * NS].rearrange("p (a n) -> p a n", n=NS)
                                       ).then_inc(s["xp_done"], 1)
                    if slot in (10, 11):
                        for m in ((0, 1) if slot == 10 else (2, 3)):
                            act.wait_ge(s["dt_psum"], 1 + q * 2 + m // 2 + 1)
                            v = halves((H0, H1)[m // 2])[:, m % 2, :]
                            nc.scalar.activation(delta[:, par, m, :], v, ACT.Relu, bias=dt_b[:, m:m + 1])
                            nc.scalar.activation(cv[:, m, :], v, ACT.Abs, bias=dt_b[:, m:m + 1]
                                                 ).then_inc(s["dt_done"], 1)
                    if slot == 11:
                        act.wait_ge(s["dt_done"], 1 + q * KI + KI)
                        nc.scalar.activation(cv[:], cv[:], ACT.Exp, scale=-1.0).then_inc(s["exp_done"], 1)
                    if slot == 12:
                        act.wait_ge(s["exp_done"], 1 + q + 1)
                        nc.scalar.activation(u[:], cv[:], ACT.Ln, bias=1.0).then_inc(s["ln_done"], 1)
                    if slot in (14, 15):
                        for j in ((0, 1) if slot == 14 else (2, 3)):
                            act.wait_ge(s["uT_psum"], 1 + q * NSUB + j + 1)
                            nc.scalar.copy(Uhi[0:SUB, par, j, :], (H0, H1)[j % 2][0:SUB, :]).then_inc(s["uhi_done"], 1)
                    if slot == 16:
                        for j in range(NSUB):
                            last = j == NSUB - 1
                            act.wait_ge(s["carry_done"], 1 + q * NSUB + j + 1)
                            nc.scalar.copy(vhi if last else Uhi[SUB:KV, par, j + 1, :],
                                           v_end if last else v_mid[:, j % 2, :]).then_inc(s["vhi_done"], 1)

                def decays(c, par, n, first=False):
                    if n == 0:
                        act.wait_ge(s["delta_done"], 1 + c + 1)
                    for m in range(KI):
                        if n == 0 and not first and m == 0:
                            act.wait_ge(s["scan_done"], 1 + c * NS * KI)
                        if n >= 3:
                            act.wait_ge(s["scan_done"], 1 + (c * NS + n - 3) * KI + m + 1)
                        act.sem_inc(net.carrier, 1)
                        nc.scalar.activation(dA[:, n % 3, m, :], delta[:, par, m, :], ACT.Exp,
                                             scale=rate[:, m, n:n + 1]).then_inc(s["da_done"], 1)

                def slots(c, par):
                    for n in range(NS + LAG):
                        if n >= LAG:
                            k = c * NS + n - LAG
                            act.wait_ge(s["ht_psum"], 1 + k * 2 + 1)
                            act.wait_ge(s["y_pool"], 1 + (k - 1 if n > LAG else k))
                            nc.scalar.activation(prod[:, n % 2, :], HB[1][:], ACT.Copy,
                                                 scale=Cs[:, par, 1, n - LAG:n - LAG + 1]).then_inc(s["prod_done"], 1)
                        if n < NS - 2:
                            decays(c, par, n + 2)
                        if n >= NS:
                            decays(c + 1, 1 - par, n - NS)
                        head(c + 1, 1 - par, n)

                for slot in range(NS + LAG):
                    head(0, 0, slot)
                decays(0, 0, 0, True)
                decays(0, 0, 1)
                with act.Fori(0, NCM // 2) as c2:
                    slots(c2 * 2, 0)
                    slots(c2 * 2 + 1, 1)

            @block.tensor
            def _(pe):
                pe.wait_ge(s["loaded"], LOADS)
                pe.wait_ge(s["setup"], 1 + 1)
                pe.wait_ge(s["const_done"], 1 + 2)
                PARTS = ((Mlo, Uhi), (Mhi, Ulo), (Mhi, Uhi))

                def head(q, par, slot):
                    if slot == 4:
                        pe.wait_ge(s["xr_done"], 1 + q * TM + TM)
                        pe.wait_ge(s["gated_done"], 1 + q * KI)
                        for j in range(TM):
                            for k in range(KD):
                                last = nc.tensor.transpose(H0[:, k * CM + j * P:k * CM + (j + 1) * P],
                                                           xr[:, j, k * P:(k + 1) * P], net.ident[:])
                        last.then_inc(s["xT_psum"], 1)
                    if slot in (5, 6):
                        if slot == 5:
                            pe.wait_ge(s["xT_done"], 1 + q * KD + KD)
                        for g in ((0, 1) if slot == 5 else (2, 3)):
                            bank = (H1, H0)[g % 2]
                            if g == 0:
                                pe.wait_ge(s["xm_done"], 1 + q)
                            if g >= 2:
                                pe.wait_ge(s["pre_done"], 1 + q * 2 + g - 1)
                            for half in range(2):
                                m = 2 * g + half
                                for k in range(KD):
                                    last = nc.tensor.matmul(bank[:, half * CM:(half + 1) * CM],
                                                            w_in[:, k, m * P:(m + 1) * P], xT[:, k, :],
                                                            start=(k == 0), stop=(k == KD - 1))
                            last.then_inc(s["in_psum"], 1)
                    if slot == 9:
                        pe.wait_ge(s["xb_done"], 1 + q * KI + KI)
                        for k in range(KI):
                            last = nc.tensor.matmul(H1[0:RANK + 2 * NS, 0:CM], w_xp[:, k, :], xb[:, par, k, :],
                                                    start=(k == 0), stop=(k == KI - 1))
                        last.then_inc(s["xp_psum"], 1)
                    if slot == 10:
                        pe.wait_ge(s["xp_done"], 1 + q * 3 + 1)
                        pe.sem_inc(net.carrier, 1)
                        for j in range(NSUB):
                            nc.tensor.matmul(H1[0:SUB, CM + j * NS:CM + (j + 1) * NS], xp[:, j * SUB:(j + 1) * SUB],
                                             net.ident[0:RANK + 2 * NS, RANK:RANK + NS], start=True, stop=True)
                        for j in range(TM):
                            last = nc.tensor.matmul(H1[:, CM + 64 + j * NS:CM + 64 + (j + 1) * NS],
                                                    xp[:, j * P:(j + 1) * P],
                                                    net.ident[0:RANK + 2 * NS, RANK + NS:RANK + 2 * NS],
                                                    start=True, stop=True)
                        last.then_inc(s["bc_psum"], 1)
                        for g in range(2):
                            pe.wait_ge(s["xp_done"], 1 + q * 3 + (1, 3)[g])
                            for half in range(2):
                                m = 2 * g + half
                                last = nc.tensor.matmul((H0, H1)[g][:, half * CM:(half + 1) * CM],
                                                        w_dt[:, m * P:(m + 1) * P], low, start=True, stop=True)
                            last.then_inc(s["dt_psum"], 1)
                    if slot in (14, 15):
                        if slot == 14:
                            pe.wait_ge(s["u_done"], 1 + q + 1)
                            pe.wait_ge(s["dt_done"], 1 + q * KI + KI)
                        for j in ((0, 1) if slot == 14 else (2, 3)):
                            if j >= 2:
                                pe.wait_ge(s["ulo_done"], 1 + q * NSUB + j - 1)
                            pe.sem_inc(net.carrier, 1)
                            for m in range(KI):
                                last = nc.tensor.transpose((H0, H1)[j % 2][0:SUB, m * P:(m + 1) * P],
                                                           u[:, m, j * SUB:(j + 1) * SUB], net.ident[:])
                            last.then_inc(s["uT_psum"], 1)
                    if slot in (16, 17):
                        for j in ((0, 1) if slot == 16 else (2, 3)):
                            pe.wait_ge(s["mlo_done"], 1 + q * NSUB + j + 1)
                            pe.wait_ge(s["ulo_done"], 1 + q * NSUB + min(j + 3, NSUB))
                            if j >= 2:
                                pe.wait_ge(s["carry_done"], 1 + q * NSUB + j - 1)
                            pe.sem_inc(net.carrier, 1)
                            for i, (m_part, u_part) in enumerate(PARTS):
                                last = nc.tensor.matmul((H0, H1)[j % 2][0:NS, :], m_part[0:SUB, par, j, :, SUB - 1],
                                                        u_part[0:SUB, par, j, :], start=(i == 0), stop=(i == 2))
                            last.then_inc(s["carry_psum"], 1)

                def tail(t, par, slot):
                    if slot == 0:
                        pe.wait_ge(s["vlo_done"], 1 + (t + 1) * NSUB)
                        pe.wait_ge(s["y_dve"], 1 + t * NS)
                        pe.wait_ge(s["y_pool"], 1 + t * NS)
                        for m in range(KI):
                            for j in range(TM):
                                last = nc.tensor.transpose(
                                    (H0, H1)[m // 2][:, (m % 2) * CM + j * P:(m % 2) * CM + (j + 1) * P],
                                    y[:, par, j, m * P:(m + 1) * P], net.ident[:])
                            if m % 2:
                                last.then_inc(s["yT_psum"], 1)
                    if slot in (2, 3):
                        j = slot - 2
                        if j == 0:
                            pe.wait_ge(s["gated_done"], 1 + t * KI + KI)
                        for k in range(KI):
                            last = nc.tensor.matmul(H1[:, j * D:(j + 1) * D], u[:, k, j * P:(j + 1) * P],
                                                    w_out[:, k, :], start=(k == 0), stop=(k == KI - 1))
                        if j == TM - 1:
                            last.then_inc(s["out_psum"], 1)

                def turn(c, n):
                    k = c * NS + n
                    pe.wait_ge(s["scan_done"], 1 + (k + 1) * KI)
                    for tt in (1, 0):
                        if tt:
                            pe.wait_ge(s["prod_done"], 1 + k)
                        else:
                            pe.wait_ge(s["y_dve"], 1 + k)
                        for m in range(KI):
                            last = nc.tensor.transpose(HB[tt][:, m * P:(m + 1) * P],
                                                       h[:, n % 3, m, tt * P:(tt + 1) * P], net.ident[:])
                        last.then_inc(s["ht_psum"], 1)

                def velocity(c, par, n):
                    if n >= 2:
                        pe.wait_ge(s["scan_done"], 1 + (c * NS + n - 1) * KI)
                    for j in range(NSUB) if n == 0 else (None,):
                        if j == 0:
                            pe.wait_ge(s["before_done"], 1 + c + 1)
                        elif j:
                            pe.wait_ge(s["vlo_done"], 1 + c * NSUB + j)
                        for m in range(KI):
                            bank = VB[(n % 2) * 2 + m // 2]
                            for jj in range(NSUB) if j is None else (j,):
                                at = (m % 2) * CM + jj * SUB
                                for i, (m_part, u_part) in enumerate(PARTS):
                                    last = nc.tensor.matmul(bank[:, at:at + SUB], u_part[:, par, jj, m * P:(m + 1) * P],
                                                            m_part[:, par, jj, n, :], start=(i == 0), stop=(i == 2))
                            if m % 2 and (j is None or j == NSUB - 1):
                                last.then_inc(s["v_psum"], 1)

                def slots(c, par):
                    velocity(c, par, 0)
                    for n in range(NS + LAG):
                        if n < NS - 1:
                            velocity(c, par, n + 1)
                        if n == NS:
                            head(c + 1, 1 - par, n)
                        if n >= 1 and n <= NS:
                            turn(c, n - 1)
                        tail(c, 1 - par, n)
                        if n != NS:
                            head(c + 1, 1 - par, n)

                for slot in range(NS + LAG):
                    head(0, 0, slot)
                with pe.Fori(0, NCM // 2) as c2:
                    slots(c2 * 2, 0)
                    slots(c2 * 2 + 1, 1)
                for slot in range(4):
                    tail(NCM, 1, slot)


def mamba_phases(net):
    nc = net.nc
    parked = nc.dram_tensor("parked", (N, D), F32, kind="Internal").ap().rearrange("(n p) d -> p n d", p=P)
    net.run(lambda n: stream_in(n, parked))
    for layer in range(LAYERS):
        net.run(lambda n: mamba_phase(n, layer, net.x_all))
    net.run(lambda n: stream_out(n, parked))


def normalise_all(net, ctx, tag, parked, back):
    nc, x = net.nc, net.x
    st, mv = net.sb(ctx, tag + "st", [P, NT, 6]), net.sb(ctx, tag + "mv", [P, NT, 2])
    var, rstd, half = net.sb(ctx, tag + "var", [P, NT]), net.sb(ctx, tag + "rstd", [P, NT]), net.sb(ctx, tag + "half", [P, NT])
    tmp = net.sb(ctx, tag + "tmp", [P, 2, TPC, D])
    residual = net.sb(ctx, tag + "residual", [P, NT, D]) if back else None
    stats, root, own, done = net.sem(tag + "stats"), net.sem(tag + "root"), net.own(tag + "own"), net.sem(tag + "done")
    moved = net.own(tag + "moved")
    net.start()
    with nc.Block() as block:
        @block.sync
        def _(sp):
            if back:
                sp.dma_start(residual[:], parked).then_inc(moved, 16)
            else:
                sp.dma_start(parked, x).then_inc(moved, 16)
            sp.wait_ge(moved, 16)

        @block.gpsimd
        def _(pool):
            nc.gpsimd.memset(half[:], -0.5).then_inc(root, 1)
            if not back:
                nc.gpsimd.memset(net.x_all[:, 0:SPARE, :], 0.0)
                nc.gpsimd.memset(net.x_all[:, SPARE + NT:, :], 0.0)
            pool.wait_ge(root, 1 + 1)
            pool.wait_ge(stats, 1 + 1)
            nc.gpsimd.tensor_scalar(var[:], mv[:, :, 1], EPS, None, ALU.add).then_inc(root, 1)
            pool.wait_ge(root, 1 + 2)
            nc.gpsimd.tensor_tensor(rstd[:], var[:], half[:], ALU.pow).then_inc(root, 1)
            if back:
                pool.wait_ge(moved, 16)
                for i in range(NCH):
                    pool.wait_ge(done, 1 + i + 1)
                    tiles = slice(i * TPC, (i + 1) * TPC)
                    nc.gpsimd.tensor_tensor(x[:, tiles, :], residual[:, tiles, :], tmp[:, i % 2], ALU.add
                                            ).then_inc(root, 1)

        @block.vector
        def _(dve):
            layer_norm_stats(nc, dve, [x[:, j, :] for j in range(NT)], st, mv, own, 0).then_inc(stats, 1)
            dve.wait_ge(root, 1 + 3)
            dve.wait_ge(moved, 16)
            for i in range(NT):
                if back and i % TPC == 0 and i >= 2 * TPC:
                    dve.wait_ge(root, 1 + 3 + i // TPC - 1)
                to = tmp[:, i // TPC % 2, i % TPC, :] if back else x[:, i, :]
                last = nc.vector.tensor_scalar(to, x[:, i, :], mv[:, i, 0:1], rstd[:, i:i + 1],
                                               ALU.subtract, ALU.mult)
                if i % TPC == TPC - 1:
                    last.then_inc(done, 1)


def stream_in(net, parked):
    with ExitStack() as ctx:
        normalise_all(net, ctx, "si_", parked, False)


def stream_out(net, parked):
    with ExitStack() as ctx:
        normalise_all(net, ctx, "so_", parked, True)


NSLOT = 2 * NT + NE
WB = (KD * HID + KH * D) // P
IDX = mybir.dt.int32


def moe_phases(net):
    nc = net.nc
    slots_x = nc.dram_tensor("slots_x", (NSLOT * P, D), F32, kind="Internal").ap()
    slots_y = nc.dram_tensor("slots_y", (NSLOT * P, D), F32, kind="Internal").ap()
    with ExitStack() as ctx:
        keep = lambda s, shape, dt=F32: net.sb(ctx, "r_" + s, shape, dt)
        mv, rstd, gate = keep("mv", [P, NT, 2]), keep("rstd", [P, NT]), keep("gate", [P, NT, NE])
        share = keep("share", [P, NT, 2])
        slot = keep("slot", [P, NT, 2], IDX)
        tile_expert = keep("tile_expert", [P, NSLOT], IDX)
        with ExitStack() as weights:
            whi = net.sb(weights, "r_whi", [P, NE * WB * P], BF16)
            wlo = net.sb(weights, "r_wlo", [P, NE * WB * P], BF16)
            net.run(lambda n: moe_gate(n, mv, rstd, gate, whi, wlo, slots_x))
            net.run(lambda n: moe_route(n, gate, share, slot, tile_expert))
            net.run(lambda n: moe_scatter(n, mv, rstd, slot, slots_x))
            net.run(lambda n: moe_experts(n, tile_expert, whi, wlo, slots_x, slots_y))
        net.run(lambda n: moe_combine(n, share, slot, slots_y))


def moe_gate(net, mv_all, rstd_all, gate, whi, wlo, slots_x):
    nc, dram, x = net.nc, net.dram, net.x
    assert NCH == NE
    ZR = SPARE
    with ExitStack() as ctx:
        sb = lambda s, shape, dt=F32: net.sb(ctx, "g_" + s, shape, dt)
        wg, bg = sb("wg", [P, KD, NE]), sb("bg", [P, NE])
        st, mv, rstd = sb("st", [P, TPC, 6]), sb("mv", [P, TPC, 2]), sb("rstd", [P, TPC])
        xn, xT = sb("xn", [P, TPC, D]), sb("xT", [P, KD, CH])
        stage = sb("stage", [P, 2, WB * P])
        zeros = net.x_all[:, 0:ZR, :]
        B = net.banks(ctx, "g_bank")
        names = ("loaded weights0 weights1 own_dve zeroed x_stats x_rstd xn_done xT_psum xT_done g_psum g_done "
                 "setup hi_done lo_done").split()
        own = ("loaded", "weights0", "weights1", "own_dve", "zeroed")
        s = {n: (net.own if n in own else net.sem)("g_" + n) for n in names}
        W1, WE = KD * HID, WB * P
        net.start()
        with nc.Block() as block:
            @block.sync
            def _(sp):
                sp.dma_start(wg[:], dram["e_wg"]).then_inc(s["loaded"], 16)
                sp.dma_start(bg[:], dram["e_bg"].partition_broadcast(P)).then_inc(s["loaded"], 16)

                def load(e, par):
                    sp.dma_start(stage[:, par, 0:W1], dram["e_w1"][e].rearrange("p k h -> p (k h)")
                                 ).then_inc(s[f"weights{par}"], 16)
                    sp.dma_start(stage[:, par, W1:WE], dram["e_w2"][e].rearrange("p k d -> p (k d)")
                                 ).then_inc(s[f"weights{par}"], 16)

                load(0, 0)
                load(1, 1)
                sp.wait_ge(s["setup"], 1 + 1)
                rows = slots_x.rearrange("(i p r) d -> i p r d", p=P, r=ZR)
                with sp.Fori(0, NSLOT // ZR) as i:
                    sp.dma_start(rows[i], zeros).then_inc(s["zeroed"], 16)
                with sp.Fori(1, NE // 2) as e2:
                    for par in range(2):
                        sp.wait_ge(s["lo_done"], 1 + e2 * 2 + par - 1)
                        load(e2 * 2 + par, par)
                sp.wait_ge(s["zeroed"], NSLOT // ZR * 16)

            @block.gpsimd
            def _(pool):
                nc.gpsimd.memset(zeros, 0.0).then_inc(s["setup"], 1)
                with pool.Fori(0, NCH) as i:
                    pool.wait_ge(s["x_stats"], 1 + i + 1)
                    inverse_root(net, pool, rstd[:], mv[:, :, 1]).then_inc(s["x_rstd"], 1)

            @block.vector
            def _(dve):
                dve.wait_ge(s["loaded"], 32)
                with dve.Fori(0, NE // 2) as c2:
                    for par in range(2):
                        c = c2 * 2 + par
                        dve.sem_clear(s["own_dve"])
                        tiles = [x[:, c * TPC + j, :] for j in range(TPC)]
                        layer_norm_stats(nc, dve, tiles, st, mv, s["own_dve"], 0).then_inc(s["x_stats"], 1)
                        dve.wait_ge(s["x_stats"], 1 + c + 1)
                        nc.vector.tensor_copy(mv_all[:, bass.ts(c, TPC), :], mv[:])
                        dve.wait_ge(s["x_rstd"], 1 + c + 1)
                        nc.vector.tensor_copy(rstd_all[:, bass.ts(c, TPC)], rstd[:])
                        for j in range(TPC):
                            nc.vector.tensor_scalar(xn[:, j, :], tiles[j], mv[:, j, 0:1], rstd[:, j:j + 1],
                                                    ALU.subtract, ALU.mult).then_inc(s["xn_done"], 1)
                        dve.wait_ge(s["hi_done"], 1 + c + 1)
                        nc.vector.tensor_tensor(wlo[:, bass.ts(c, WE)], stage[:, par, :], whi[:, bass.ts(c, WE)],
                                                ALU.subtract).then_inc(s["lo_done"], 1)
                        dve.wait_ge(s["g_psum"], 1 + c + 1)
                        nc.vector.tensor_tensor(gate[:, bass.ts(c, TPC), :],
                                                B[2][:, 0:TPC * NE].rearrange("p (j e) -> p j e", e=NE),
                                                bg[:].unsqueeze(1).broadcast_to([P, TPC, NE]), ALU.add
                                                ).then_inc(s["g_done"], 1)

            @block.scalar
            def _(act):
                with act.Fori(0, NE // 2) as c2:
                    for par in range(2):
                        c = c2 * 2 + par
                        act.wait_ge(s[f"weights{par}"], c2 * 32 + 32)
                        act.sem_inc(net.carrier, 1)
                        nc.scalar.copy(whi[:, bass.ts(c, WE)], stage[:, par, :]).then_inc(s["hi_done"], 1)
                        act.wait_ge(s["xT_psum"], 1 + c * TPC + TPC)
                        for k in range(KD):
                            nc.scalar.copy(xT[:, k, :], B[k][:]).then_inc(s["xT_done"], 1)

            @block.tensor
            def _(pe):
                pe.wait_ge(s["loaded"], 32)
                with pe.Fori(0, NCH) as c:
                    for j in range(TPC):
                        pe.wait_ge(s["xn_done"], 1 + c * TPC + j + 1)
                        pe.wait_ge(s["xT_done"], 1 + c * KD)
                        for k in range(KD):
                            last = nc.tensor.transpose(B[k][:, j * P:(j + 1) * P], xn[:, j, k * P:(k + 1) * P],
                                                       net.ident[:])
                        last.then_inc(s["xT_psum"], 1)
                    pe.wait_ge(s["xT_done"], 1 + c * KD + KD)
                    pe.wait_ge(s["g_done"], 1 + c)
                    for j in range(TPC):
                        for k in range(KD):
                            last = nc.tensor.matmul(B[2][:, j * NE:(j + 1) * NE], xT[:, k, j * P:(j + 1) * P], wg[:, k, :],
                                                    start=(k == 0), stop=(k == KD - 1))
                    last.then_inc(s["g_psum"], 1)


def moe_route(net, gate, share, slot, tile_expert):
    nc, dram = net.nc, net.dram
    with ExitStack() as ctx:
        sb = lambda s, shape, dt=F32: net.sb(ctx, "o_" + s, shape, dt)
        rank, bound, tile_no = sb("rank", [P, NE]), sb("bound", [P, NT]), sb("tile_no", [P, NSLOT])
        upto, ones = sb("upto", [P, P]), sb("ones", [P, P])
        one1, one2, tmp = (sb(t, [P, NT, NE]) for t in ("one1", "one2", "tmp"))
        top1, top2, col = (sb(t, [P, NT]) for t in ("top1", "top2", "col"))
        chosen, total, upto_tile, keep_on, where = (sb(t, [P, NE, NT]) for t in (
            "chosen", "total", "upto_tile", "keep_on", "where"))
        tiles, ends, one_e = sb("tiles", [P, NE]), sb("ends", [P, NE]), sb("one_e", [P, NE])
        passed, number = sb("passed", [P, NSLOT, NE]), sb("number", [P, NSLOT])
        B = net.banks(ctx, "o_bank")
        names = "loaded own_dve setup exp_in exp_out pair_in pair_out chosen_done count_psum".split()
        s = {n: (net.own if n in ("loaded", "own_dve") else net.sem)("o_" + n) for n in names}
        over = lambda t: t[:].unsqueeze(2).broadcast_to([P, NT, NE])
        flat = lambda t: t[:].rearrange("p e i -> p (e i)")
        turned = lambda t: t[:].rearrange("p e i -> p i e")

        net.start()
        with nc.Block() as block:
            @block.sync
            def _(sp):
                for t, key in ((rank, "rank"), (bound, "bound"), (tile_no, "tile_no")):
                    sp.dma_start(t[:], dram[key].partition_broadcast(P)).then_inc(s["loaded"], 16)
                sp.dma_start(upto[:], dram["causal"]).then_inc(s["loaded"], 16)

            @block.gpsimd
            def _(pool):
                nc.gpsimd.memset(ones[:], 1.0)
                nc.gpsimd.memset(one_e[:], 1.0)
                nc.gpsimd.memset(keep_on[:], 1.0).then_inc(s["setup"], 1)
                pool.wait_ge(s["setup"], 1 + 1)
                nc.gpsimd.memset(keep_on[:, :, 0:1], 0.0).then_inc(s["setup"], 1)

            @block.vector
            def _(dve):
                dve.wait_ge(s["loaded"], 64)
                dve.wait_ge(s["setup"], 1 + 2)
                own = [0]

                def after(ins):
                    own[0] += 1
                    ins.then_inc(s["own_dve"], 1)
                    dve.wait_ge(s["own_dve"], own[0])

                V = nc.vector
                after(V.tensor_reduce(top1[:], gate[:], AX.X, ALU.max))
                V.tensor_tensor(gate[:], gate[:], over(top1), ALU.subtract).then_inc(s["exp_in"], 1)
                dve.wait_ge(s["exp_out"], 1 + 1)
                after(V.tensor_reduce(top1[:], gate[:], AX.X, ALU.add))
                after(V.reciprocal(top2[:], top1[:]))
                after(V.tensor_tensor(gate[:], gate[:], over(top2), ALU.mult))

                def pick(one, top):
                    after(V.tensor_reduce(top[:], gate[:], AX.X, ALU.max))
                    after(V.tensor_tensor(tmp[:], gate[:], over(top), ALU.is_equal))
                    after(V.tensor_tensor(tmp[:], tmp[:], rank[:].unsqueeze(1).broadcast_to([P, NT, NE]), ALU.mult))
                    after(V.tensor_reduce(col[:], tmp[:], AX.X, ALU.max))
                    after(V.tensor_tensor(one[:], tmp[:], over(col), ALU.is_equal))

                pick(one1, top1)
                after(V.scalar_tensor_tensor(gate[:], one1[:], -2.0, gate[:], ALU.mult, ALU.add))
                pick(one2, top2)
                V.tensor_tensor(turned(chosen), one1[:], one2[:], ALU.add).then_inc(s["chosen_done"], 1)
                V.tensor_tensor(top2[:], top2[:], top1[:], ALU.subtract).then_inc(s["pair_in"], 1)
                dve.wait_ge(s["pair_out"], 1 + 1)
                after(V.tensor_scalar(top1[:], top2[:], 1.0, None, ALU.add))
                after(V.reciprocal(col[:], top1[:]))
                V.tensor_copy(share[:, :, 0], col[:])
                V.tensor_tensor(share[:, :, 1], top2[:], col[:], ALU.mult)
                dve.wait_ge(s["count_psum"], 1 + 1)
                after(V.tensor_copy(flat(total), B[1][:, 0:NE * NT]))
                after(V.tensor_tensor_scan(flat(upto_tile), flat(keep_on), flat(total), 0.0, ALU.mult, ALU.add))
                after(V.tensor_tensor(where[:], upto_tile[:, :, NT - 1:NT].broadcast_to([P, NE, NT]),
                                      bound[:].unsqueeze(1).broadcast_to([P, NE, NT]), ALU.is_gt))
                after(V.tensor_reduce(tiles[:], where[:], AX.X, ALU.add))
                after(V.tensor_tensor_scan(ends[:], one_e[:], tiles[:], 0.0, ALU.mult, ALU.add))
                after(V.tensor_tensor(tiles[:], ends[:], tiles[:], ALU.subtract))
                after(V.tensor_scalar(tiles[:], tiles[:], float(P), -1.0, ALU.mult, ALU.add))
                after(V.tensor_tensor(flat(where), flat(upto_tile), flat(total), ALU.subtract))
                after(V.tensor_tensor(flat(where), flat(where), B[0][:, 0:NE * NT], ALU.add))
                after(V.tensor_tensor(where[:], where[:], tiles[:].unsqueeze(2).broadcast_to([P, NE, NT]), ALU.add))
                for i, one in enumerate((one1, one2)):
                    after(V.tensor_tensor(tmp[:], one[:], turned(where), ALU.mult))
                    after(V.tensor_reduce(col[:], tmp[:], AX.X, ALU.add))
                    after(V.tensor_copy(slot[:, :, i], col[:]))
                after(V.tensor_tensor(passed[:], ends[:].unsqueeze(1).broadcast_to([P, NSLOT, NE]),
                                      tile_no[:].unsqueeze(2).broadcast_to([P, NSLOT, NE]), ALU.is_le))
                after(V.tensor_reduce(number[:], passed[:], AX.X, ALU.add))
                after(V.tensor_scalar(number[:], number[:], float(NE - 1), None, ALU.min))
                after(V.tensor_copy(tile_expert[:], number[:]))

            @block.scalar
            def _(act):
                act.wait_ge(s["exp_in"], 1 + 1)
                nc.scalar.activation(gate[:], gate[:], ACT.Exp).then_inc(s["exp_out"], 1)
                act.wait_ge(s["pair_in"], 1 + 1)
                nc.scalar.activation(top2[:], top2[:], ACT.Exp).then_inc(s["pair_out"], 1)

            @block.tensor
            def _(pe):
                pe.wait_ge(s["loaded"], 64)
                pe.wait_ge(s["setup"], 1 + 2)
                pe.wait_ge(s["chosen_done"], 1 + 1)
                nc.tensor.matmul(B[0][:, 0:NE * NT], upto[:], flat(chosen), start=True, stop=True)
                nc.tensor.matmul(B[1][:, 0:NE * NT], ones[:], flat(chosen), start=True, stop=True
                                 ).then_inc(s["count_psum"], 1)


def moe_scatter(net, mv, rstd, slot, slots_x):
    nc, x = net.nc, net.x
    with ExitStack() as ctx:
        xn = net.sb(ctx, "c_xn", [P, 2, TPC, D])
        at = net.sb(ctx, "c_at", [P, 2, TPC * 2], IDX)
        ready = net.sem("c_ready")
        sent = [net.own(f"c_sent{par}") for par in range(2)]
        BYTES = TPC * 2 * 16
        net.start()
        with nc.Block() as block:
            @block.vector
            def _(dve):
                def chunk(c, par):
                    nc.vector.tensor_copy(at[:, par, :], slot[:, bass.ts(c, TPC), :].rearrange("p j i -> p (j i)"))
                    for j in range(TPC):
                        t = c * TPC + j
                        last = nc.vector.tensor_scalar(xn[:, par, j, :], x[:, t, :], mv[:, t, 0:1],
                                                       rstd[:, bass.ts(t, 1)], ALU.subtract, ALU.mult)
                    last.then_inc(ready, 1)

                chunk(0, 0)
                chunk(1, 1)
                with dve.Fori(1, NCH // 2) as c2:
                    for par in range(2):
                        dve.wait_ge(sent[par], c2 * BYTES)
                        dve.sem_inc(net.carrier, 1)
                        chunk(c2 * 2 + par, par)

            @block.gpsimd
            def _(pool):
                with pool.Fori(0, NCH // 2) as c2:
                    for par in range(2):
                        pool.wait_ge(ready, 1 + c2 * 2 + par + 1)
                        pool.sem_inc(net.carrier, 1)
                        for j in range(TPC):
                            for i in range(2):
                                nc.gpsimd.indirect_dma_start(
                                    slots_x, bass.IndirectOffsetOnAxis(at[:, par, j * 2 + i:j * 2 + i + 1], 0),
                                    xn[:, par, j, :], None).then_inc(sent[par], 16)
                for par in range(2):
                    pool.wait_ge(sent[par], NCH // 2 * BYTES)


def moe_experts(net, tile_expert, whi, wlo, slots_x, slots_y):
    nc, dram = net.nc, net.dram
    with ExitStack() as ctx:
        sb = lambda t, shape, dt=F32: net.sb(ctx, "x_" + t, shape, dt)
        b1, b2 = sb("b1", [P, NE * KH]), sb("b2", [P, NE, D])
        x_in = sb("x_in", [P, 2, D])
        xhi, xlo = sb("xhi", [P, 2, KD * P], BF16), sb("xlo", [P, 2, KD * P], BF16)
        h = sb("h", [P, 2, KH * P])
        hhi, hlo = sb("hhi", [P, 2, KH * P], BF16), sb("hlo", [P, 2, KH * P], BF16)
        y = sb("y", [P, 2, D])
        banks = net.banks(ctx, "x_bank")
        HB, XB, YB = (banks[0:2], banks[2:4]), banks[4:6], banks[6:8]
        HALF = KH * P // 2
        names = "loaded x_in0 x_in1 xT_psum xhi_done xlo_done h_psum h_done hhi_done hlo_done y_psum y_done y_out0 y_out1"
        s = {n: (net.own if n == "loaded" or "y_out" in n else net.sem)("x_" + n) for n in names.split()}

        def rounds(engine, body, last=None):
            for k in range(4):
                body(k, k // 2, k % 2, k < 2, False)
            with engine.Fori(2, NSLOT // 2 - 1) as k2:
                for par in range(2):
                    body(k2 * 2 + par, k2, par, False, False)
            for par in range(2):
                body(NSLOT - 2 + par, NSLOT // 2 - 1, par, False, par == 1)

        def expert(engine, k):
            return engine.value_load(tile_expert[0:1, bass.ts(k, 1)], min_val=0, max_val=NE - 1)

        net.start()
        with nc.Block() as block:
            @block.sync
            def _(sp):
                sp.dma_start(b1[:], dram["e_b1"].rearrange("p e m -> p (e m)")).then_inc(s["loaded"], 16)
                sp.dma_start(b2[:], dram["e_b2"].partition_broadcast(P)).then_inc(s["loaded"], 16)

                def body(k, k2, par, first, last):
                    if not first:
                        sp.wait_ge(s["xT_psum"], 1 + k - 1)
                    sp.dma_start(x_in[:, par, :], slots_x[bass.ts(k, P), :]).then_inc(s[f"x_in{par}"], 16)

                rounds(sp, body)

            @block.gpsimd
            def _(pool):
                with pool.Fori(0, NSLOT // 2) as k2:
                    for par in range(2):
                        k = k2 * 2 + par
                        pool.wait_ge(s["y_done"], 1 + k + 1)
                        pool.sem_inc(net.carrier, 1)
                        nc.gpsimd.dma_start(slots_y[bass.ts(k, P), :], y[:, par, :]).then_inc(s[f"y_out{par}"], 16)
                for par in range(2):
                    pool.wait_ge(s[f"y_out{par}"], NSLOT // 2 * 16)

            @block.tensor
            def _(pe):
                PARTS_X = ((wlo, xhi), (whi, xlo), (whi, xhi))
                PARTS_H = ((hlo, whi), (hhi, wlo), (hhi, whi))

                def turn(k, k2, par, first):
                    pe.wait_ge(s[f"x_in{par}"], 1 + k2 * 16 + 16)
                    if not first:
                        pe.wait_ge(s["xlo_done"], 1 + k - 1)
                    for i in range(KD):
                        last = nc.tensor.transpose(XB[par][:, i * P:(i + 1) * P], x_in[:, par, i * P:(i + 1) * P],
                                                   net.ident[:])
                    last.then_inc(s["xT_psum"], 1)

                def second(k, par, first):
                    e = expert(pe, k)
                    pe.wait_ge(s["hlo_done"], 1 + (k + 1) * 2)
                    if not first:
                        pe.wait_ge(s["y_done"], 1 + k - 1)
                    pe.sem_inc(net.carrier, 1)
                    for m in range(KH):
                        for i, (h_part, w_part) in enumerate(PARTS_H):
                            last = nc.tensor.matmul(YB[par][:, 0:D], h_part[:, par, m * P:(m + 1) * P],
                                                    w_part[:, bass.ts(e * (WB // 2) + KD * KH // 2 + m, D)],
                                                    start=(m == 0 and i == 0), stop=(m == KH - 1 and i == 2))
                    last.then_inc(s["y_psum"], 1)

                def body(k, k2, par, first, last_round):
                    e = expert(pe, k)
                    if not last_round:
                        turn(k + 1, k2 + par, 1 - par, first and par == 0)
                    pe.wait_ge(s["xlo_done"], 1 + k + 1)
                    for b in range(2):
                        if not first:
                            pe.wait_ge(s["h_done"], 1 + (k - 2) * 2 + b + 1)
                        pe.sem_inc(net.carrier, 1)
                        for m in range(b * KH // 2, (b + 1) * KH // 2):
                            at = m % (KH // 2) * P
                            for kk in range(KD):
                                for i, (w_part, x_part) in enumerate(PARTS_X):
                                    last = nc.tensor.matmul(HB[par][b][:, at:at + P],
                                                            w_part[:, bass.ts(e * WB + kk * KH + m, P)],
                                                            x_part[:, par, kk * P:(kk + 1) * P],
                                                            start=(kk == 0 and i == 0), stop=(kk == KD - 1 and i == 2))
                        last.then_inc(s["h_psum"], 1)
                    if not (first and par == 0):
                        second(k - 1, 1 - par, first)

                turn(0, 0, 0, True)
                rounds(pe, body)
                second(NSLOT - 1, 1, False)

            @block.scalar
            def _(act):
                act.wait_ge(s["loaded"], 32)

                def part(k, par, first):
                    act.wait_ge(s["xT_psum"], 1 + k + 1)
                    if not first:
                        act.wait_ge(s["h_psum"], 1 + (k - 1) * 2)
                    nc.scalar.copy(xhi[:, par, :], XB[par][:, 0:KD * P]).then_inc(s["xhi_done"], 1)

                def body(k, k2, par, first, last_round):
                    e = expert(act, k)
                    if not last_round:
                        part(k + 1, 1 - par, first and par == 0)
                    for b in range(2):
                        act.wait_ge(s["h_psum"], 1 + k * 2 + b + 1)
                        if not first:
                            act.wait_ge(s["hlo_done"], 1 + (k - 1) * 2)
                        act.sem_inc(net.carrier, 1)
                        for m in range(b * KH // 2, (b + 1) * KH // 2):
                            at = m % (KH // 2) * P
                            last = nc.scalar.activation(h[:, par, m * P:(m + 1) * P], HB[par][b][:, at:at + P], ACT.Relu,
                                                        bias=b1[:, bass.ts(e * KH + m, 1)])
                        last.then_inc(s["h_done"], 1)

                part(0, 0, True)
                rounds(act, body)

            @block.vector
            def _(dve):
                dve.wait_ge(s["loaded"], 32)

                def part(k, par):
                    dve.wait_ge(s["xhi_done"], 1 + k + 1)
                    nc.vector.tensor_tensor(xlo[:, par, :], XB[par][:, 0:KD * P], xhi[:, par, :], ALU.subtract
                                            ).then_inc(s["xlo_done"], 1)

                def result(k, k2, par, first):
                    e = expert(dve, k)
                    dve.wait_ge(s["y_psum"], 1 + k + 1)
                    if not first:
                        dve.wait_ge(s[f"y_out{par}"], k2 * 16)
                    dve.sem_inc(net.carrier, 1)
                    nc.vector.tensor_tensor(y[:, par, :], YB[par][:, 0:D], b2[:, bass.ts(e, 1), :].rearrange("p o d -> p (o d)"), ALU.add
                                            ).then_inc(s["y_done"], 1)

                def body(k, k2, par, first, last_round):
                    if not last_round:
                        part(k + 1, 1 - par)
                    for b in range(2):
                        cols = slice(b * HALF, (b + 1) * HALF)
                        dve.wait_ge(s["h_done"], 1 + k * 2 + b + 1)
                        if not first:
                            dve.wait_ge(s["y_psum"], 1 + k - 1)
                        nc.vector.tensor_copy(hhi[:, par, cols], h[:, par, cols]).then_inc(s["hhi_done"], 1)
                        dve.wait_ge(s["hhi_done"], 1 + k * 2 + b + 1)
                        nc.vector.tensor_tensor(hlo[:, par, cols], h[:, par, cols], hhi[:, par, cols], ALU.subtract
                                                ).then_inc(s["hlo_done"], 1)
                    if not (first and par == 0):
                        result(k - 1, k2 + par - 1, 1 - par, first or (isinstance(k, int) and k <= 2))

                part(0, 0)
                rounds(dve, body)
                result(NSLOT - 1, NSLOT // 2 - 1, 1, False)


def moe_combine(net, share, slot, slots_y):
    nc, x = net.nc, net.x
    with ExitStack() as ctx:
        got = net.sb(ctx, "q_got", [P, 2, TPC, 2, D])
        at = net.sb(ctx, "q_at", [P, 2, TPC * 2], IDX)
        z = net.sb(ctx, "q_z", [P, TPC, D])
        st, mv, rstd = net.sb(ctx, "q_st", [P, TPC, 6]), net.sb(ctx, "q_mv", [P, TPC, 2]), net.sb(ctx, "q_rstd", [P, TPC])
        at_done, z_stats, z_rstd, x_done = (net.sem("q_" + t) for t in ("at_done", "z_stats", "z_rstd", "x_done"))
        rows = [net.own(f"q_rows{par}") for par in range(2)]
        own_dve = net.own("q_own_dve")
        BYTES = TPC * 2 * 16
        net.start()
        with nc.Block() as block:
            @block.gpsimd
            def _(pool):
                def gather(c, c2, par):
                    pool.wait_ge(at_done, 1 + c + 1)
                    pool.sem_inc(net.carrier, 1)
                    for j in range(TPC):
                        for i in range(2):
                            nc.gpsimd.indirect_dma_start(
                                got[:, par, j, i, :], None, slots_y,
                                bass.IndirectOffsetOnAxis(at[:, par, j * 2 + i:j * 2 + i + 1], 0)).then_inc(rows[par], 16)

                def root(c):
                    pool.wait_ge(z_stats, 1 + c + 1)
                    inverse_root(net, pool, rstd[:], mv[:, :, 1]).then_inc(z_rstd, 1)

                gather(0, 0, 0)
                with pool.Fori(0, NCH // 2 - 1) as c2:
                    for par in range(2):
                        gather(c2 * 2 + par + 1, c2 + par, 1 - par)
                        root(c2 * 2 + par)
                gather(NCH - 1, NCH // 2 - 1, 1)
                root(NCH - 2)
                root(NCH - 1)

            @block.vector
            def _(dve):
                def indices(c, par):
                    nc.vector.tensor_copy(at[:, par, :], slot[:, bass.ts(c, TPC), :].rearrange("p j i -> p (j i)")
                                          ).then_inc(at_done, 1)

                def chunk(c, c2, par, more):
                    dve.sem_clear(own_dve)
                    dve.wait_ge(rows[par], c2 * BYTES + BYTES)
                    dve.sem_inc(net.carrier, 1)
                    for j in range(TPC):
                        nc.vector.tensor_scalar(z[:, j, :], got[:, par, j, 0, :], share[:, c * TPC + j, 0:1], None, ALU.mult
                                                ).then_inc(own_dve, 1)
                    for j in range(TPC):
                        dve.wait_ge(own_dve, j + 1)
                        nc.vector.scalar_tensor_tensor(z[:, j, :], got[:, par, j, 1, :], share[:, c * TPC + j, 1:2],
                                                       z[:, j, :], ALU.mult, ALU.add).then_inc(own_dve, 1)
                    dve.wait_ge(own_dve, 2 * TPC)
                    if more:
                        indices(c + 2, par)
                    layer_norm_stats(nc, dve, [z[:, j, :] for j in range(TPC)], st, mv, own_dve, 2 * TPC
                                     ).then_inc(z_stats, 1)
                    dve.wait_ge(z_rstd, 1 + c + 1)
                    for j in range(TPC):
                        last = nc.vector.tensor_scalar(z[:, j, :], z[:, j, :], mv[:, j, 0:1], rstd[:, j:j + 1],
                                                       ALU.subtract, ALU.mult)
                    last.then_inc(own_dve, 1)
                    dve.wait_ge(own_dve, 2 * TPC + 2)
                    xc = x[:, bass.ts(c, TPC), :]
                    nc.vector.tensor_tensor(xc, xc, z[:], ALU.add).then_inc(x_done, 1)
                    dve.wait_ge(x_done, 1 + c + 1)
                    dve.sem_inc(net.carrier, 1)

                indices(0, 0)
                indices(1, 1)
                with dve.Fori(0, NCH // 2 - 1) as c2:
                    for par in range(2):
                        c = c2 * 2 + par
                        chunk(c, c2, par, True)
                for par in range(2):
                    chunk(NCH - 2 + par, NCH // 2 - 1, par, False)


def build(nc, dram, out, phases):
    with ExitStack() as ctx:
        net = Net(nc, ctx, dram, out)
        stored = ctx.enter_context(nc.semaphore("stored"))
        with nc.Block() as block:
            @block.gpsimd
            def _(pool):
                nc.gpsimd.memset(net.half[:], -0.5)
            @block.sync
            def _(sp):
                sp.dma_start(net.x, dram["x"].rearrange("(n p) d -> p n d", p=P)).then_inc(stored, 16)
                sp.dma_start(net.ident[:], dram["ident"]).then_inc(stored, 16)
                sp.wait_ge(stored, 32)
        for phase in phases:
            if phase in (mamba_phases, moe_phases):
                phase(net)
            else:
                net.run(phase)
        with nc.Block() as block:
            @block.sync
            def _(sp):
                sp.dma_start(out.rearrange("(n p) d -> p n d", p=P), net.x).then_inc(stored, 16)
                sp.wait_ge(stored, 48)


def layout(a):
    import numpy as np

    def rows(w):
        return np.ascontiguousarray(w.reshape(-1, P, w.shape[-1]).transpose(1, 0, 2))

    def col(v):
        return np.ascontiguousarray(v.reshape(-1, P).T)

    a = {k: np.asarray(v) for k, v in a.items()}
    t = np.arange(P)
    sub = np.arange(SUB)
    decay = np.zeros((KV, NS, SUB), np.float32)
    gap = sub[None, :] - sub[:, None]
    decay[:SUB] = np.where(gap >= 0, 0.6 ** np.maximum(gap, 0), 0.0)[:, None, :]
    for n in range(NS):
        decay[SUB + n, n] = 0.6 ** (sub + 1)
    d = {
        "x": a["L0_attn_x"][0],
        "ident": np.eye(P, dtype=np.float32),
        "causal": (t[:, None] <= t[None, :]).astype(np.float32),
        "head_rows": (t[:, None] // DH == np.arange(8)[None, :]).astype(np.float32),
        "wqkv": rows(np.concatenate([a["L0_attn_Wq"].T, a["L0_attn_Wk"].T, a["L0_attn_Wv"].T], axis=1)),
        "wo": rows(a["L0_attn_Wo"].T),
        "bo": a["L0_attn_bo"],
        "f_w1": rows(a["L0_ffn_W1"].T),
        "f_w2": rows(a["L0_ffn_W2"].T),
        "f_b1": col(a["L0_ffn_b1"]),
        "f_b2": a["L0_ffn_b2"],
        "f_scale": a["L0_ffn_scale"].reshape(1),
        "decay": decay,
    }
    for l in range(LAYERS):
        d |= {
            f"m{l}_norm": col(a["L1_attn_norm_w"][l]),
            f"m{l}_in": rows(a["L1_attn_in_proj_w"][l].T),
            f"m{l}_conv": rows(a["L1_attn_conv_w"][l]),
            f"m{l}_conv_b": col(a["L1_attn_conv_b"][l]),
            f"m{l}_xp": rows(a["L1_attn_x_proj_w"][l].T),
            f"m{l}_dt": np.ascontiguousarray(a["L1_attn_dt_w"][l].T),
            f"m{l}_dt_b": col(a["L1_attn_dt_b"][l]),
            f"m{l}_alog": rows(a["L1_attn_A_log"][l]),
            f"m{l}_skip": col(a["L1_attn_Dp"][l]),
            f"m{l}_out": rows(a["L1_attn_out_w"][l].T),
        }
    d |= {
        "e_w1": np.ascontiguousarray(a["L1_ffn_W1"].reshape(NE, KD, P, HID).transpose(0, 2, 1, 3)),
        "e_b1": np.ascontiguousarray(a["L1_ffn_b1"].reshape(NE, KH, P).transpose(2, 0, 1)),
        "e_w2": np.ascontiguousarray(a["L1_ffn_W2"].reshape(NE, KH, P, D).transpose(0, 2, 1, 3)),
        "e_b2": a["L1_ffn_b2"],
        "e_wg": rows(a["L1_ffn_Wg"]),
        "e_bg": a["L1_ffn_bg"],
        "rank": np.arange(NE, 0, -1).astype(np.float32),
        "bound": (np.arange(NT) * P).astype(np.float32),
        "tile_no": np.arange(2 * NT + NE).astype(np.float32),
    }
    return {k: np.ascontiguousarray(v) for k, v in d.items()}


PHASES = (attention_phase, ffn_phase, mamba_phases, moe_phases)


def kernel(**inputs):
    from concourse import bacc
    from concourse.bass_utils import run_bass_kernel_spmd

    arrays = layout(inputs)
    nc = bacc.Bacc("TRN2", target_bir_lowering=False, num_devices=1)
    dram = {name: nc.dram_tensor(f"in_{name}", a.shape, mybir.dt.from_np(a.dtype), kind="ExternalInput").ap()
            for name, a in arrays.items()}
    out = nc.dram_tensor("out_x", (N, D), F32, kind="ExternalOutput").ap()
    build(nc, dram, out, PHASES)
    r = run_bass_kernel_spmd(nc, [{f"in_{name}": a for name, a in arrays.items()}], core_ids=[0])
    return r.results[0]["out_x"].reshape(1, N, D)
```
